# Optimizing a Trainium2 kernel written in Bass

```python
import numpy as np
import jax
import jax.numpy as jnp

def _softmax(x, axis=-1):
    return jax.nn.softmax(x, axis=axis)

def _gelu(x):
    return jax.nn.gelu(x, approximate=True)

def _silu(x):
    return jax.nn.silu(x)

def _sigmoid(x):
    return jax.nn.sigmoid(x)

def _layernorm(x, axis=-1, eps=1e-05):
    m = jnp.mean(x, axis=axis, keepdims=True)
    v = jnp.var(x, axis=axis, keepdims=True)
    return (x - m) / jnp.sqrt(v + eps)

def _scatter_add(tgt, idx, src, axis=0):
    return tgt.at[idx].add(src)

def _segment_sum(src, seg, n):
    return jax.ops.segment_sum(src, seg, n)
kernel_name = 'mk_xattn_ffn_d4_seqx_r8_f9d2dc'

def setup_inputs(seed: int=0):
    np.random.seed(seed)
    _w = jnp.asarray

    def _rec_inputs():
        import jax
        import jax.numpy as jnp
        _rk = jax.random.key(seed)
        x = 7.22e-05 + 1 * jax.random.normal(jax.random.fold_in(_rk, 1), (16, 128, 256), jnp.float32)
        _lenS = 128 - jax.random.randint(jax.random.fold_in(_rk, 7), (16,), 0, max(1, 128 // 4) + 1, jnp.int32)
        _lenS2 = 128 - jax.random.randint(jax.random.fold_in(_rk, 8), (16,), 0, max(1, 128 // 4) + 1, jnp.int32)
        _ctx_2048P = jax.random.normal(jax.random.fold_in(_rk, 11), (16, 16, 256), jnp.float32)
        _ctx_2048c = jax.random.dirichlet(jax.random.fold_in(_rk, 511), 0.3 * jnp.ones((16,), jnp.float32), (16, 128))
        _ctx_2048t = jnp.einsum('bsk,bkd->bsd', _ctx_2048c, _ctx_2048P)
        _ctx_2048t = _ctx_2048t * jax.lax.rsqrt(jnp.mean(jnp.square(_ctx_2048t)) + 1e-12) * 0.953939
        ctx_2048 = 4.13588e-05 + 0.999923 * (_ctx_2048t + 0.3 * jax.random.normal(jax.random.fold_in(_rk, 611), (16, 128, 256), jnp.float32))
        fside_S2_0 = -0.00337071 + 1.01897 * jax.random.normal(jax.random.fold_in(_rk, 14), (128,), jnp.float32)
        _validS = jnp.arange(128)[None, :] < _lenS[:, None]
        _validS2 = jnp.arange(128)[None, :] < _lenS2[:, None]
        _causal = jnp.tril(jnp.ones((128, 128), dtype=bool))
        mask_SxS2_bc0 = jnp.logical_not(jnp.broadcast_to(_validS2[0:1, :], (128, 128)))
        mask_BxS2_bk0 = jnp.logical_not(jnp.broadcast_to(_validS2[:, :], (16, 128)))
        return (x, ctx_2048, fside_S2_0, mask_SxS2_bc0, mask_BxS2_bk0)
    x, ctx_2048, fside_S2_0, mask_SxS2_bc0, mask_BxS2_bk0 = _rec_inputs()

    def _L0_xattn_setup():
        import jax, jax.numpy as jnp
        import numpy as np
        B, LQ, LKV = (4, 128, 128)
        HID, H, G = (256, 32, 8)
        HD = HID // H
        HPG = H // G
        key = jax.random.key(seed)
        ks = jax.random.split(key, 10)
        s = 0.02
        inp = {'X': jax.random.normal(ks[0], (B, LQ, HID), jnp.float32), 'encoder_output': jax.random.normal(ks[1], (B, LKV, HID), jnp.float32), 'causal_mask': jnp.triu(jnp.ones((LQ, LKV), bool), 1), 'padding_mask': jnp.zeros((B, LKV), bool).at[B // 2:, LKV - LKV // 4:].set(True), 'Wq': jax.random.normal(ks[2], (HID, HID), jnp.float32) * s, 'bq': jnp.zeros((HID,), jnp.float32), 'Wk': jax.random.normal(ks[3], (G * HD, HID), jnp.float32) * s, 'bk': jnp.zeros((G * HD,), jnp.float32), 'Wv': jax.random.normal(ks[4], (G * HD, HID), jnp.float32) * s, 'bv': jnp.zeros((G * HD,), jnp.float32), 'Wo': jax.random.normal(ks[5], (HID, HID), jnp.float32) * s, 'bo': jnp.zeros((HID,), jnp.float32)}
        return inp
    _L0_xattn_all = _L0_xattn_setup()
    _L0_xattn_in = {k: v for k, v in _L0_xattn_all.items() if k in ('Wq', 'bq', 'Wk', 'bk', 'Wv', 'bv', 'Wo', 'bo')}
    del _L0_xattn_all

    def _L0_ffn_setup():
        import jax, jax.numpy as jnp
        import numpy as np
        ACT_BITS = 8
        EPS = 1e-05

        def act_quant(x, bits=ACT_BITS):
            qb = float(2 ** (bits - 1))
            scale = qb / jnp.clip(jnp.max(jnp.abs(x), axis=-1, keepdims=True), EPS)
            xq = jnp.clip(jnp.round(x * scale), -qb, qb - 1) / scale
            return x + jax.lax.stop_gradient(xq - x)

        def weight_quant(w):
            scale = 1.0 / jnp.clip(jnp.mean(jnp.abs(w)), EPS)
            wq = jnp.clip(jnp.round(w * scale), -1.0, 1.0) / scale
            return w + jax.lax.stop_gradient(wq - w)

        def fwht(x):
            shape = x.shape
            n = shape[-1]
            x = x.reshape(-1, n)
            h = 1
            while h < n:
                x = x.reshape(-1, n // (2 * h), 2, h)
                a, b = (x[..., 0, :], x[..., 1, :])
                x = jnp.stack([a + b, a - b], axis=-2).reshape(-1, n)
                h *= 2
            return (x * (1.0 / np.sqrt(n)).astype(np.float32)).reshape(shape)

        def bitlinear(x, w):
            return jnp.einsum('bsh,oh->bso', act_quant(x), weight_quant(w))

        def h_bitlinear(x, w):
            return jnp.einsum('bsh,oh->bso', act_quant(fwht(x)), weight_quant(w))
        key = jax.random.key(seed)
        k1, k2, k3, k4 = jax.random.split(key, 4)
        H, I = (256, 1024)
        B, S = (4, 256)
        std_in = 1.0 / np.sqrt(H)
        std_mid = 1.0 / np.sqrt(I)
        return {'x': jax.random.normal(k1, (B, S, H), dtype=jnp.float32), 'w_gate': jax.random.normal(k2, (I, H), dtype=jnp.float32) * std_in, 'w_up': jax.random.normal(k3, (I, H), dtype=jnp.float32) * std_in, 'w_down': jax.random.normal(k4, (H, I), dtype=jnp.float32) * std_mid}
    _L0_ffn_all = _L0_ffn_setup()
    _L0_ffn_in = {k: v for k, v in _L0_ffn_all.items() if k in ('w_gate', 'w_up', 'w_down')}
    del _L0_ffn_all

    def _L1_xattn_setup():
        import jax, jax.numpy as jnp
        import numpy as np
        key = jax.random.key(seed)
        ks = jax.random.split(key, 5)
        B, D, L, NH = (2, 128, 256, 8)
        H = D // NH
        return {'v': jax.random.normal(ks[0], (B, D, L), jnp.float32), 'k': jax.random.normal(ks[1], (H, L), jnp.float32) * 0.1, 'bias': jax.random.normal(ks[2], (D,), jnp.float32), 'x1': jax.random.normal(ks[3], (B, D, L), jnp.float32), 'x2': jax.random.normal(ks[4], (B, D, L), jnp.float32), 'num_heads': NH}
    _L1_xattn_all = _L1_xattn_setup()
    _L1_xattn_in = {k: v for k, v in _L1_xattn_all.items() if k in ('k',)}
    del _L1_xattn_all

    def _L1_ffn_setup():
        import jax, jax.numpy as jnp
        import numpy as np
        B, S, H = (2, 256, 256)
        E, K, F = (32, 4, 176)
        FS = 704
        EPS = 1e-06
        CAP = 128
        key = jax.random.key(seed)
        ks = jax.random.split(key, 10)
        s = 0.02
        return {'hidden_states': jax.random.normal(ks[0], (B, S, H), jnp.float32), 'w_norm': 1.0 + 0.02 * jax.random.normal(ks[1], (H,), jnp.float32), 'w_router': s * jax.random.normal(ks[2], (H, E), jnp.float32), 'w_gate': s * jax.random.normal(ks[3], (E, H, F), jnp.float32), 'w_up': s * jax.random.normal(ks[4], (E, H, F), jnp.float32), 'w_down': s * jax.random.normal(ks[5], (E, F, H), jnp.float32), 'sw_gate': s * jax.random.normal(ks[6], (H, FS), jnp.float32), 'sw_up': s * jax.random.normal(ks[7], (H, FS), jnp.float32), 'sw_down': s * jax.random.normal(ks[8], (FS, H), jnp.float32), 'w_shared_gate': s * jax.random.normal(ks[9], (H, 1), jnp.float32)}
    _L1_ffn_all = _L1_ffn_setup()
    _L1_ffn_in = {k: v for k, v in _L1_ffn_all.items() if k in ('w_norm', 'w_router', 'w_gate', 'w_up', 'w_down', 'sw_gate', 'sw_up', 'sw_down', 'w_shared_gate')}
    del _L1_ffn_all

    def _L2_xattn_setup():
        import jax, jax.numpy as jnp
        import numpy as np
        import math
        EMBED = 256
        HEADS = 32
        GROUPS = 8
        GROUP_HEADS = HEADS // GROUPS
        HEAD_DIM = EMBED // HEADS
        B, S = (4, 128)
        key = jax.random.key(seed)
        ks = jax.random.split(key, 8)
        sc = 0.02
        return {'q': jax.random.normal(ks[0], (B, S, EMBED), jnp.float32), 'k': jax.random.normal(ks[1], (B, S, EMBED), jnp.float32), 'v': jax.random.normal(ks[2], (B, S, EMBED), jnp.float32), 'Wq': jax.random.normal(ks[3], (EMBED, EMBED), jnp.float32) * sc, 'Wk': jax.random.normal(ks[4], (GROUPS * HEAD_DIM, EMBED), jnp.float32) * sc, 'Wv': jax.random.normal(ks[5], (GROUPS * HEAD_DIM, EMBED), jnp.float32) * sc, 'Wfc': jax.random.normal(ks[6], (EMBED, EMBED), jnp.float32) * sc, 'bfc': jnp.zeros((EMBED,), jnp.float32)}
    _L2_xattn_all = _L2_xattn_setup()
    _L2_xattn_in = {k: v for k, v in _L2_xattn_all.items() if k in ('Wq', 'Wk', 'Wv', 'Wfc', 'bfc')}
    del _L2_xattn_all

    def _L2_ffn_setup():
        import jax, jax.numpy as jnp
        import numpy as np
        TOPK = 2
        NORM_TOPK = True
        SCALE = 1.0
        EPS = 1e-09
        key = jax.random.key(seed)
        ks = jax.random.split(key, 9)
        h, i, E = (256, 128, 16)
        std = 0.02
        return {'x': jax.random.normal(ks[0], (1, 256, h), jnp.float32), 'Wr': jax.random.normal(ks[1], (E, h), jnp.float32) * std, 'bias': jnp.zeros((E,), jnp.float32), 'Wg': jax.random.normal(ks[2], (E, h, i), jnp.float32) * std, 'Wu': jax.random.normal(ks[3], (E, h, i), jnp.float32) * std, 'Wd': jax.random.normal(ks[4], (E, i, h), jnp.float32) * std, 'sWg': jax.random.normal(ks[5], (h, i), jnp.float32) * std, 'sWu': jax.random.normal(ks[6], (h, i), jnp.float32) * std, 'sWd': jax.random.normal(ks[7], (i, h), jnp.float32) * std}
    _L2_ffn_all = _L2_ffn_setup()
    _L2_ffn_in = {k: v for k, v in _L2_ffn_all.items() if k in ('Wr', 'bias', 'Wg', 'Wu', 'Wd', 'sWg', 'sWu', 'sWd')}
    del _L2_ffn_all

    def _L3_xattn_setup():
        import jax, jax.numpy as jnp
        import numpy as np
        N_HEAD = 8
        key = jax.random.key(seed)
        k1, k2, k3 = jax.random.split(key, 3)
        b, d, m = (4, 128, 256)
        c, n = (128, 256)
        q = jax.random.normal(k1, (b, d, m), dtype=jnp.float32)
        k = jax.random.normal(k2, (d // d * b, d, n), dtype=jnp.float32).reshape(b, d, n)
        v = jax.random.normal(k3, (b, c, n), dtype=jnp.float32)
        return {'q': q, 'k': k, 'v': v}
    _L3_xattn_all = _L3_xattn_setup()
    _L3_xattn_in = {k: v for k, v in _L3_xattn_all.items() if k in ()}
    del _L3_xattn_all

    def _L3_ffn_setup():
        import jax, jax.numpy as jnp
        import numpy as np
        TOP_K = 2
        key = jax.random.key(seed)
        ks = jax.random.split(key, 5)
        B, S, D, M, E = (4, 256, 256, 256, 8)
        x = jax.random.normal(ks[0], (B, S, D), dtype=jnp.float32)
        gate_kernel = jax.random.normal(ks[1], (D, E), dtype=jnp.float32) / np.sqrt(D)
        wi_0 = jax.random.normal(ks[2], (E, D, M), dtype=jnp.float32) / np.sqrt(D)
        wi_1 = jax.random.normal(ks[3], (E, D, M), dtype=jnp.float32) / np.sqrt(D)
        wo = jax.random.normal(ks[4], (E, M, D), dtype=jnp.float32) / np.sqrt(M)
        return {'x': x, 'gate_kernel': gate_kernel, 'wi_0': wi_0, 'wi_1': wi_1, 'wo': wo}
    _L3_ffn_all = _L3_ffn_setup()
    _L3_ffn_in = {k: v for k, v in _L3_ffn_all.items() if k in ('gate_kernel', 'wi_0', 'wi_1', 'wo')}
    del _L3_ffn_all
    return {'x': x, 'ctx_2048': ctx_2048, 'fside_S2_0': fside_S2_0, 'mask_SxS2_bc0': mask_SxS2_bc0, 'mask_BxS2_bk0': mask_BxS2_bk0, 'L0_xattn_Wq': _L0_xattn_in['Wq'], 'L0_xattn_bq': _L0_xattn_in['bq'], 'L0_xattn_Wk': _L0_xattn_in['Wk'], 'L0_xattn_bk': _L0_xattn_in['bk'], 'L0_xattn_Wv': _L0_xattn_in['Wv'], 'L0_xattn_bv': _L0_xattn_in['bv'], 'L0_xattn_Wo': _L0_xattn_in['Wo'], 'L0_xattn_bo': _L0_xattn_in['bo'], 'L0_ffn_w_gate': _L0_ffn_in['w_gate'], 'L0_ffn_w_up': _L0_ffn_in['w_up'], 'L0_ffn_w_down': _L0_ffn_in['w_down'], 'L1_xattn_k': _L1_xattn_in['k'], 'L1_ffn_w_norm': _L1_ffn_in['w_norm'], 'L1_ffn_w_router': _L1_ffn_in['w_router'], 'L1_ffn_w_gate': _L1_ffn_in['w_gate'], 'L1_ffn_w_up': _L1_ffn_in['w_up'], 'L1_ffn_w_down': _L1_ffn_in['w_down'], 'L1_ffn_sw_gate': _L1_ffn_in['sw_gate'], 'L1_ffn_sw_up': _L1_ffn_in['sw_up'], 'L1_ffn_sw_down': _L1_ffn_in['sw_down'], 'L1_ffn_w_shared_gate': _L1_ffn_in['w_shared_gate'], 'L2_xattn_Wq': _L2_xattn_in['Wq'], 'L2_xattn_Wk': _L2_xattn_in['Wk'], 'L2_xattn_Wv': _L2_xattn_in['Wv'], 'L2_xattn_Wfc': _L2_xattn_in['Wfc'], 'L2_xattn_bfc': _L2_xattn_in['bfc'], 'L2_ffn_Wr': _L2_ffn_in['Wr'], 'L2_ffn_bias': _L2_ffn_in['bias'], 'L2_ffn_Wg': _L2_ffn_in['Wg'], 'L2_ffn_Wu': _L2_ffn_in['Wu'], 'L2_ffn_Wd': _L2_ffn_in['Wd'], 'L2_ffn_sWg': _L2_ffn_in['sWg'], 'L2_ffn_sWu': _L2_ffn_in['sWu'], 'L2_ffn_sWd': _L2_ffn_in['sWd'], 'L3_ffn_gate_kernel': _L3_ffn_in['gate_kernel'], 'L3_ffn_wi_0': _L3_ffn_in['wi_0'], 'L3_ffn_wi_1': _L3_ffn_in['wi_1'], 'L3_ffn_wo': _L3_ffn_in['wo']}

def reference(x, ctx_2048, fside_S2_0, mask_SxS2_bc0, mask_BxS2_bk0, L0_xattn_Wq, L0_xattn_bq, L0_xattn_Wk, L0_xattn_bk, L0_xattn_Wv, L0_xattn_bv, L0_xattn_Wo, L0_xattn_bo, L0_ffn_w_gate, L0_ffn_w_up, L0_ffn_w_down, L1_xattn_k, L1_ffn_w_norm, L1_ffn_w_router, L1_ffn_w_gate, L1_ffn_w_up, L1_ffn_w_down, L1_ffn_sw_gate, L1_ffn_sw_up, L1_ffn_sw_down, L1_ffn_w_shared_gate, L2_xattn_Wq, L2_xattn_Wk, L2_xattn_Wv, L2_xattn_Wfc, L2_xattn_bfc, L2_ffn_Wr, L2_ffn_bias, L2_ffn_Wg, L2_ffn_Wu, L2_ffn_Wd, L2_ffn_sWg, L2_ffn_sWu, L2_ffn_sWd, L3_ffn_gate_kernel, L3_ffn_wi_0, L3_ffn_wi_1, L3_ffn_wo):
    import jax
    import jax.numpy as jnp

    def _L0_xattn_ref(X, encoder_output, causal_mask, padding_mask, Wq, bq, Wk, bk, Wv, bv, Wo, bo):
        import jax, jax.numpy as jnp
        import numpy as np
        B, LQ, LKV = (4, 128, 128)
        HID, H, G = (256, 32, 8)
        HD = HID // H
        HPG = H // G
        b = X.shape[0]
        q = X @ Wq.T + bq
        k = encoder_output @ Wk.T + bk
        v = encoder_output @ Wv.T + bv
        q = q.reshape(b, LQ, G, HPG, HD).transpose(0, 2, 3, 1, 4)
        k = k.reshape(b, LKV, G, HD).transpose(0, 2, 1, 3)
        v = v.reshape(b, LKV, G, HD).transpose(0, 2, 1, 3)
        scores = jnp.einsum('bgrqd,bgkd->bgrqk', q, k) / jnp.sqrt(jnp.float32(HD))
        scores = jnp.where(causal_mask[None, None, None, :, :], -jnp.inf, scores)
        scores = jnp.where(padding_mask[:, None, None, None, :], -jnp.inf, scores)
        w = jax.nn.softmax(scores, axis=-1)
        out = jnp.einsum('bgrqk,bgkd->bgrqd', w, v)
        out = out.reshape(b, H, LQ, HD).transpose(0, 2, 1, 3).reshape(b, LQ, HID)
        return out @ Wo.T + bo

    def _L0_ffn_ref(x, w_gate, w_up, w_down):
        import jax, jax.numpy as jnp
        import numpy as np
        ACT_BITS = 8
        EPS = 1e-05

        def act_quant(x, bits=ACT_BITS):
            qb = float(2 ** (bits - 1))
            scale = qb / jnp.clip(jnp.max(jnp.abs(x), axis=-1, keepdims=True), EPS)
            xq = jnp.clip(jnp.round(x * scale), -qb, qb - 1) / scale
            return x + jax.lax.stop_gradient(xq - x)

        def weight_quant(w):
            scale = 1.0 / jnp.clip(jnp.mean(jnp.abs(w)), EPS)
            wq = jnp.clip(jnp.round(w * scale), -1.0, 1.0) / scale
            return w + jax.lax.stop_gradient(wq - w)

        def fwht(x):
            shape = x.shape
            n = shape[-1]
            x = x.reshape(-1, n)
            h = 1
            while h < n:
                x = x.reshape(-1, n // (2 * h), 2, h)
                a, b = (x[..., 0, :], x[..., 1, :])
                x = jnp.stack([a + b, a - b], axis=-2).reshape(-1, n)
                h *= 2
            return (x * (1.0 / np.sqrt(n)).astype(np.float32)).reshape(shape)

        def bitlinear(x, w):
            return jnp.einsum('bsh,oh->bso', act_quant(x), weight_quant(w))

        def h_bitlinear(x, w):
            return jnp.einsum('bsh,oh->bso', act_quant(fwht(x)), weight_quant(w))
        gate = bitlinear(x, w_gate)
        up = bitlinear(x, w_up)
        intermediate = jax.nn.silu(gate) * up
        return h_bitlinear(intermediate, w_down)

    def _L1_xattn_ref(v, k, bias, x1, x2, num_heads):
        import jax, jax.numpy as jnp
        import numpy as np
        B, D, L = v.shape
        H = D // num_heads
        fft_size = 2 * L
        vr = v.reshape(B, H, num_heads, L)
        x1r = x1.reshape(B, H, num_heads, L)
        x2r = x2.reshape(B, H, num_heads, L)
        kv = vr[:, :, :, None, :] * x2r[:, :, None, :, :]
        k_f = jnp.fft.rfft(k.astype(jnp.float32), n=fft_size)
        y = jnp.fft.irfft(jnp.fft.rfft(kv, n=fft_size) * k_f[None, :, None, None, :], n=fft_size)[..., :L]
        skip = bias.astype(jnp.float32).reshape(H, num_heads)[None, :, :, None, None]
        y = y + kv * skip
        out = jnp.einsum('bhijl,bhil->bhjl', y, x1r)
        return out.reshape(B, D, L)

    def _L1_ffn_ref(hidden_states, w_norm, w_router, w_gate, w_up, w_down, sw_gate, sw_up, sw_down, w_shared_gate):
        import jax, jax.numpy as jnp
        import numpy as np
        B, S, H = (2, 256, 256)
        E, K, F = (32, 4, 176)
        FS = 704
        EPS = 1e-06
        CAP = 128
        inp = hidden_states
        xf = inp.astype(jnp.float32)
        var = jnp.mean(xf * xf, axis=-1, keepdims=True)
        x = (w_norm * (xf * jax.lax.rsqrt(var + EPS))).astype(inp.dtype)
        Bq, Sq, Hq = x.shape
        x = x.reshape(-1, Hq)
        T = Bq * Sq
        logits = x @ w_router
        probs = jax.nn.softmax(logits.astype(jnp.float32), axis=-1)
        w_topk, sel = jax.lax.top_k(probs, K)
        w_topk = w_topk.astype(x.dtype)
        flat_e = sel.reshape(-1)
        order = jnp.argsort(flat_e)
        sorted_e = flat_e[order]
        counts = jnp.zeros((E,), jnp.int32).at[flat_e].add(1)
        starts = jnp.cumsum(counts) - counts
        pos = jnp.arange(T * K) - starts[sorted_e]
        tok = order // K
        valid = pos < CAP
        dest = jnp.where(valid, pos, CAP)
        buf = jnp.zeros((E, CAP + 1, Hq), x.dtype).at[sorted_e, dest].set(x[tok])
        buf = buf[:, :CAP]
        g = jnp.einsum('ech,ehf->ecf', buf, w_gate)
        u = jnp.einsum('ech,ehf->ecf', buf, w_up)
        y = jnp.einsum('ecf,efh->ech', jax.nn.silu(g) * u, w_down)
        wv = w_topk.reshape(-1)[order] * valid.astype(x.dtype)
        gath = y[sorted_e, jnp.minimum(pos, CAP - 1)]
        out = jnp.zeros((T, Hq), x.dtype).at[tok].add(gath * wv[:, None])
        sh = jax.nn.silu(x @ sw_gate) * (x @ sw_up) @ sw_down
        sh = jax.nn.sigmoid(x @ w_shared_gate) * sh
        out = out + sh
        return inp + out.reshape(Bq, Sq, Hq)

    def _L2_xattn_ref(q, k, v, Wq, Wk, Wv, Wfc, bfc):
        import jax, jax.numpy as jnp
        import numpy as np
        import math
        EMBED = 256
        HEADS = 32
        GROUPS = 8
        GROUP_HEADS = HEADS // GROUPS
        HEAD_DIM = EMBED // HEADS
        B, S = (4, 128)
        N, S_, _ = q.shape
        qh = (q @ Wq.T).reshape(N, S_, HEADS, HEAD_DIM).transpose(0, 2, 1, 3)
        kh = (k @ Wk.T).reshape(N, S_, GROUPS, HEAD_DIM).transpose(0, 2, 1, 3)
        vh = (v @ Wv.T).reshape(N, S_, GROUPS, HEAD_DIM).transpose(0, 2, 1, 3)
        kh = jnp.repeat(kh, GROUP_HEADS, axis=1)
        vh = jnp.repeat(vh, GROUP_HEADS, axis=1)
        score = jnp.einsum('bhqd,bhkd->bhqk', qh, kh) / math.sqrt(HEAD_DIM)
        attn = jax.nn.softmax(score, axis=-1)
        out = jnp.einsum('bhqk,bhkd->bhqd', attn, vh)
        out = out.transpose(0, 2, 1, 3).reshape(N, S_, EMBED)
        return out @ Wfc.T + bfc

    def _L2_ffn_ref(x, Wr, bias, Wg, Wu, Wd, sWg, sWu, sWd):
        import jax, jax.numpy as jnp
        import numpy as np
        TOPK = 2
        NORM_TOPK = True
        SCALE = 1.0
        EPS = 1e-09
        b, s, h = x.shape
        E = Wr.shape[0]
        xt = x.reshape(b * s, h)
        logits = xt @ Wr.T + bias
        probs = jax.nn.softmax(logits, axis=-1)
        topk_val, topk_idx = jax.lax.top_k(probs, TOPK)
        if NORM_TOPK:
            w = topk_val / (jnp.sum(topk_val, axis=-1, keepdims=True) + EPS)
        else:
            w = topk_val
        w = w * SCALE
        g = jnp.einsum('th,ehi->tei', xt, Wg)
        u = jnp.einsum('th,ehi->tei', xt, Wu)
        y = jnp.einsum('tei,eih->teh', jax.nn.silu(g) * u, Wd)
        oh = jax.nn.one_hot(topk_idx, E, dtype=x.dtype)
        routed = jnp.einsum('tke,tk,teh->th', oh, w, y)
        shared = jax.nn.silu(xt @ sWg) * (xt @ sWu) @ sWd
        return (routed + shared).reshape(b, s, h)

    def _L3_xattn_ref(q, k, v):
        import jax, jax.numpy as jnp
        import numpy as np
        N_HEAD = 8
        b, d, m = q.shape
        c = v.shape[1]
        h = N_HEAD
        qh = q.reshape(b * h, d // h, m)
        kh = k.reshape(b * h, d // h, -1)
        vh = v.reshape(b * h, c // h, -1)
        scale = 1.0 / jnp.sqrt(jnp.asarray(d // h, dtype=q.dtype))
        qk = jnp.einsum('bdm,bdn->bmn', qh, kh) * scale
        sm = jax.nn.softmax(qk, axis=-1)
        ret = jnp.einsum('bmn,bcn->bcm', sm, vh)
        return ret.reshape(b, c, m)

    def _L3_ffn_ref(x, gate_kernel, wi_0, wi_1, wo):
        import jax, jax.numpy as jnp
        import numpy as np
        TOP_K = 2
        E = gate_kernel.shape[-1]
        gate_logits = jnp.einsum('bsd,de->bse', x, gate_kernel)
        top_k_weights, top_k_indices = jax.lax.top_k(gate_logits, TOP_K)
        top_k_weights = jax.nn.softmax(top_k_weights.astype(jnp.float32), axis=-1).astype(x.dtype)
        combine_w = jnp.sum(jax.nn.one_hot(top_k_indices, E, dtype=x.dtype) * top_k_weights[..., None], axis=-2)
        h0 = jnp.einsum('bsd,edm->bsem', x, wi_0)
        h1 = jnp.einsum('bsd,edm->bsem', x, wi_1)
        h = jax.nn.silu(h0) * h1 * combine_w[..., None]
        out = jnp.einsum('bsem,emd->bsd', h, wo)
        return out
    x = x + _L0_xattn_ref(_layernorm(x, axis=-1), ctx_2048, mask_SxS2_bc0, mask_BxS2_bk0, L0_xattn_Wq, L0_xattn_bq, L0_xattn_Wk, L0_xattn_bk, L0_xattn_Wv, L0_xattn_bv, L0_xattn_Wo, L0_xattn_bo)
    x = x + _L0_ffn_ref(_layernorm(x, axis=-1), L0_ffn_w_gate, L0_ffn_w_up, L0_ffn_w_down)
    x = x + _L1_xattn_ref(_layernorm(x, axis=-1), L1_xattn_k, fside_S2_0, ctx_2048, ctx_2048, 8)
    x = x + _L1_ffn_ref(_layernorm(x, axis=-1), L1_ffn_w_norm, L1_ffn_w_router, L1_ffn_w_gate, L1_ffn_w_up, L1_ffn_w_down, L1_ffn_sw_gate, L1_ffn_sw_up, L1_ffn_sw_down, L1_ffn_w_shared_gate)
    x = x + _L2_xattn_ref(_layernorm(x, axis=-1), ctx_2048, ctx_2048, L2_xattn_Wq, L2_xattn_Wk, L2_xattn_Wv, L2_xattn_Wfc, L2_xattn_bfc)
    x = x + _L2_ffn_ref(_layernorm(x, axis=-1), L2_ffn_Wr, L2_ffn_bias, L2_ffn_Wg, L2_ffn_Wu, L2_ffn_Wd, L2_ffn_sWg, L2_ffn_sWu, L2_ffn_sWd)
    x = x + _L3_xattn_ref(_layernorm(x, axis=-1), ctx_2048, ctx_2048)
    x = x + _L3_ffn_ref(_layernorm(x, axis=-1), L3_ffn_gate_kernel, L3_ffn_wi_0, L3_ffn_wi_1, L3_ffn_wo)
    return x

_drawn_inputs = setup_inputs


def setup_inputs(seed=0):
    import zlib

    import numpy as np

    out = dict(_drawn_inputs(seed))
    spreads = {'L0_xattn_bq': (0.0, 0.8),
     'L0_xattn_bk': (0.0, 2.0),
     'L0_xattn_bv': (0.0, 0.1),
     'L0_xattn_bo': (0.0, 0.1),
     'L2_xattn_bfc': (0.0, 2.0),
     'L2_ffn_bias': (0.0, 2.0)}
    factors = {'L0_xattn_Wq': 8.0,
     'L0_xattn_Wk': 8.0,
     'L1_ffn_w_norm': 8.0,
     'L1_ffn_w_router': 8.0,
     'L1_ffn_w_gate': 8.0,
     'L1_ffn_w_up': 8.0,
     'L1_ffn_w_down': 8.0,
     'L1_ffn_sw_gate': 8.0,
     'L1_ffn_sw_up': 8.0,
     'L1_ffn_sw_down': 8.0,
     'L1_ffn_w_shared_gate': 8.0,
     'L2_xattn_Wq': 64.0,
     'L2_xattn_Wk': 64.0,
     'L2_xattn_Wv': 40.968,
     'L2_xattn_Wfc': 42.032,
     'L2_ffn_Wr': 64.0,
     'L2_ffn_Wg': 64.0,
     'L2_ffn_Wu': 64.0,
     'L2_ffn_Wd': 64.0,
     'L2_ffn_sWg': 61.037,
     'L2_ffn_sWu': 53.206,
     'L2_ffn_sWd': 53.534,
     'L3_ffn_gate_kernel': 8.0,
     'L3_ffn_wi_0': 8.0,
     'L3_ffn_wi_1': 8.0,
     'L3_ffn_wo': 8.0}
    for name, (base, spread) in spreads.items():
        noise = np.random.default_rng([zlib.crc32(name.encode()), seed]).standard_normal(out[name].shape)
        drawn = base * np.exp(spread * noise) if base else spread * noise
        out[name] = jnp.asarray(drawn.astype(out[name].dtype))
    for name, factor in factors.items():
        out[name] = (out[name] * factor).astype(out[name].dtype)
    return out
```

```python
from contextlib import ExitStack, contextmanager

import concourse.bass as bass
from concourse import mybir

P = 128
B = 16
T = B * P
D = 256
KC = D // P
H, HD = 32, 8
G = 8
R = H // G
W4 = 4 * P
LN_EPS = 1e-5
NEG = -1e30

F32 = mybir.dt.float32
BF16 = mybir.dt.bfloat16
U8 = mybir.dt.uint8
U32 = mybir.dt.uint32
I32 = mybir.dt.int32
ALU = mybir.AluOpType
ACT = mybir.ActivationFunctionType
AX = mybir.AxisListType


def over_batches(eng, body):
    body(0, 0, True, False)
    with eng.Fori(0, (B - 2) // 2) as i:
        body(i * 2 + 1, 1, False, False)
        body(i * 2 + 2, 0, False, False)
    body(B - 1, 1, False, True)


def over_tiles(eng, body, n=B):
    body(0, 0)
    body(1, 1)
    with eng.Fori(1, n // 2 - 1) as i:
        body(i * 2, 0)
        body(i * 2 + 1, 1)
    body(n - 2, 0)
    body(n - 1, 1)


def after(t, n):
    return not isinstance(t, int) or t >= n


def ahead(t, n, total=B):
    return not isinstance(t, int) or t + n < total


MAX_SLOTS = 48 * P


class Core:

    def __init__(self, nc, ctx, dram):
        self.nc, self.ctx, self.dram = nc, ctx, dram
        self.x = self.sb("x_rows", [P, B * D])
        self.stats = self.sb("ln_mean_var", [P, B, 2])
        self.rstd = self.sb("ln_rstd", [P, B])
        self.slots = nc.dram_tensor("expert_slots", (MAX_SLOTS, D), F32, kind="Internal").ap()
        self.results = nc.dram_tensor("expert_results", (MAX_SLOTS, D), F32, kind="Internal").ap()
        self.scattered = ctx.enter_context(nc.semaphore("scattered"))
        self.gathered = [ctx.enter_context(nc.semaphore(f"gathered{u}")) for u in range(2)]
        self.n_scattered, self.n_gathered = 0, 0
        self.minus_half = self.sb("minus_half", [P, B])
        self.ident = self.sb("ident", [P, P])
        self.identb = self.sb("identb", [P, P], BF16)
        self.head_of_row = self.sb("head_of_row", [P, R])
        self.chan_head_of_row = self.sb("chan_head_of_row", [P, P // 16])
        self.group_of_row = self.sb("group_of_row", [P, 4])

    def sb(self, name, shape, dt=F32, ctx=None):
        return (ctx or self.ctx).enter_context(self.nc.sbuf_tensor(name, shape, dt))

    def ps(self, name, shape, dt=F32, ctx=None):
        return (ctx or self.ctx).enter_context(self.nc.psum_tensor(name, shape, dt))

    def sem(self, name, ctx):
        s = ctx.enter_context(self.nc.semaphore(name))
        self.stage_sems.append(s.num)
        return s

    @contextmanager
    def stage(self):
        self.stage_sems = []
        with ExitStack() as st:
            yield st
        nums = sorted(self.stage_sems)
        first = nums[0]
        for n, following in zip(nums, nums[1:] + [-1]):
            if following != n + 1:
                self.nc.gpsimd.sem_clear(range(first, n + 1))
                first = following

    def xt(self, b):
        return self.x[:, bass.ds(b * D, D)]


def row_stats(dve, core, b, six):
    dve.bn_stats(six[:, :], core.xt(b))
    dve.drain()
    dve.bn_aggr(six[:, 0:2], six[:, :])
    dve.drain()
    dve.tensor_copy(core.stats[:, bass.ds(b, 1), :].rearrange("p a s -> p (a s)"), six[:, 0:2])


def all_rstd(pool, core, done):
    pool.tensor_scalar(core.rstd[:, :], core.stats[:, :, 1], LN_EPS, 1.0, ALU.add, ALU.mult)
    pool.drain()
    pool.tensor_tensor(core.rstd[:, :], core.rstd[:, :], core.minus_half[:, :], ALU.pow).then_inc(done, 1)


def normalise(dve, core, out, b):
    return dve.tensor_scalar(out, core.xt(b), core.stats[:, bass.ds(b, 1), 0], core.rstd[:, bass.ds(b, 1)],
                             ALU.subtract, ALU.mult)


def load_inputs(core):
    nc, dram = core.nc, core.dram
    with core.stage() as st:
        x_in, const, zeroed, zero_out = (core.sem(f"load_{n}", st) for n in ("x_in", "const", "zeroed", "zero_out"))
        zeros = core.sb("load_zeros", [P, D], F32, st)
        six = core.sb("load_six", [P, 6], F32, st)
        band = core.sb("load_band", [P, 4, R], F32, st)
        block = st.enter_context(nc.Block())

        @block.sync
        def _(sp):
            sp.dma_start(core.x[:, :].rearrange("p (b d) -> p b d", b=B),
                         dram["x"].rearrange("b p d -> p b d")).then_inc(x_in, 16)
            sp.wait_ge(x_in, 16)
            sp.wait_ge(zeroed, 1)
            sp.dma_start(core.slots.rearrange("(n p) d -> p n d", p=P),
                         zeros[:, :].unsqueeze(1).broadcast_to([P, MAX_SLOTS // P, D])).then_inc(zero_out, 16)
            sp.wait_ge(zero_out, 16)

        @block.gpsimd
        def _(pool):
            pool.memset(zeros[:, :], 0.0).then_inc(zeroed, 1)
            pool.memset(core.minus_half[:, :], -0.5)
            pool.memset(core.ident[:, :], 0.0).then_inc(const, 1)
            pool.memset(core.identb[:, :], 0.0).then_inc(const, 1)
            pool.wait_ge(const, 2)
            for m in (core.ident, core.identb):
                pool.affine_select(out=m[:, :], in_=m[:, :], compare_op=ALU.not_equal, fill=1.0, base=0,
                                   pattern=[[-1, P]], channel_multiplier=1).then_inc(const, 1)
            pool.memset(band[:, :, :], 1.0).then_inc(const, 1)
            pool.wait_ge(const, 5)
            pool.affine_select(out=band[:, :, :].rearrange("p g r -> p (g r)"), in_=band[:, :, :].rearrange("p g r -> p (g r)"), compare_op=ALU.is_ge, fill=0.0, base=0,
                               pattern=[[-HD, P // HD]], channel_multiplier=1).then_inc(const, 1)
            pool.wait_ge(const, 6)
            pool.affine_select(out=band[:, :, :].rearrange("p g r -> p (g r)"), in_=band[:, :, :].rearrange("p g r -> p (g r)"), compare_op=ALU.is_ge, fill=0.0, base=HD - 1,
                               pattern=[[HD, P // HD]], channel_multiplier=-1).then_inc(const, 1)

        @block.vector
        def _(dve):
            dve.wait_ge(const, 7)
            dve.tensor_reduce(core.head_of_row[:, :], band[:, :, :].rearrange("p g r -> p r g"), AX.X, ALU.add)
            dve.tensor_reduce(core.group_of_row[:, :], band[:, :, :], AX.X, ALU.add)
            dve.tensor_reduce(core.chan_head_of_row[:, :], band[:, :, :].rearrange("p g (h two) -> p (g h) two", two=2),
                              AX.X, ALU.add)
            dve.wait_ge(x_in, 16)
            for b in range(B):
                row_stats(dve, core, b, six)
                dve.drain()


def store_output(core, out):
    nc = core.nc
    with core.stage() as st:
        stored = core.sem("x_stored", st)
        block = st.enter_context(nc.Block())

        @block.sync
        def _(sp):
            sp.dma_start(out.rearrange("b p d -> p b d"),
                         core.x[:, :].rearrange("p (b d) -> p b d", b=B)).then_inc(stored, 16)
            sp.wait_ge(stored, 16)


def gqa_attention(core, name, w, masked):
    nc, dram = core.nc, core.dram
    with core.stage() as st:
        def sb(n, shape, dt=F32):
            return core.sb(f"{name}_{n}", shape, dt, st)

        def sem(n):
            return core.sem(f"{name}_{n}", st)

        wq, wk, wo = (sb(n, [P, KC, D]) for n in ("wq", "wk", "wo"))
        wv = sb("wv", [P, KC, G * HD])
        bias_o = sb("bias_o", [P, D])
        if masked:
            bias_q, bias_k = sb("bias_q", [P, KC]), sb("bias_k", [P, KC])
            bias_v = sb("bias_v", [P, G * HD])
            pad_u8, pair_u8 = sb("pad_u8", [P, T], U8), sb("pair_u8", [P, P], U8)
            pad_neg, pair_neg = sb("pad_neg", [P, T], BF16), sb("pair_neg", [P, P], BF16)
            mask = [sb(f"mask{u}", [P, P], BF16) for u in range(2)]
        ctxT = [sb(f"ctxT{u}", [P, KC, P]) for u in range(2)]
        xn = sb("xn", [P, D])
        xnT = sb("xnT", [P, KC, P])
        qT, kT = sb("qT", [P, KC, P]), sb("kT", [P, KC, P])
        q_group = [sb(f"q_group{u}", [P, G, P]) for u in range(2)]
        k_head = [sb(f"k_head{u}", [P, KC, R, P]) for u in range(2)]
        v_aug = [sb(f"v_aug{u}", [P, G, 32]) for u in range(2)]
        row_max = sb("row_max", [P, 2, R])
        prob = [sb(f"prob{s}", [P, W4]) for s in range(2)]
        probT = [sb(f"probT{s}", [P, W4]) for s in range(2)]
        o_sb = [sb(f"o_sb{c}", [P, W4]) for c in range(2)]
        recip = sb("recip", [P, R, 4])
        attn = sb("attn", [P, D])
        attnT = sb("attnT", [P, KC, P])
        y_sb = sb("y_sb", [P, D])
        six = sb("six", [P, 6])
        ps_s = [core.ps(f"{name}_ps_s{s}", [P, W4], F32, st) for s in range(2)]
        ps_t = [core.ps(f"{name}_ps_t{s}", [P, W4], F32, st) for s in range(2)]
        ps_o = [core.ps(f"{name}_ps_o{c}", [P, W4], F32, st) for c in range(2)]
        ps_in = core.ps(f"{name}_ps_in", [P, W4], F32, st)
        ps_out = core.ps(f"{name}_ps_out", [P, W4], F32, st)

        (w_in, const_done, mask_done, rstd_done, xn_done, xnT_put, xnT_done, qk_put, qk_done, q_spread,
         k_spread, v_put, v_done, s_put, max_sub, exp_done, t_put, t_done, pv_put, o_done, r_put, attn_done,
         a_put, a_done, y_put, x_done) = (sem(n) for n in (
             "w_in", "const_done", "mask_done", "rstd_done", "xn_done", "xnT_put", "xnT_done", "qk_put",
             "qk_done", "q_spread", "k_spread", "v_put", "v_done", "s_put", "max_sub", "exp_done", "t_put", "t_done",
             "pv_put", "o_done", "r_put", "attn_done", "a_put", "a_done", "y_put", "x_done"))
        ctx_in = [sem(f"ctx_in{u}") for u in range(2)]
        n_loads = 10 if masked else 5
        block = st.enter_context(nc.Block())

        @block.sync
        def _(sp):
            def load_ctx(b, u):
                sp.dma_start(ctxT[u][:, :, :], dram["ctxT"][bass.ds(b, 1)].rearrange("a p c t -> p (a c) t"))\
                  .then_inc(ctx_in[u], 16)

            load_ctx(0, 0)
            for buf, key in ((wq, "wq"), (wk, "wk"), (wv, "wv"), (wo, "wo")):
                sp.dma_start(buf[:, :, :], dram[w[key]]).then_inc(w_in, 16)
            sp.dma_start(bias_o[:, :], dram[w["bo"]].partition_broadcast(P)).then_inc(w_in, 16)
            if masked:
                sp.dma_start(bias_q[:, :], dram[w["bq"]]).then_inc(w_in, 16)
                sp.dma_start(bias_k[:, :], dram[w["bk"]]).then_inc(w_in, 16)
                sp.dma_start(bias_v[:, :], dram[w["bv"]].partition_broadcast(P)).then_inc(w_in, 16)
                sp.dma_start(pair_u8[:, :], dram["pair_mask"]).then_inc(w_in, 16)
                sp.dma_start(pad_u8[:, :], dram["pad_mask"].partition_broadcast(P)).then_inc(w_in, 16)
            load_ctx(1, 1)
            with sp.Fori(0, (B - 2) // 2) as i:
                for u in range(2):
                    sp.wait_ge(v_put, i * 2 + u + 1)
                    load_ctx(i * 2 + u + 2, u)

        @block.gpsimd
        def _(pool):
            all_rstd(pool, core, rstd_done)
            for u in range(2):
                pool.memset(q_group[u][:, :, :], 0.0).then_inc(const_done, 1)
                pool.memset(v_aug[u][:, :, :], 0.0).then_inc(const_done, 1)
            pool.wait_ge(const_done, 4)
            for u in range(2):
                pool.memset(v_aug[u][:, :, HD], 1.0).then_inc(const_done, 1)
            if masked:
                pool.wait_ge(w_in, 16 * n_loads)
                pool.tensor_scalar(pair_neg[:, :], pair_u8[:, :], NEG, 1.0, ALU.mult, ALU.mult)
                pool.tensor_scalar(pad_neg[:, :], pad_u8[:, :], NEG, 1.0, ALU.mult, ALU.mult)
                pool.drain()

            def spread(b, u):
                if masked:
                    pool.wait_ge(s_put, b * G - G) if not (isinstance(b, int) and b < 2) else None
                    pool.tensor_tensor(mask[u][:, :], pair_neg[:, :], pad_neg[:, bass.ds(b * P, P)], ALU.add)\
                        .then_inc(mask_done, 1)
                elif not (isinstance(b, int) and b < 2):
                    pool.wait_ge(s_put, b * G - G)
                pool.wait_ge(qk_done, b * 4 + 4)
                for c in range(KC):
                    pool.tensor_tensor(k_head[u][:, c, :, :],
                                       kT[:, c:c + 1, :].broadcast_to([P, R, P]),
                                       core.head_of_row[:, :].unsqueeze(2).broadcast_to([P, R, P]), ALU.mult)\
                        .then_inc(k_spread, 1)
                for c in range(KC):
                    pool.tensor_tensor(q_group[u][:, 4 * c:4 * c + 4, :],
                                       qT[:, c:c + 1, :].broadcast_to([P, 4, P]),
                                       core.group_of_row[:, :].unsqueeze(2).broadcast_to([P, 4, P]), ALU.mult)\
                        .then_inc(q_spread, 1)

            spread(0, 0)
            spread(1, 1)
            with pool.Fori(0, (B - 2) // 2) as i:
                for u in range(2):
                    spread(i * 2 + u + 2, u)

        @block.vector
        def _(dve):
            def xn_of(b):
                if not (isinstance(b, int) and b == 0):
                    dve.wait_ge(xnT_put, b)
                normalise(dve, core, xn[:, :], b).then_inc(xn_done, 1)

            def values(b, u):
                dve.wait_ge(v_put, b + 1)
                psv = ps_in[:, 0:G * HD].rearrange("p (g d) -> p g d", g=G)
                if not (isinstance(b, int) and b < 2):
                    dve.wait_ge(pv_put, b * G - G)
                if masked:
                    dve.tensor_tensor(v_aug[u][:, :, 0:HD], psv, bias_v[:, :].rearrange("p (g d) -> p g d", g=G),
                                      ALU.add).then_inc(v_done, 1)
                else:
                    dve.tensor_copy(v_aug[u][:, :, 0:HD], psv).then_inc(v_done, 1)

            def subtract_max(b, g):
                s = g % 2
                dve.wait_ge(s_put, b * G + g + 1)
                scores = ps_s[s][:, :].rearrange("p (r k) -> p r k", r=R)
                dve.tensor_reduce(row_max[:, s, :], scores, AX.X, ALU.max)
                dve.drain()
                if not (isinstance(b, int) and b == 0 and g < 2):
                    dve.wait_ge(t_put, b * G + g - 1)
                dve.tensor_tensor(prob[s][:, :].rearrange("p (r k) -> p r k", r=R), scores,
                                  row_max[:, s, :].unsqueeze(2).broadcast_to([P, R, P]), ALU.subtract)\
                   .then_inc(max_sub, 1)

            def weigh(b, c):
                dve.wait_ge(r_put, b * 2 + c + 1)
                o = ps_out[:, :].rearrange("p (r g e) -> p r g e", r=R, g=4)
                dve.reciprocal(recip[:, :, :], o[:, :, :, HD])
                dve.drain()
                if c == 0 and not (isinstance(b, int) and b == 0):
                    dve.wait_ge(a_put, b)
                dve.tensor_tensor(attn[:, c * P:c * P + P].rearrange("p (g r d) -> p r g d", g=4, r=R),
                                  o[:, :, :, 0:HD], recip[:, :, :].unsqueeze(3).broadcast_to([P, R, 4, HD]),
                                  ALU.mult).then_inc(attn_done, 1)

            def add_to_x(b):
                dve.wait_ge(y_put, b + 1)
                dve.tensor_tensor(y_sb[:, :], ps_out[:, D:2 * D], bias_o[:, :], ALU.add)
                dve.drain()
                dve.tensor_tensor(core.xt(b), core.xt(b), y_sb[:, :], ALU.add).then_inc(x_done, 1)
                dve.drain()
                row_stats_late(dve, b)

            def row_stats_late(dve, b):
                row_stats(dve, core, b, six)

            def batch(b, u, first, last):
                for g in range(G):
                    subtract_max(b, g)
                    if g == 0 and not last:
                        xn_of(b + 1)
                    if g == 3 and not first:
                        weigh(b - 1, 1)
                    if g == 5 and not last:
                        values(b + 1, 1 - u)
                    if g == 6 and not first:
                        add_to_x(b - 1)
                    if g == 7:
                        weigh(b, 0)

            dve.wait_ge(rstd_done, 1)
            xn_of(0)
            dve.wait_ge(w_in, 16 * n_loads)
            dve.wait_ge(const_done, 6)
            values(0, 0)
            over_batches(dve, batch)
            weigh(B - 1, 1)
            add_to_x(B - 1)

        @block.scalar
        def _(act):
            def copy_xnT(b):
                act.wait_ge(xnT_put, b + 1)
                if not (isinstance(b, int) and b == 0):
                    act.wait_ge(qk_put, b)
                act.activation(xnT[:, :, :].rearrange("p c t -> p (c t)"), ps_in[:, 0:D], ACT.Copy)\
                    .then_inc(xnT_done, 1)

            def copy_qk(b):
                act.wait_ge(qk_put, b + 1)
                if not (isinstance(b, int) and b == 0):
                    act.wait_ge(q_spread, b * 2)
                    act.wait_ge(k_spread, b * 2)
                for n, (to, bias) in enumerate(((qT, "q"), (kT, "k"))):
                    for c in range(KC):
                        src = ps_in[:, (n * KC + c) * P:(n * KC + c + 1) * P]
                        if masked:
                            act.activation(to[:, c, :], src, ACT.Identity,
                                           bias=(bias_q if bias == "q" else bias_k)[:, c:c + 1]).then_inc(qk_done, 1)
                        else:
                            act.activation(to[:, c, :], src, ACT.Copy).then_inc(qk_done, 1)

            def exps(b, g):
                act.wait_ge(max_sub, b * G + g + 1)
                act.activation(prob[g % 2][:, :], prob[g % 2][:, :], ACT.Exp, scale=HD ** -0.5)\
                    .then_inc(exp_done, 1)

            def copy_probT(b, g):
                act.wait_ge(t_put, b * G + g + 1)
                if not (isinstance(b, int) and b == 0 and g < 2):
                    act.wait_ge(pv_put, b * G + g - 1)
                act.activation(probT[g % 2][:, :], ps_t[g % 2][:, :], ACT.Copy).then_inc(t_done, 1)

            def copy_o(b, c):
                act.wait_ge(pv_put, b * G + 4 * c + 4)
                if not (isinstance(b, int) and b == 0):
                    act.wait_ge(r_put, b * 2 + c - 1)
                act.activation(o_sb[c][:, :], ps_o[c][:, :], ACT.Copy).then_inc(o_done, 1)

            def copy_attnT(b):
                act.wait_ge(a_put, b + 1)
                if not (isinstance(b, int) and b == 0):
                    act.wait_ge(y_put, b)
                act.activation(attnT[:, :, :].rearrange("p c t -> p (c t)"), ps_out[:, 0:D], ACT.Copy)\
                    .then_inc(a_done, 1)

            def batch(b, u, first, last):
                for g in range(G):
                    exps(b, g)
                    if g >= 1:
                        copy_probT(b, g - 1)
                    elif not first:
                        copy_probT(b - 1, G - 1)
                    if g == 1 and not first:
                        copy_o(b - 1, 1)
                    if g == 1 and not last:
                        copy_xnT(b + 1)
                    if g == 3 and not last:
                        copy_qk(b + 1)
                    if g == 4 and not first:
                        copy_attnT(b - 1)
                    if g == 5:
                        copy_o(b, 0)

            copy_xnT(0)
            act.wait_ge(w_in, 16 * n_loads)
            copy_qk(0)
            over_batches(act, batch)
            copy_probT(B - 1, G - 1)
            copy_o(B - 1, 1)
            copy_attnT(B - 1)

        @block.tensor
        def _(pe):
            def turn_xn(b):
                pe.wait_ge(xn_done, b + 1)
                if not (isinstance(b, int) and b == 0):
                    pe.wait_ge(v_done, b)
                for c in range(KC):
                    last = pe.transpose(ps_in[:, c * P:c * P + P], xn[:, c * P:c * P + P], core.ident[:, :])
                last.then_inc(xnT_put, 1)

            def project_qk(b, u):
                pe.wait_ge(xnT_done, b + 1)
                pe.wait_ge(ctx_in[u], (b - u) * 8 + 16)
                for n, (wt, src) in enumerate(((wq, xnT), (wk, ctxT[u]))):
                    for m in range(KC):
                        for c in range(KC):
                            last = pe.matmul(ps_in[:, (n * KC + m) * P:(n * KC + m + 1) * P],
                                             wt[:, c, m * P:m * P + P], src[:, c, :], start=(c == 0), stop=(c == KC - 1))
                last.then_inc(qk_put, 1)

            def project_v(b, u):
                pe.wait_ge(qk_done, b * 4 + 4)
                for c in range(KC):
                    last = pe.matmul(ps_in[:, 0:G * HD], ctxT[u][:, c, :], wv[:, c, :], start=(c == 0), stop=(c == KC - 1))
                last.then_inc(v_put, 1)

            def scores(b, g, u):
                if g == 0:
                    if masked:
                        pe.wait_ge(mask_done, b + 1)
                if g % 4 == 0:
                    pe.wait_ge(k_spread, b * 2 + g // 4 + 1)
                    pe.wait_ge(q_spread, b * 2 + g // 4 + 1)
                if not (isinstance(b, int) and b == 0 and g < 2):
                    pe.wait_ge(max_sub, b * G + g - 1)
                mm = pe.matmul(ps_s[g % 2][:, :], q_group[u][:, g, :],
                               k_head[u][:, g // 4, :, :].rearrange("p r k -> p (r k)"), start=True, stop=not masked)
                if masked:
                    mm = pe.matmul(ps_s[g % 2][:, :].rearrange("p (r k) -> p r k", r=R), core.identb[:, :],
                                   mask[u][:, :].unsqueeze(1).broadcast_to([P, R, P]), start=False, stop=True)
                mm.then_inc(s_put, 1)

            def turn_prob(b, g):
                pe.wait_ge(exp_done, b * G + g + 1)
                if not (isinstance(b, int) and b == 0 and g < 2):
                    pe.wait_ge(t_done, b * G + g - 1)
                for r in range(R):
                    last = pe.transpose(ps_t[g % 2][:, r * P:r * P + P], prob[g % 2][:, r * P:r * P + P], core.ident[:, :])
                last.then_inc(t_put, 1)

            def weigh_values(b, g, u):
                pe.wait_ge(t_done, b * G + g + 1)
                if g == 0:
                    pe.wait_ge(v_done, b + 1)
                if g % 4 == 0 and not (isinstance(b, int) and b == 0):
                    pe.wait_ge(o_done, b * 2 + g // 4 - 1)
                rows = slice(32 * (g % 4), 32 * (g % 4) + 32)
                pe.matmul(ps_o[g // 4][rows, :], v_aug[u][:, g, :], probT[g % 2][:, :], start=True, stop=True)\
                  .then_inc(pv_put, 1)

            def turn_o(b, c):
                pe.wait_ge(o_done, b * 2 + c + 1)
                if c == 1:
                    pe.wait_ge(attn_done, b * 2 + 1)
                elif not (isinstance(b, int) and b == 0):
                    pe.wait_ge(x_done, b)
                for r in range(R):
                    last = pe.transpose(ps_out[:, r * P:r * P + P], o_sb[c][:, r * P:r * P + P], core.ident[:, :])
                last.then_inc(r_put, 1)

            def turn_attn(b):
                pe.wait_ge(attn_done, b * 2 + 2)
                for c in range(KC):
                    last = pe.transpose(ps_out[:, c * P:c * P + P], attn[:, c * P:c * P + P], core.ident[:, :])
                last.then_inc(a_put, 1)

            def project_out(b):
                pe.wait_ge(a_done, b + 1)
                for c in range(KC):
                    last = pe.matmul(ps_out[:, D:2 * D], attnT[:, c, :], wo[:, c, :], start=(c == 0), stop=(c == KC - 1))
                last.then_inc(y_put, 1)

            def batch(b, u, first, last):
                for g in range(G):
                    scores(b, g, u)
                    if g >= 1:
                        turn_prob(b, g - 1)
                    elif not first:
                        turn_prob(b - 1, G - 1)
                    if g >= 2:
                        weigh_values(b, g - 2, u)
                    elif not first:
                        weigh_values(b - 1, G - 2 + g, 1 - u)
                    if g == 1 and not last:
                        turn_xn(b + 1)
                    if g == 2 and not first:
                        turn_o(b - 1, 1)
                    if g == 3 and not last:
                        project_qk(b + 1, 1 - u)
                    if g == 4 and not last:
                        project_v(b + 1, 1 - u)
                    if g == 4 and not first:
                        turn_attn(b - 1)
                    if g == 5 and not first:
                        project_out(b - 1)
                    if g == 6:
                        turn_o(b, 0)

            turn_xn(0)
            pe.wait_ge(w_in, 16 * n_loads)
            project_qk(0, 0)
            project_v(0, 0)
            over_batches(pe, batch)
            turn_prob(B - 1, G - 1)
            weigh_values(B - 1, G - 2, 1)
            weigh_values(B - 1, G - 1, 1)
            turn_o(B - 1, 1)
            turn_attn(B - 1)
            project_out(B - 1)


def channel_attention(core, name):
    nc, dram = core.nc, core.dram
    CH, CD = 8, 16
    with core.stage() as st:
        def sb(n, shape, dt=F32):
            return core.sb(f"{name}_{n}", shape, dt, st)

        def sem(n):
            return core.sem(f"{name}_{n}", st)

        ctxT = [sb(f"ctxT{u}", [P, KC, P]) for u in range(2)]
        ctx = [sb(f"ctx{u}", [P, D]) for u in range(2)]
        xn = [sb(f"xn{u}", [P, D]) for u in range(2)]
        q_head = [sb(f"q_head{u}", [P, CH, D]) for u in range(2)]
        v_aug = [sb(f"v_aug{u}", [P, KC, CH, 32]) for u in range(2)]
        row_max = sb("row_max", [P, 2, 2])
        prob = [sb(f"prob{s}", [P, W4]) for s in range(2)]
        probT = [sb(f"probT{s}", [P, W4]) for s in range(2)]
        o_sb = [sb(f"o_sb{c}", [P, D]) for c in range(2)]
        recip = sb("recip", [P, 2, 4])
        attn = sb("attn", [P, 2, P])
        six = sb("six", [P, 6])
        ps_s = [core.ps(f"{name}_ps_s{s}", [P, W4], F32, st) for s in range(2)]
        ps_t = [core.ps(f"{name}_ps_t{s}", [P, W4], F32, st) for s in range(2)]
        ps_o = [core.ps(f"{name}_ps_o{c}", [P, D], F32, st) for c in range(2)]
        ps_out = core.ps(f"{name}_ps_out", [P, W4], F32, st)
        (const_done, rstd_done, xn_done, q_spread, v_done, s_put, max_sub, exp_done, t_put, t_done, pv_put, o_done,
         r_put, attn_done, a_put, x_done) = (sem(n) for n in (
             "const_done", "rstd_done", "xn_done", "q_spread", "v_done", "s_put", "max_sub", "exp_done", "t_put",
             "t_done", "pv_put", "o_done", "r_put", "attn_done", "a_put", "x_done"))
        ctx_in = [sem(f"ctx_in{u}") for u in range(2)]
        block = st.enter_context(nc.Block())

        def ctx_loaded(eng, b, u):
            eng.wait_ge(ctx_in[u], (b - u) * 16 + 32)

        @block.sync
        def _(sp):
            def load_ctx(b, u):
                sp.dma_start(ctxT[u][:, :, :], dram["ctxT"][bass.ds(b, 1)].rearrange("a p c t -> p (a c) t"))\
                  .then_inc(ctx_in[u], 16)
                sp.dma_start(ctx[u][:, :], dram["ctx"][bass.ds(b, 1)].rearrange("a p d -> p (a d)"))\
                  .then_inc(ctx_in[u], 16)

            load_ctx(0, 0)
            load_ctx(1, 1)
            with sp.Fori(0, (B - 2) // 2) as i:
                for u in range(2):
                    sp.wait_ge(s_put, i * (2 * CH) + (u + 1) * CH)
                    sp.wait_ge(v_done, i * 2 + u + 1)
                    load_ctx(i * 2 + u + 2, u)

        @block.gpsimd
        def _(pool):
            all_rstd(pool, core, rstd_done)
            for u in range(2):
                pool.memset(v_aug[u][:, :, :, :], 0.0).then_inc(const_done, 1)
            pool.wait_ge(const_done, 2)
            for u in range(2):
                pool.memset(v_aug[u][:, :, :, CD], 1.0).then_inc(const_done, 1)

            def spread(b, u):
                pool.wait_ge(xn_done, b + 1)
                if after(b, 2):
                    pool.wait_ge(s_put, b * CH - CH)
                pool.tensor_tensor(q_head[u][:, :, :], xn[u][:, :].unsqueeze(1).broadcast_to([P, CH, D]),
                                   core.chan_head_of_row[:, :].unsqueeze(2).broadcast_to([P, CH, D]), ALU.mult)\
                    .then_inc(q_spread, 1)

            over_tiles(pool, spread)

        @block.vector
        def _(dve):
            def xn_of(b, u):
                if after(b, 2):
                    dve.wait_ge(q_spread, b - 1)
                normalise(dve, core, xn[u][:, :], b).then_inc(xn_done, 1)

            def subtract_max(b, g):
                s = g % 2
                dve.wait_ge(s_put, b * CH + g + 1)
                scores = ps_s[s][:, :].rearrange("p (r k) -> p r k", r=2)
                dve.tensor_reduce(row_max[:, s, :], scores, AX.X, ALU.max)
                dve.drain()
                if after(b, 1) or g >= 2:
                    dve.wait_ge(t_put, b * CH + g - 1)
                dve.tensor_tensor(prob[s][:, :].rearrange("p (r k) -> p r k", r=2), scores,
                                  row_max[:, s, :].unsqueeze(2).broadcast_to([P, 2, D]), ALU.subtract)\
                   .then_inc(max_sub, 1)

            def weigh(b, c):
                dve.wait_ge(r_put, b * 2 + c + 1)
                o = ps_out[:, c * D:c * D + D].rearrange("p (m h e) -> p m h e", m=2, h=4)
                dve.reciprocal(recip[:, :, :], o[:, :, :, CD])
                dve.drain()
                if c == 0 and after(b, 1):
                    dve.wait_ge(a_put, b)
                dve.tensor_tensor(attn[:, :, c * 64:c * 64 + 64].rearrange("p m (h d) -> p m h d", h=4),
                                  o[:, :, :, 0:CD], recip[:, :, :].unsqueeze(3).broadcast_to([P, 2, 4, CD]),
                                  ALU.mult).then_inc(attn_done, 1)

            def add_to_x(b):
                dve.wait_ge(a_put, b + 1)
                dve.tensor_tensor(core.xt(b), core.xt(b), ps_out[:, 0:D], ALU.add).then_inc(x_done, 1)
                dve.drain()
                row_stats(dve, core, b, six)

            def batch(b, u):
                for g in range(CH):
                    subtract_max(b, g)
                    if g == 0 and ahead(b, 1):
                        xn_of(b + 1, 1 - u)
                    if g == 3 and after(b, 1):
                        weigh(b - 1, 1)
                    if g == 5 and after(b, 1):
                        add_to_x(b - 1)
                    if g == 7:
                        weigh(b, 0)

            dve.wait_ge(rstd_done, 1)
            xn_of(0, 0)
            over_tiles(dve, batch)
            weigh(B - 1, 1)
            add_to_x(B - 1)

        @block.scalar
        def _(act):
            def values(b, u):
                ctx_loaded(act, b, u)
                if after(b, 2):
                    act.wait_ge(pv_put, b * CH - CH)
                act.activation(v_aug[u][:, :, :, 0:CD], ctxT[u][:, :, :].rearrange("p c (h d) -> p c h d", h=CH),
                               ACT.Copy).then_inc(v_done, 1)

            def exps(b, g):
                act.wait_ge(max_sub, b * CH + g + 1)
                act.activation(prob[g % 2][:, :], prob[g % 2][:, :], ACT.Exp, scale=CD ** -0.5)\
                    .then_inc(exp_done, 1)

            def copy_probT(b, g):
                act.wait_ge(t_put, b * CH + g + 1)
                if after(b, 1) or g >= 2:
                    act.wait_ge(pv_put, b * CH + g - 1)
                act.activation(probT[g % 2][:, :], ps_t[g % 2][:, :], ACT.Copy).then_inc(t_done, 1)

            def copy_o(b, c):
                act.wait_ge(pv_put, b * CH + 4 * c + 4)
                if after(b, 1):
                    act.wait_ge(r_put, b * 2 + c - 1)
                act.activation(o_sb[c][:, :], ps_o[c][:, :], ACT.Copy).then_inc(o_done, 1)

            def batch(b, u):
                for g in range(CH):
                    exps(b, g)
                    if g >= 1:
                        copy_probT(b, g - 1)
                    elif after(b, 1):
                        copy_probT(b - 1, CH - 1)
                    if g == 1 and after(b, 1):
                        copy_o(b - 1, 1)
                    if g == 4 and ahead(b, 1):
                        values(b + 1, 1 - u)
                    if g == 5:
                        copy_o(b, 0)

            act.wait_ge(const_done, 4)
            values(0, 0)
            over_tiles(act, batch)
            copy_probT(B - 1, CH - 1)
            copy_o(B - 1, 1)

        @block.tensor
        def _(pe):
            def scores(b, g, u):
                if g == 0:
                    ctx_loaded(pe, b, u)
                    pe.wait_ge(q_spread, b + 1)
                if after(b, 1) or g >= 2:
                    pe.wait_ge(max_sub, b * CH + g - 1)
                for m in range(2):
                    last = pe.matmul(ps_s[g % 2][:, m * D:m * D + D], q_head[u][:, g, m * P:m * P + P], ctx[u][:, :],
                                     start=True, stop=True)
                last.then_inc(s_put, 1)

            def turn_prob(b, g):
                pe.wait_ge(exp_done, b * CH + g + 1)
                if after(b, 1) or g >= 2:
                    pe.wait_ge(t_done, b * CH + g - 1)
                for m in range(2):
                    for n in range(2):
                        last = pe.transpose(ps_t[g % 2][:, n * D + m * P:n * D + m * P + P],
                                            prob[g % 2][:, m * D + n * P:m * D + n * P + P], core.ident[:, :])
                last.then_inc(t_put, 1)

            def weigh_values(b, g, u):
                pe.wait_ge(t_done, b * CH + g + 1)
                if g == 0:
                    pe.wait_ge(v_done, b + 1)
                if g % 4 == 0 and after(b, 1):
                    pe.wait_ge(o_done, b * 2 + g // 4 - 1)
                rows = slice(32 * (g % 4), 32 * (g % 4) + 32)
                for n in range(2):
                    last = pe.matmul(ps_o[g // 4][rows, :], v_aug[u][:, n, g, :], probT[g % 2][:, n * D:n * D + D],
                                     start=(n == 0), stop=(n == 1))
                last.then_inc(pv_put, 1)

            def turn_o(b, c):
                pe.wait_ge(o_done, b * 2 + c + 1)
                if c == 1:
                    pe.wait_ge(attn_done, b * 2 + 1)
                elif after(b, 1):
                    pe.wait_ge(x_done, b)
                for m in range(2):
                    last = pe.transpose(ps_out[:, c * D + m * P:c * D + m * P + P], o_sb[c][:, m * P:m * P + P],
                                        core.ident[:, :])
                last.then_inc(r_put, 1)

            def turn_attn(b):
                pe.wait_ge(attn_done, b * 2 + 2)
                for m in range(2):
                    last = pe.transpose(ps_out[:, m * P:m * P + P], attn[:, m, :], core.ident[:, :])
                last.then_inc(a_put, 1)

            def batch(b, u):
                for g in range(CH):
                    scores(b, g, u)
                    if g >= 1:
                        turn_prob(b, g - 1)
                    elif after(b, 1):
                        turn_prob(b - 1, CH - 1)
                    if g >= 2:
                        weigh_values(b, g - 2, u)
                    elif after(b, 1):
                        weigh_values(b - 1, CH - 2 + g, 1 - u)
                    if g == 2 and after(b, 1):
                        turn_o(b - 1, 1)
                    if g == 4 and after(b, 1):
                        turn_attn(b - 1)
                    if g == 6:
                        turn_o(b, 0)

            over_tiles(pe, batch)
            turn_prob(B - 1, CH - 1)
            weigh_values(B - 1, CH - 2, 1)
            weigh_values(B - 1, CH - 1, 1)
            turn_o(B - 1, 1)
            turn_attn(B - 1)


MAGIC = 1.5 * 2.0 ** 23
FF = 1024
NF = FF // P


def hadamard_ffn(core, name):
    nc, dram = core.nc, core.dram
    with core.stage() as st:
        def sb(n, shape, dt=F32):
            return core.sb(f"{name}_{n}", shape, dt, st)

        def sem(n):
            return core.sem(f"{name}_{n}", st)

        raw = [sb(f"w_raw{n}", [P, KC * FF]) for n in range(3)]
        wq = [sb(f"w_int{n}", [P, KC * FF], BF16) for n in range(3)]
        gate_w, up_w = (wq[n][:, :].rearrange("p (c f) -> p c f", c=KC) for n in range(2))
        down_w = wq[2][:, :].rearrange("p (c f) -> p c f", c=NF)
        had = sb("had", [P, P])
        ones = sb("ones", [P, P])
        magic = sb("magic", [P, 1])
        w_sum, w_mean, w_scale = sb("w_sum", [P, 3]), sb("w_mean", [P, 3]), sb("w_scale", [P, 3])
        xn = sb("xn", [P, D])
        xq = sb("xq", [P, D], BF16)
        xqT = [sb(f"xqT{u}", [P, KC, P], BF16) for u in range(2)]
        a_max, a_rec = sb("a_max", [P, 1]), sb("a_rec", [P, 1])
        deq = [sb(f"deq{u}", [P, 2]) for u in range(2)]
        b_max, b_rec, b_deq = sb("b_max", [P, 1]), sb("b_rec", [P, 1]), sb("b_deq", [P, 1])
        gate = sb("gate", [P, FF])
        prod = [sb(f"prod{u}", [P, FF]) for u in range(2)]
        fly = sb("fly", [P, FF])
        mixed = [sb(f"mixed{u}", [P, FF]) for u in range(2)]
        mixedT = sb("mixedT", [P, FF])
        rounded = sb("rounded", [P, FF])
        hq = sb("hq", [P, FF], BF16)
        hqT = sb("hqT", [P, FF], BF16)
        six = sb("six", [P, 6])
        ps_g = core.ps(f"{name}_ps_g", [P, FF], F32, st)
        ps_u = core.ps(f"{name}_ps_u", [P, FF], F32, st)
        ps_t = core.ps(f"{name}_ps_t", [P, FF], F32, st)
        ps_f = core.ps(f"{name}_ps_f", [P, FF], F32, st)
        ps_hqT = ps_t[:, 0:W4].bitcast(BF16)
        ps_y = ps_t[:, W4:W4 + D]
        ps_xqT = ps_t[:, W4 + D:W4 + D + P].bitcast(BF16)
        (w_in, const_done, rstd_done, sum_done, mean_put, w_done, xq_done, deq_done, xqT_put, xqT_done, gate_put,
         up_put, silu_done, prod_done, mixed_done, mixT_put, mixT_done, had_put, b_scale, round_done, hq_done,
         hqT_put, hqT_done, y_put, x_done) = (sem(n) for n in (
             "w_in", "const_done", "rstd_done", "sum_done", "mean_put", "w_done", "xq_done", "deq_done", "xqT_put",
             "xqT_done", "gate_put", "up_put", "silu_done", "prod_done", "mixed_done", "mixT_put", "mixT_done",
             "had_put", "b_scale", "round_done", "hq_done", "hqT_put", "hqT_done", "y_put", "x_done"))
        block = st.enter_context(nc.Block())

        @block.sync
        def _(sp):
            for n, key in enumerate(("l0f_wg", "l0f_wu", "l0f_wd")):
                sp.dma_start(raw[n][:, :], dram[key]).then_inc(w_in, 16)
            sp.dma_start(had[:, :], dram["had"]).then_inc(w_in, 16)

        @block.gpsimd
        def _(pool):
            all_rstd(pool, core, rstd_done)
            pool.memset(ones[:, :], 1.0).then_inc(const_done, 1)
            pool.memset(magic[:, :], MAGIC).then_inc(const_done, 1)

            def butterflies(t, u):
                pool.wait_ge(prod_done, t + 1)
                if after(t, 2):
                    pool.wait_ge(mixT_put, t - 1)
                for n, (src, dst) in enumerate(((prod[u], fly), (fly, prod[u]), (prod[u], mixed[u]))):
                    v, o = (m[:, :].rearrange("p (a two c) -> p a two c", two=2, c=P << n) for m in (src, dst))
                    if n:
                        pool.drain()
                    pool.tensor_tensor(o[:, :, 0, :], v[:, :, 0, :], v[:, :, 1, :], ALU.add)
                    last = pool.tensor_tensor(o[:, :, 1, :], v[:, :, 0, :], v[:, :, 1, :], ALU.subtract)
                last.then_inc(mixed_done, 1)

            over_tiles(pool, butterflies)

        @block.vector
        def _(dve):
            dve.wait_ge(w_in, 64)
            for n in range(3):
                dve.tensor_reduce(w_sum[:, n:n + 1], raw[n][:, :], AX.X, ALU.add, apply_absolute_value=True)\
                   .then_inc(sum_done, 1)
            dve.wait_ge(mean_put, 1)
            dve.tensor_scalar(w_mean[:, :], ps_f[:, 0:3], 1.0 / (D * FF), 1e-5, ALU.mult, ALU.max)
            dve.drain()
            dve.reciprocal(w_scale[:, :], w_mean[:, :])
            dve.drain()
            for n in range(3):
                dve.tensor_scalar(raw[n][:, :], raw[n][:, :], w_scale[:, n:n + 1], 1.0, ALU.mult, ALU.min)
                dve.drain()
                dve.tensor_scalar(raw[n][:, :], raw[n][:, :], -1.0, MAGIC, ALU.max, ALU.add)
                dve.drain()
                dve.tensor_scalar(wq[n][:, :], raw[n][:, :], MAGIC, None, ALU.subtract).then_inc(w_done, 1)

            def quantise_x(t, u):
                dve.drain()
                normalise(dve, core, xn[:, :], t)
                dve.drain()
                dve.tensor_reduce(a_max[:, :], xn[:, :], AX.X, ALU.max, apply_absolute_value=True)
                dve.drain()
                dve.tensor_scalar(a_max[:, :], a_max[:, :], 1e-5, None, ALU.max)
                dve.drain()
                dve.reciprocal(a_rec[:, :], a_max[:, :])
                if after(t, 2):
                    dve.wait_ge(silu_done, t - 1)
                dve.tensor_scalar(deq[u][:, :], w_mean[:, 0:2], a_max[:, :], 1.0 / 128, ALU.mult, ALU.mult)\
                   .then_inc(deq_done, 1)
                dve.drain()
                dve.tensor_scalar(a_rec[:, :], a_rec[:, :], 128.0, None, ALU.mult)
                dve.drain()
                dve.tensor_scalar(xn[:, :], xn[:, :], a_rec[:, :], MAGIC, ALU.mult, ALU.add)
                dve.drain()
                if after(t, 1):
                    dve.wait_ge(xqT_put, t)
                dve.tensor_scalar(xq[:, :], xn[:, :], MAGIC, 127.0, ALU.subtract, ALU.min).then_inc(xq_done, 1)

            def gate_times_up(t, u):
                dve.wait_ge(silu_done, t + 1)
                dve.wait_ge(up_put, t + 1)
                if after(t, 2):
                    dve.wait_ge(mixed_done, t - 1)
                dve.scalar_tensor_tensor(out=prod[u][:, :], in0=ps_u[:, :], scalar=deq[u][:, 1:2], in1=gate[:, :],
                                         op0=ALU.mult, op1=ALU.mult).then_inc(prod_done, 1)

            def scale_h(t):
                dve.wait_ge(had_put, t + 1)
                dve.tensor_reduce(b_max[:, :], ps_f[:, :], AX.X, ALU.max, apply_absolute_value=True)
                dve.drain()
                dve.tensor_scalar(b_max[:, :], b_max[:, :], 1.0 / 32, 1e-5, ALU.mult, ALU.max)
                dve.drain()
                dve.reciprocal(b_rec[:, :], b_max[:, :])
                dve.tensor_scalar(b_deq[:, :], b_max[:, :], w_mean[:, 2:3], 1.0 / 128, ALU.mult, ALU.mult)
                dve.drain()
                dve.tensor_scalar(b_rec[:, :], b_rec[:, :], 128.0 / 32, None, ALU.mult).then_inc(b_scale, 1)

            def quantise_h(t):
                dve.wait_ge(round_done, t + 1)
                if after(t, 1):
                    dve.wait_ge(hqT_put, t)
                dve.tensor_scalar(hq[:, :], rounded[:, :], MAGIC, 127.0, ALU.subtract, ALU.min).then_inc(hq_done, 1)

            def add_to_x(t):
                dve.wait_ge(y_put, t + 1)
                dve.scalar_tensor_tensor(out=core.xt(t), in0=ps_y, scalar=b_deq[:, :], in1=core.xt(t),
                                         op0=ALU.mult, op1=ALU.add).then_inc(x_done, 1)
                dve.drain()
                row_stats(dve, core, t, six)

            def tile(t, u):
                if ahead(t, 1):
                    gate_times_up(t + 1, 1 - u)
                scale_h(t)
                if ahead(t, 2):
                    quantise_x(t + 2, u)
                quantise_h(t)
                add_to_x(t)

            dve.wait_ge(rstd_done, 1)
            quantise_x(0, 0)
            quantise_x(1, 1)
            gate_times_up(0, 0)
            over_tiles(dve, tile)

        @block.scalar
        def _(act):
            def copy_xqT(t, u):
                act.wait_ge(xqT_put, t + 1)
                if after(t, 2):
                    act.wait_ge(up_put, t - 1)
                act.activation(xqT[u][:, :, :].rearrange("p c t -> p (c t)"), ps_xqT, ACT.Copy).then_inc(xqT_done, 1)

            def silu(t, u):
                act.wait_ge(gate_put, t + 1)
                act.wait_ge(deq_done, t + 1)
                if after(t, 1):
                    act.wait_ge(prod_done, t)
                act.activation(gate[:, :], ps_g[:, :], ACT.Silu, scale=deq[u][:, 0:1]).then_inc(silu_done, 1)

            def copy_mixedT(t):
                act.wait_ge(mixT_put, t + 1)
                if after(t, 1):
                    act.wait_ge(had_put, t)
                act.activation(mixedT[:, :], ps_t[:, :], ACT.Copy).then_inc(mixT_done, 1)

            def round_h(t):
                act.wait_ge(b_scale, t + 1)
                if after(t, 1):
                    act.wait_ge(hq_done, t)
                act.activation(rounded[:, :], ps_f[:, :], ACT.Identity, bias=magic[:, :], scale=b_rec[:, :])\
                    .then_inc(round_done, 1)

            def copy_hqT(t):
                act.wait_ge(hqT_put, t + 1)
                if after(t, 1):
                    act.wait_ge(y_put, t)
                act.activation(hqT[:, :], ps_hqT, ACT.Copy).then_inc(hqT_done, 1)

            def tile(t, u):
                if ahead(t, 1):
                    silu(t + 1, 1 - u)
                copy_mixedT(t)
                if ahead(t, 2):
                    copy_xqT(t + 2, u)
                round_h(t)
                copy_hqT(t)

            act.wait_ge(const_done, 2)
            copy_xqT(0, 0)
            copy_xqT(1, 1)
            silu(0, 0)
            over_tiles(act, tile)

        @block.tensor
        def _(pe):
            def turn_xq(t, u):
                pe.wait_ge(xq_done, t + 1)
                if after(t, 1):
                    pe.wait_ge(xqT_done, t)
                for c in range(KC):
                    last = pe.transpose(ps_xqT[:, c * P:c * P + P], xq[:, c * P:c * P + P], core.identb[:, :])
                last.then_inc(xqT_put, 1)

            def gate_up(t, u):
                pe.wait_ge(xqT_done, t + 1)
                for ps, w, free, put in ((ps_g, gate_w, silu_done, gate_put), (ps_u, up_w, prod_done, up_put)):
                    if after(t, 1):
                        pe.wait_ge(free, t)
                    for h in range(2):
                        for c in range(KC):
                            last = pe.matmul(ps[:, h * W4:h * W4 + W4], xqT[u][:, c, :], w[:, c, h * W4:h * W4 + W4],
                                             start=(c == 0), stop=(c == KC - 1))
                    last.then_inc(put, 1)

            def turn_mixed(t, u):
                pe.wait_ge(mixed_done, t + 1)
                if ahead(t, 1):
                    pe.wait_ge(xqT_done, t + 2)
                if after(t, 1):
                    pe.wait_ge(x_done, t)
                for c in range(NF):
                    last = pe.transpose(ps_t[:, c * P:c * P + P], mixed[u][:, c * P:c * P + P], core.ident[:, :])
                last.then_inc(mixT_put, 1)

            def transform(t):
                pe.wait_ge(mixT_done, t + 1)
                if after(t, 1):
                    pe.wait_ge(round_done, t)
                for c in range(NF):
                    last = pe.matmul(ps_f[:, c * P:c * P + P], mixedT[:, c * P:c * P + P], had[:, :], start=True, stop=True)
                last.then_inc(had_put, 1)

            def turn_hq(t):
                pe.wait_ge(hq_done, t + 1)
                for c in range(NF):
                    last = pe.transpose(ps_hqT[:, c * P:c * P + P], hq[:, c * P:c * P + P], core.identb[:, :])
                last.then_inc(hqT_put, 1)

            def down(t):
                pe.wait_ge(hqT_done, t + 1)
                for c in range(NF):
                    last = pe.matmul(ps_y, hqT[:, c * P:c * P + P], down_w[:, c, :], start=(c == 0), stop=(c == NF - 1))
                last.then_inc(y_put, 1)

            def tile(t, u):
                if ahead(t, 1):
                    gate_up(t + 1, 1 - u)
                turn_mixed(t, u)
                transform(t)
                if ahead(t, 2):
                    turn_xq(t + 2, u)
                turn_hq(t)
                down(t)

            pe.wait_ge(const_done, 2)
            pe.wait_ge(sum_done, 3)
            pe.matmul(ps_f[:, 0:3], ones[:, :], w_sum[:, :], start=True, stop=True).then_inc(mean_put, 1)
            turn_xq(0, 0)
            turn_xq(1, 1)
            pe.wait_ge(w_done, 3)
            gate_up(0, 0)
            over_tiles(pe, tile)


def gated_long_conv(core, name):
    nc, dram = core.nc, core.dram
    NH, N8 = 16, 8
    COLS = B * N8 * N8
    with core.stage() as st:
        def sb(n, shape, dt=F32, c=st):
            return core.sb(f"{name}_{n}", shape, dt, c)

        def sem(n):
            return core.sem(f"{name}_{n}", st)

        ctxT = sb("ctxT", [P, KC, B, P])
        vT = sb("vT", [P, KC, B, P])
        outT = sb("outT", [P, KC, B, P])
        xn = [sb(f"xn{u}", [P, D]) for u in range(2)]
        skip = sb("skip", [P, P])
        taps = sb("taps", [P, NH, D])
        six = sb("six", [P, 6])
        (ctx_in, taps_in, rstd_done, xn_done, xnT_put, xnT_done, kv_done, tap_done, y_put, z_done, fold_done,
         gated, skip_sum, skip_done, out_put, x_done) = (sem(n) for n in (
             "ctx_in", "taps_in", "rstd_done", "xn_done", "xnT_put", "xnT_done", "kv_done", "tap_done", "y_put",
             "z_done", "fold_done", "gated", "skip_sum", "skip_done", "out_put", "x_done"))

        with ExitStack() as ph:
            ps = [core.ps(f"{name}_ps_x{u}", [P, W4], F32, ph) for u in range(2)]
            block = ph.enter_context(nc.Block())

            @block.sync
            def _(sp):
                for c in range(KC):
                    sp.dma_start(ctxT[:, c, :, :], dram["ctxT"][:, :, c, :].rearrange("b p t -> p b t"))\
                      .then_inc(ctx_in, 16)
                sp.dma_start(skip[:, :], dram["skip"].partition_broadcast(P)).then_inc(ctx_in, 16)
                sp.dma_start(taps[:, :, :], dram["l1a_taps"]).then_inc(taps_in, 16)

            @block.gpsimd
            def _(pool):
                all_rstd(pool, core, rstd_done)

            @block.vector
            def _(dve):
                dve.wait_ge(rstd_done, 1)

                def tile(b, u):
                    if after(b, 2):
                        dve.wait_ge(xnT_put, b - 1)
                    normalise(dve, core, xn[u][:, :], b).then_inc(xn_done, 1)

                over_tiles(dve, tile)

            @block.scalar
            def _(act):
                def tile(b, u):
                    act.wait_ge(xnT_put, b + 1)
                    act.activation(vT[:, :, bass.ds(b, 1), :].rearrange("p c a t -> p c (a t)"),
                                   ps[u][:, 0:D].rearrange("p (c t) -> p c t", c=KC), ACT.Copy).then_inc(xnT_done, 1)

                over_tiles(act, tile)

            @block.tensor
            def _(pe):
                def tile(b, u):
                    pe.wait_ge(xn_done, b + 1)
                    if after(b, 2):
                        pe.wait_ge(xnT_done, b - 1)
                    for c in range(KC):
                        last = pe.transpose(ps[u][:, c * P:c * P + P], xn[u][:, c * P:c * P + P], core.ident[:, :])
                    last.then_inc(xnT_put, 1)

                over_tiles(pe, tile)

        with ExitStack() as ph:
            kv = [sb(f"kv{u}", [P, KC, COLS], F32, ph) for u in range(2)]
            tap = [sb(f"tap{u}", [P, D], F32, ph) for u in range(2)]
            z = [sb(f"z{c}", [P, COLS], F32, ph) for c in range(2)]
            ps = [[core.ps(f"{name}_ps_y{u}{c}", [P, COLS], F32, ph) for c in range(KC)] for u in range(2)]
            block = ph.enter_context(nc.Block())

            @block.gpsimd
            def _(pool):
                pool.wait_ge(ctx_in, 48)

                def outer(h, u):
                    for c in range(KC):
                        i_rows = vT[:, c, :, bass.ds(h * N8, N8)].unsqueeze(3).broadcast_to([P, B, N8, N8])
                        j_rows = ctxT[:, c, :, bass.ds(h * N8, N8)].unsqueeze(2).broadcast_to([P, B, N8, N8])
                        if c == 0 and after(h, 2):
                            pool.wait_ge(y_put, h * 2 - 2)
                        pool.tensor_tensor(kv[u][:, c, :].rearrange("p (b i j) -> p b i j", b=B, i=N8),
                                           i_rows, j_rows, ALU.mult).then_inc(kv_done, 1)

                over_tiles(pool, outer, NH)

            @block.scalar
            def _(act):
                act.wait_ge(taps_in, 16)

                def stage(h, u):
                    if after(h, 2):
                        act.wait_ge(y_put, h * 2 - 2)
                    act.activation(tap[u][:, :], taps[:, bass.ds(h, 1), :].rearrange("p a l -> p (a l)"), ACT.Copy)\
                        .then_inc(tap_done, 1)

                over_tiles(act, stage, NH)

            @block.tensor
            def _(pe):
                def conv(h, u):
                    pe.wait_ge(tap_done, h + 1)
                    for c in range(KC):
                        pe.wait_ge(kv_done, h * 2 + c + 1)
                        if after(h, 2):
                            pe.wait_ge(z_done, h * 2 - 3 + c)
                        for n in range(2):
                            cols = slice(n * W4, n * W4 + W4)
                            for m in range(c + 1):
                                last = pe.matmul(ps[u][c][:, cols], tap[u][:, (c - m) * P:(c - m) * P + P],
                                                 kv[u][:, m, cols], start=(m == 0), stop=(m == c))
                        last.then_inc(y_put, 1)

                over_tiles(pe, conv, NH)

            @block.vector
            def _(dve):
                dve.wait_ge(ctx_in, 48)

                def gate(h, u):
                    for c in range(KC):
                        dve.wait_ge(y_put, h * 2 + c + 1)
                        x1 = ctxT[:, c, :, bass.ds(h * N8, N8)].unsqueeze(3).broadcast_to([P, B, N8, N8])
                        if after(h, 1):
                            dve.wait_ge(fold_done, h * 2 - 1 + c)
                        dve.tensor_tensor(z[c][:, :].rearrange("p (b i j) -> p b i j", b=B, i=N8),
                                          ps[u][c][:, :].rearrange("p (b i j) -> p b i j", b=B, i=N8), x1, ALU.mult)\
                           .then_inc(z_done, 1)
                    for c in range(KC):
                        dve.wait_ge(z_done, h * 2 + c + 1)
                        dve.tensor_reduce(outT[:, c, :, bass.ds(h * N8, N8)],
                                          z[c][:, :].rearrange("p (b i j) -> p b j i", b=B, i=N8), AX.X, ALU.add)\
                           .then_inc(fold_done, 1)

                over_tiles(dve, gate, NH)

        with ExitStack() as ph:
            weight = sb("skip_weight", [P, KC, B, NH], F32, ph)
            ps = [core.ps(f"{name}_ps_o{u}", [P, W4], F32, ph) for u in range(2)]
            block = ph.enter_context(nc.Block())

            @block.gpsimd
            def _(pool):
                for c in range(KC):
                    pool.tensor_tensor(vT[:, c, :, :], vT[:, c, :, :], ctxT[:, c, :, :], ALU.mult)
                    pool.drain()
                    pool.tensor_tensor(vT[:, c, :, :], vT[:, c, :, :],
                                       skip[:, :].unsqueeze(1).broadcast_to([P, B, P]), ALU.mult).then_inc(gated, 1)

            @block.vector
            def _(dve):
                for c in range(KC):
                    dve.wait_ge(gated, c + 1)
                    dve.tensor_reduce(weight[:, c, :, :], vT[:, c, :, :].rearrange("p b (h i) -> p b h i", i=N8),
                                      AX.X, ALU.add)
                    dve.drain()
                    dve.tensor_tensor(vT[:, c, :, :].rearrange("p b (h j) -> p b h j", j=N8),
                                      weight[:, c, :, :].unsqueeze(3).broadcast_to([P, B, NH, N8]),
                                      ctxT[:, c, :, :].rearrange("p b (h j) -> p b h j", j=N8), ALU.mult)
                    dve.drain()
                    dve.tensor_tensor(outT[:, c, :, :], outT[:, c, :, :], vT[:, c, :, :], ALU.add)\
                       .then_inc(skip_done, 1)
                for b in range(B):
                    dve.wait_ge(out_put, b + 1)
                    dve.tensor_tensor(core.xt(b), core.xt(b), ps[b % 2][:, 0:D], ALU.add).then_inc(x_done, 1)
                    dve.drain()
                    row_stats(dve, core, b, six)

            @block.tensor
            def _(pe):
                pe.wait_ge(skip_done, KC)
                for b in range(B):
                    if b >= 2:
                        pe.wait_ge(x_done, b - 1)
                    for c in range(KC):
                        last = pe.transpose(ps[b % 2][:, c * P:c * P + P], outT[:, c, b, :], core.ident[:, :])
                    last.then_inc(out_put, 1)


def over_ring(eng, body, n, ring):
    for r in range(ring):
        body(r, r)
    with eng.Fori(1, n // ring - 1) as i:
        for r in range(ring):
            body(i * ring + r, r)
    for r in range(ring):
        body(n - ring + r, r)


RING = 4


def moe_ffn(core, name, E, K, FE, capacity=None, shared=0, rms=False, biased=False, renorm=False, top_softmax=False):
    nc, dram = core.nc, core.dram
    NT = E * capacity // P if capacity else T * K // P + E
    NT += NT % RING and RING - NT % RING
    FCH = FE // 2 if FE > P else FE
    NJ = FE // FCH
    NL = E + (1 if rms else 0)
    FS = -(-shared // P)
    with core.stage() as st:
        def sb(n, shape, dt=F32):
            return core.sb(f"{name}_{n}", shape, dt, st)

        def sem(n):
            return core.sem(f"{name}_{n}", st)

        rows = sb("rows", [P, B, D])
        row1 = [sb(f"row1_{u}", [P, D]) for u in range(2)]
        xT1 = [sb(f"xT1_{u}", [P, KC, P]) for u in range(2)]
        router = sb("router", [P, KC, NL])
        logit = sb("logit", [P, B, NL])
        prob = sb("prob", [P, B, E])
        red = sb("red", [P, B])
        top, top_i = sb("top", [P, B, 8]), sb("top_i", [P, B, 8], U32)
        topf = sb("topf", [P, B, 8])
        expert = sb("expert", [P, E])
        onehot = sb("onehot", [P, B, K, E])
        chosen = sb("chosen", [P, 2 * B, E], BF16)
        before, onesb = sb("before", [P, P], BF16), sb("onesb", [P, P], BF16)
        place = sb("place", [P, B, E])
        spot = sb("spot", [P, B, K])
        spot2 = sb("spot2", [P, B, K])
        flag = sb("flag", [P, B, K])
        weight = sb("weight", [P, B, K])
        to_slot, from_slot = sb("to_slot", [P, B, K], U32), sb("from_slot", [P, B, K], U32)
        six = sb("six", [P, 6])
        xin = [sb(f"xin{r}", [P, D]) for r in range(RING)]
        xinT = [sb(f"xinT{u}", [P, KC, P]) for u in range(2)]
        act_sb = [sb(f"act_sb{u}", [P, FE]) for u in range(2)]
        h_sb = [sb(f"h_sb{u}", [P, FE]) for u in range(2)]
        hT_sb = [sb(f"hT_sb{u}", [FCH, NJ, P]) for u in range(2)]
        y_sb = [sb(f"y_sb{u}", [P, D]) for u in range(2)]
        got = [sb(f"got{u}", [P, K, D]) for u in range(2)]
        if capacity:
            w_gu = [sb(f"w_gu{r}", [P, KC, 2 * FE]) for r in range(RING)]
            w_d = [sb(f"w_d{r}", [FCH, NJ, D]) for r in range(RING)]
        else:
            w_gu_all = sb("w_gu_all", [P, E * KC * 2 * FE])
            w_d_all = sb("w_d_all", [FCH, E * NJ * D])
            tiles, ends, base = sb("tiles", [P, E]), sb("ends", [P, E]), sb("base", [P, E])
            ones_e = sb("ones_e", [P, E])
            tile_no = sb("tile_no", [P, NT])
            past = sb("past", [P, NT, E])
            owner, owner_i = sb("owner", [P, NT]), sb("owner_i", [P, NT], I32)
        if biased:
            bias = sb("bias", [P, E])
        if rms:
            norm_w = sb("norm_w", [P, D])
            square, squares, rms_f = sb("square", [P, D]), sb("squares", [P, B]), sb("rms_f", [P, B])
            gate_f = sb("gate_f", [P, B])
        if shared:
            xT = sb("xT", [P, KC, T])
            sw_g, sw_u = sb("sw_g", [P, KC, shared]), sb("sw_u", [P, KC, shared])
            sw_d = sb("sw_d", [P, FS, D])
            s_act = [sb(f"s_act{u}", [P, W4]) for u in range(2)]
            s_hT = [sb(f"s_hT{u}", [P, FS, W4]) for u in range(2)]
        ps_x = [core.ps(f"{name}_ps_x{u}", [P, D], F32, st) for u in range(2)]
        ps_l = core.ps(f"{name}_ps_l", [P, W4], F32, st)
        ps_p = core.ps(f"{name}_ps_p", [P, W4], F32, st)
        ps_g = [core.ps(f"{name}_ps_g{u}", [P, W4], F32, st) for u in range(2)]
        ps_u = [core.ps(f"{name}_ps_u{u}", [P, W4], F32, st) for u in range(2)]
        (w_in, sw_in, ew_in, const_done, rstd_done, ln_done, sq_done, rms_done, row_done, row_kept, xT_put, xT_done,
         l_put, l_done, max_done, e_done, chosen_done, place_put, counted, owner_done, to_done, from_done, gate_e,
         sg_put, s_silu, s_mul, sd_put, sd_done, in_turned, in_copied, gu_put, e_silu, e_mul, h_turned,
         h_copied, yd_put, y_copied, added) = (sem(n) for n in (
             "w_in", "sw_in", "ew_in", "const_done", "rstd_done", "ln_done", "sq_done", "rms_done", "row_done",
             "row_kept", "xT_put", "xT_done", "l_put", "l_done", "max_done", "e_done", "chosen_done", "place_put",
             "counted", "owner_done", "to_done", "from_done", "gate_e", "sg_put", "s_silu", "s_mul",
             "sd_put", "sd_done", "in_turned", "in_copied", "gu_put", "e_silu", "e_mul", "h_turned", "h_copied",
             "yd_put", "y_copied", "added"))
        xin_in = [sem(f"xin_in{r}") for r in range(RING)]
        ring_in = [sem(f"ring_in{r}") for r in range(RING)]
        y_out = [sem(f"y_out{r}") for r in range(2)]
        scattered, got_in = core.scattered, core.gathered
        scattered_before, got_before = core.n_scattered, core.n_gathered
        core.n_scattered += B * K * 16
        core.n_gathered += B // 2 * K * 16
        n_loads = 1 + rms + biased
        slots, results = core.slots[0:NT * P, :], core.results[0:NT * P, :]
        block = st.enter_context(nc.Block())

        def chunk_rows(f):
            return min(P, shared - f * P)

        @block.sync
        def _(sp):
            sp.dma_start(router[:, :, :], dram[f"{name}_router"]).then_inc(w_in, 16)
            if biased:
                sp.dma_start(bias[:, :], dram[f"{name}_bias"].partition_broadcast(P)).then_inc(w_in, 16)
            if rms:
                sp.dma_start(norm_w[:, :], dram[f"{name}_norm_w"].partition_broadcast(P)).then_inc(w_in, 16)
            if shared:
                sp.dma_start(sw_g[:, :, :], dram[f"{name}_sw_g"]).then_inc(sw_in, 16)
                sp.dma_start(sw_u[:, :, :], dram[f"{name}_sw_u"]).then_inc(sw_in, 16)
                whole = shared // P * P
                sp.dma_start(sw_d[:, 0:shared // P, :], dram[f"{name}_sw_d"][0:whole, :]
                             .rearrange("(f p) d -> p f d", p=P)).then_inc(sw_in, 16)
                if shared > whole:
                    sp.dma_start(sw_d[0:shared - whole, FS - 1, :], dram[f"{name}_sw_d"][whole:shared, :])\
                      .then_inc(sw_in, 16)
            if not capacity:
                sp.dma_start(w_gu_all[:, :].rearrange("p (e n) -> p e n", e=E), dram[f"{name}_w_gu"]
                             .rearrange("e p c n -> p e (c n)")).then_inc(ew_in, 16)
                sp.dma_start(w_d_all[:, :].rearrange("p (e n) -> p e n", e=E), dram[f"{name}_w_d"]
                             .rearrange("e p c n -> p e (c n)")).then_inc(ew_in, 16)

            def store(j, u):
                sp.wait_ge(y_copied, j + 1)
                sp.dma_start(results[bass.ds(j * P, P), :], y_sb[u][:, :]).then_inc(y_out[u], 16)

            def load(j, r):
                if capacity:
                    if after(j, RING):
                        sp.wait_ge(yd_put, j - (RING - 1))
                    sp.dma_start(w_gu[r][:, :, :], dram[f"{name}_w_gu"][bass.ds(j, 1)]
                                 .rearrange("e p c n -> p (e c) n")).then_inc(ring_in[r], 16)
                    sp.dma_start(w_d[r][:, :, :], dram[f"{name}_w_d"][bass.ds(j, 1)]
                                 .rearrange("e p c n -> p (e c) n")).then_inc(ring_in[r], 16)
                if isinstance(j, int) and j == 0:
                    sp.wait_ge(scattered, scattered_before + B * K * 16)
                if after(j, RING):
                    sp.wait_ge(in_turned, j - (RING - 1))
                sp.dma_start(xin[r][:, :], slots[bass.ds(j * P, P), :]).then_inc(xin_in[r], 16)
                if after(j, 3):
                    store(j - 3, (r + 1) % 2)

            over_ring(sp, load, NT, RING)
            for j in range(NT - 3, NT):
                store(j, j % 2)

        @block.gpsimd
        def _(pool):
            all_rstd(pool, core, rstd_done)
            pool.iota(expert[:, :], [[1, E]], base=0, channel_multiplier=0, allow_small_or_imprecise_dtypes=True)\
                .then_inc(const_done, 1)
            pool.memset(before[:, :], 1.0).then_inc(const_done, 1)
            pool.memset(onesb[:, :], 1.0).then_inc(const_done, 1)
            pool.wait_ge(const_done, 3)
            pool.affine_select(out=before[:, :], in_=before[:, :], compare_op=ALU.is_gt, fill=0.0, base=0,
                               pattern=[[1, P]], channel_multiplier=-1).then_inc(const_done, 1)
            if not capacity:
                pool.memset(ones_e[:, :], 1.0).then_inc(const_done, 1)
                pool.iota(tile_no[:, :], [[1, NT]], base=0, channel_multiplier=0,
                          allow_small_or_imprecise_dtypes=True).then_inc(const_done, 1)
            if rms:
                pool.wait_ge(sq_done, B)
                pool.tensor_scalar(rms_f[:, :], squares[:, :], 1.0 / D, 1e-6, ALU.mult, ALU.add)
                pool.drain()
                pool.tensor_tensor(rms_f[:, :], rms_f[:, :], core.minus_half[:, :], ALU.pow).then_inc(rms_done, 1)
            pool.wait_ge(to_done, 1)
            pool.wait_ge(row_kept, B)
            for t in range(B):
                for k in range(K):
                    limit = dict(bounds_check=E * capacity - 1, oob_is_err=False) if capacity else {}
                    pool.indirect_dma_start(
                        out=slots, out_offset=bass.IndirectOffsetOnAxis(ap=to_slot[:, t, k:k + 1], axis=0),
                        in_=rows[:, t, :], in_offset=None, **limit).then_inc(scattered, 16)
            pool.wait_ge(from_done, 1)
            for u in range(2):
                pool.wait_ge(y_out[u], NT // 2 * 16)
            for t in range(B):
                if t >= 2:
                    pool.wait_ge(added, t - 1)
                for k in range(K):
                    pool.indirect_dma_start(
                        out=got[t % 2][:, k, :], out_offset=None, in_=results,
                        in_offset=bass.IndirectOffsetOnAxis(ap=from_slot[:, t, k:k + 1], axis=0))\
                        .then_inc(got_in[t % 2], 16)

        @block.vector
        def _(dve):
            dve.memset(chosen[:, 0:B, :], 0.0)
            dve.wait_ge(rstd_done, 1)
            if rms:
                def first(t, u):
                    normalise(dve, core, rows[:, bass.ds(t, 1), :].rearrange("p a d -> p (a d)"), t)
                    dve.drain()
                    dve.tensor_tensor(core.xt(t), core.xt(t), rows[:, bass.ds(t, 1), :].rearrange("p a d -> p (a d)"),
                                      ALU.add).then_inc(ln_done, 1)

                over_tiles(dve, first)
                dve.wait_ge(rms_done, 1)
            dve.wait_ge(w_in, 16 * n_loads)

            def row(t, u):
                if after(t, 2):
                    dve.wait_ge(row_kept, t - 1)
                    dve.wait_ge(xT_put, t - 1)
                if rms:
                    dve.scalar_tensor_tensor(out=row1[u][:, :], in0=rows[:, bass.ds(t, 1), :].rearrange("p a d -> p (a d)"),
                                             scalar=rms_f[:, bass.ds(t, 1)], in1=norm_w[:, :], op0=ALU.mult,
                                             op1=ALU.mult).then_inc(row_done, 1)
                else:
                    normalise(dve, core, row1[u][:, :], t).then_inc(row_done, 1)

            def keep_logits(t):
                dve.wait_ge(l_put, t + 1)
                out = logit[:, bass.ds(t, 1), :].rearrange("p a e -> p (a e)")
                if biased:
                    dve.tensor_tensor(out, ps_l[:, 0:NL], bias[:, :], ALU.add).then_inc(l_done, 1)
                else:
                    dve.tensor_copy(out, ps_l[:, 0:NL]).then_inc(l_done, 1)

            def tile(t, u):
                if ahead(t, 1):
                    row(t + 1, 1 - u)
                keep_logits(t)

            row(0, 0)
            over_tiles(dve, tile)
            dve.drain()

            logits = logit[:, :, 0:E]
            if top_softmax:
                ranked = logit
            else:
                ranked = prob
                dve.tensor_reduce(red[:, :], logits, AX.X, ALU.max)
                dve.drain()
                dve.tensor_tensor(prob[:, :, :], logits, red[:, :].unsqueeze(2).broadcast_to([P, B, E]), ALU.subtract)\
                   .then_inc(max_done, 1)
                dve.wait_ge(e_done, 1)
                dve.tensor_reduce(red[:, :], prob[:, :, :], AX.X, ALU.add)
                dve.drain()
                dve.reciprocal(red[:, :], red[:, :])
                dve.drain()
                dve.tensor_tensor(prob[:, :, :], prob[:, :, :], red[:, :].unsqueeze(2).broadcast_to([P, B, E]), ALU.mult)
                dve.drain()
            for t in range(B):
                dve.max(top[:, t, :], ranked[:, t, 0:E])
            dve.drain()
            for t in range(B):
                dve.max_index(top_i[:, t, :], top[:, t, :], ranked[:, t, 0:E])
            dve.drain()
            dve.tensor_copy(topf[:, :, :], top_i[:, :, :])
            dve.wait_ge(const_done, 4 if capacity else 6)
            dve.drain()
            for k in range(K):
                dve.tensor_tensor(onehot[:, :, k, :], expert[:, :].unsqueeze(1).broadcast_to([P, B, E]),
                                  topf[:, :, k:k + 1].broadcast_to([P, B, E]), ALU.is_equal)
            dve.drain()
            with nc.allow_low_precision(reason="zeros and ones"):
                dve.tensor_reduce(chosen[:, B:, :], onehot[:, :, :, :].rearrange("p t k e -> p t e k"), AX.X, ALU.add)\
                   .then_inc(chosen_done, 1)
            if top_softmax:
                dve.tensor_tensor(weight[:, :, :], top[:, :, 0:K], top[:, :, 0:1].broadcast_to([P, B, K]), ALU.subtract)\
                   .then_inc(max_done, 1)
                dve.wait_ge(e_done, 1)
                source = weight[:, :, :]
            else:
                source = top[:, :, 0:K]
            if top_softmax or renorm:
                dve.tensor_reduce(red[:, :], source, AX.X, ALU.add)
                dve.drain()
                if renorm:
                    dve.tensor_scalar(red[:, :], red[:, :], 1e-9, None, ALU.add)
                    dve.drain()
                dve.reciprocal(red[:, :], red[:, :])
                dve.drain()
                dve.tensor_tensor(weight[:, :, :], source, red[:, :].unsqueeze(2).broadcast_to([P, B, K]), ALU.mult)
            if rms:
                dve.wait_ge(gate_e, 1)
                dve.tensor_scalar(gate_f[:, :], gate_f[:, :], 1.0, None, ALU.add)
                dve.drain()
                dve.reciprocal(gate_f[:, :], gate_f[:, :])
            dve.wait_ge(place_put, 1)
            if capacity:
                dve.tensor_copy(place[:, :, :], ps_p[:, 0:B * E].rearrange("p (t e) -> p t e", t=B))
            else:
                dve.wait_ge(counted, 1)
                dve.tensor_scalar(tiles[:, :], ps_l[:, 0:E], 127.0, 1.0 / P, ALU.add, ALU.mult)
                dve.drain()
                dve.tensor_scalar(tiles[:, :], tiles[:, :], 1.0 / 256 - 0.5, MAGIC, ALU.add, ALU.add)
                dve.drain()
                dve.tensor_scalar(tiles[:, :], tiles[:, :], MAGIC, None, ALU.subtract)
                dve.drain()
                dve.tensor_tensor_scan(ends[:, :], ones_e[:, :], tiles[:, :], 0.0, ALU.mult, ALU.add)
                dve.drain()
                dve.tensor_tensor(base[:, :], ends[:, :], tiles[:, :], ALU.subtract)
                dve.tensor_tensor(past[:, :, :], tile_no[:, :].unsqueeze(2).broadcast_to([P, NT, E]),
                                  ends[:, :].unsqueeze(1).broadcast_to([P, NT, E]), ALU.is_ge)
                dve.drain()
                dve.tensor_scalar(base[:, :], base[:, :], float(P), None, ALU.mult)
                dve.tensor_reduce(owner[:, :], past[:, :, :], AX.X, ALU.add)
                dve.drain()
                dve.tensor_scalar(owner_i[:, :], owner[:, :], float(E - 1), None, ALU.min).then_inc(owner_done, 1)
                dve.tensor_tensor(place[:, :, :], ps_p[:, 0:B * E].rearrange("p (t e) -> p t e", t=B),
                                  base[:, :].unsqueeze(1).broadcast_to([P, B, E]), ALU.add)
            dve.drain()
            for k in range(K):
                dve.tensor_tensor(onehot[:, :, k, :], onehot[:, :, k, :], place[:, :, :], ALU.mult)
            dve.drain()
            dve.tensor_reduce(spot[:, :, :], onehot[:, :, :, :], AX.X, ALU.add)
            dve.drain()
            if capacity:
                dve.tensor_scalar(flag[:, :, :], spot[:, :, :], float(capacity), None, ALU.is_lt)
                dve.tensor_scalar(spot2[:, :, :], spot[:, :, :], float(capacity - 1), None, ALU.min)
                dve.drain()
                dve.tensor_tensor(weight[:, :, :], top[:, :, 0:K], flag[:, :, :], ALU.mult)
                dve.scalar_tensor_tensor(out=spot2[:, :, :], in0=topf[:, :, 0:K], scalar=float(capacity),
                                         in1=spot2[:, :, :], op0=ALU.mult, op1=ALU.add)
                dve.drain()
                dve.tensor_scalar(flag[:, :, :], flag[:, :, :], -float(2 * T * K), float(2 * T * K), ALU.mult, ALU.add)
                dve.tensor_copy(from_slot[:, :, :], spot2[:, :, :]).then_inc(from_done, 1)
                dve.drain()
                dve.tensor_tensor(to_slot[:, :, :], spot2[:, :, :], flag[:, :, :], ALU.add).then_inc(to_done, 1)
            else:
                dve.tensor_copy(to_slot[:, :, :], spot[:, :, :]).then_inc(to_done, 1)
                dve.tensor_copy(from_slot[:, :, :], spot[:, :, :]).then_inc(from_done, 1)

            def shared_mul(q, f):
                n, m = q * FS + f, chunk_rows(f)
                dve.wait_ge(s_silu, n + 1)
                if n - q % 2 >= 2 * FS and f == 0:
                    dve.wait_ge(sd_put, (q - 1) * 4)
                dve.tensor_tensor(s_hT[q % 2][0:m, f, :], ps_u[n % 2][0:m, :], s_act[n % 2][0:m, :], ALU.mult)\
                   .then_inc(s_mul, 1)

            def shared_add(q):
                for i in range(4):
                    t = 4 * q + i
                    dve.wait_ge(sd_put, t + 1)
                    if rms:
                        dve.scalar_tensor_tensor(out=core.xt(t), in0=ps_l[:, 0:D], scalar=gate_f[:, t:t + 1],
                                                 in1=core.xt(t), op0=ALU.mult, op1=ALU.add).then_inc(sd_done, 1)
                    else:
                        dve.tensor_tensor(core.xt(t), core.xt(t), ps_l[:, 0:D], ALU.add).then_inc(sd_done, 1)

            if shared:
                for q in range(4):
                    for f in range(FS):
                        shared_mul(q, f)
                        if f == min(1, FS - 1) and q:
                            shared_add(q - 1)
                shared_add(3)

            def mul(j, u):
                dve.wait_ge(e_silu, j + 1)
                if after(j, 2):
                    dve.wait_ge(h_turned, j - 1)
                dve.tensor_tensor(h_sb[u][:, :], ps_g[u][:, FE:2 * FE], act_sb[u][:, :], ALU.mult).then_inc(e_mul, 1)

            def copy_y(j, r):
                u = r % 2
                dve.wait_ge(yd_put, j + 1)
                if after(j, 2):
                    dve.wait_ge(y_out[u], (j - u) * 8)
                dve.tensor_copy(y_sb[u][:, :], ps_l[:, 0:D]).then_inc(y_copied, 1)

            def expert_tile(j, r):
                if ahead(j, 1, NT):
                    mul(j + 1, (r + 1) % 2)
                copy_y(j, r)

            mul(0, 0)
            over_ring(dve, expert_tile, NT, RING)

            for t in range(B):
                dve.wait_ge(got_in[t % 2], got_before + (t // 2 + 1) * 16 * K)
                for k in range(K):
                    last = dve.scalar_tensor_tensor(out=core.xt(t), in0=got[t % 2][:, k, :], scalar=weight[:, t, k:k + 1],
                                                    in1=core.xt(t), op0=ALU.mult, op1=ALU.add)
                    if k < K - 1:
                        dve.drain()
                last.then_inc(added, 1)
                dve.drain()
                row_stats(dve, core, t, six)

        @block.scalar
        def _(act):
            if rms:
                def squares_of(t, u):
                    act.wait_ge(ln_done, t + 1)
                    act.activation(square[:, :], rows[:, bass.ds(t, 1), :].rearrange("p a d -> p (a d)"), ACT.Square,
                                   accum_out=squares[:, bass.ds(t, 1)]).then_inc(sq_done, 1)
                    act.drain()

                over_tiles(act, squares_of)

            def tile(t, u):
                act.wait_ge(row_done, t + 1)
                act.activation(rows[:, bass.ds(t, 1), :].rearrange("p a d -> p (a d)"), row1[u][:, :], ACT.Copy)\
                    .then_inc(row_kept, 1)
                act.wait_ge(xT_put, t + 1)
                if after(t, 2):
                    act.wait_ge(l_put, t - 1)
                if shared:
                    act.activation(xT[:, :, bass.ds(t * P, P)], ps_x[u][:, :].rearrange("p (c t) -> p c t", c=KC), ACT.Copy)
                act.activation(xT1[u][:, :, :], ps_x[u][:, :].rearrange("p (c t) -> p c t", c=KC), ACT.Copy)\
                    .then_inc(xT_done, 1)

            over_tiles(act, tile)
            act.wait_ge(max_done, 1)
            if top_softmax:
                act.activation(weight[:, :, :], weight[:, :, :], ACT.Exp).then_inc(e_done, 1)
            else:
                act.activation(prob[:, :, :], prob[:, :, :], ACT.Exp).then_inc(e_done, 1)
            if rms:
                act.activation(gate_f[:, :], logit[:, :, E], ACT.Exp, scale=-1.0).then_inc(gate_e, 1)
            if shared:
                for q in range(4):
                    for f in range(FS):
                        n, m = q * FS + f, chunk_rows(f)
                        act.wait_ge(sg_put, n + 1)
                        if n >= 2:
                            act.wait_ge(s_mul, n - 1)
                        act.activation(s_act[n % 2][0:m, :], ps_g[n % 2][0:m, :], ACT.Silu).then_inc(s_silu, 1)

            def copy_in(j, u):
                act.wait_ge(in_turned, j + 1)
                if after(j, 2):
                    act.wait_ge(gu_put, j - 1)
                act.activation(xinT[u][:, :, :].rearrange("p c t -> p (c t)"), ps_x[u][:, :], ACT.Copy)\
                    .then_inc(in_copied, 1)

            def silu(j, u):
                act.wait_ge(gu_put, j + 1)
                if after(j, 2):
                    act.wait_ge(e_mul, j - 1)
                act.activation(act_sb[u][:, :], ps_g[u][:, 0:FE], ACT.Silu).then_inc(e_silu, 1)

            def copy_h(j, u):
                act.wait_ge(h_turned, j + 1)
                if after(j, 2):
                    act.wait_ge(yd_put, j - 1)
                act.activation(hT_sb[u][:, :, :].rearrange("p c t -> p (c t)"), ps_u[u][0:FCH, 0:NJ * P], ACT.Copy)\
                    .then_inc(h_copied, 1)

            def expert_tile(j, r):
                if ahead(j, 1, NT):
                    silu(j + 1, (r + 1) % 2)
                copy_h(j, r % 2)
                if ahead(j, 2, NT):
                    copy_in(j + 2, r % 2)

            copy_in(0, 0)
            copy_in(1, 1)
            silu(0, 0)
            over_ring(act, expert_tile, NT, RING)

        @block.tensor
        def _(pe):
            def turn_row(t, u):
                pe.wait_ge(row_done, t + 1)
                if after(t, 2):
                    pe.wait_ge(xT_done, t - 1)
                for c in range(KC):
                    last = pe.transpose(ps_x[u][:, c * P:c * P + P], row1[u][:, c * P:c * P + P], core.ident[:, :])
                last.then_inc(xT_put, 1)

            def route(t, u):
                pe.wait_ge(xT_done, t + 1)
                if after(t, 1):
                    pe.wait_ge(l_done, t)
                for c in range(KC):
                    last = pe.matmul(ps_l[:, 0:NL], xT1[u][:, c, :], router[:, c, :], start=(c == 0), stop=(c == KC - 1))
                last.then_inc(l_put, 1)

            def tile(t, u):
                if ahead(t, 1):
                    turn_row(t + 1, 1 - u)
                route(t, u)

            pe.wait_ge(w_in, 16 * n_loads)
            turn_row(0, 0)
            over_tiles(pe, tile)

            pe.wait_ge(const_done, 4 if capacity else 6)
            pe.wait_ge(chosen_done, 1)
            flat = chosen[:, :, :].rearrange("p t e -> p (t e)")
            for d in range(B):
                last = pe.matmul(ps_p[:, 0:B * E], onesb[:, :] if d else before[:, :], flat[:, (B - d) * E:(2 * B - d) * E],
                                 start=(d == 0), stop=(d == B - 1))
            last.then_inc(place_put, 1)
            if not capacity:
                pe.wait_ge(l_done, B)
                for t in range(B):
                    last = pe.matmul(ps_l[:, 0:E], onesb[:, :], chosen[:, B + t, :], start=(t == 0), stop=(t == B - 1))
                last.then_inc(counted, 1)

            def shared_gu(q, f):
                n, m = q * FS + f, chunk_rows(f)
                if n >= 2:
                    pe.wait_ge(s_mul, n - 1)
                for ps, w in ((ps_g, sw_g), (ps_u, sw_u)):
                    for c in range(KC):
                        last = pe.matmul(ps[n % 2][0:m, :], w[:, c, f * P:f * P + m], xT[:, c, q * W4:q * W4 + W4],
                                         start=(c == 0), stop=(c == KC - 1))
                last.then_inc(sg_put, 1)

            def shared_down(q):
                pe.wait_ge(s_mul, (q + 1) * FS)
                for i in range(4):
                    t = 4 * q + i
                    if t:
                        pe.wait_ge(sd_done, t)
                    elif not capacity:
                        pe.wait_ge(owner_done, 1)
                    for f in range(FS):
                        m = chunk_rows(f)
                        last = pe.matmul(ps_l[:, 0:D], s_hT[q % 2][0:m, f, i * P:i * P + P], sw_d[0:m, f, :],
                                         start=(f == 0), stop=(f == FS - 1))
                    last.then_inc(sd_put, 1)

            if shared:
                pe.wait_ge(sw_in, 16 * (3 + (shared % P > 0)))
                for q in range(4):
                    for f in range(FS):
                        shared_gu(q, f)
                        if f == min(1, FS - 1) and q:
                            shared_down(q - 1)
                shared_down(3)
                pe.wait_ge(sd_done, B)
                pe.wait_ge(s_mul, 4 * FS)

            def turn_in(j, r):
                pe.wait_ge(xin_in[r], (j - r) * (16 // RING) + 16)
                if after(j, 2):
                    pe.wait_ge(in_copied, j - 1)
                for c in range(KC):
                    last = pe.transpose(ps_x[r % 2][:, c * P:c * P + P], xin[r][:, c * P:c * P + P], core.ident[:, :])
                last.then_inc(in_turned, 1)

            def gate_up(j, r):
                if not capacity:
                    e = pe.value_load(owner_i[0:1, bass.ds(j, 1)], min_val=0, max_val=E - 1)
                if capacity:
                    pe.wait_ge(ring_in[r], (j - r) * (32 // RING) + 32)
                pe.wait_ge(in_copied, j + 1)
                if after(j, 2):
                    pe.wait_ge(e_mul, j - 1)
                for c in range(KC):
                    w = w_gu[r][:, c, :] if capacity else w_gu_all[:, bass.ds(e * (KC * 2 * FE) + c * 2 * FE, 2 * FE)]
                    last = pe.matmul(ps_g[r % 2][:, 0:2 * FE], xinT[r % 2][:, c, :], w, start=(c == 0), stop=(c == KC - 1))
                last.then_inc(gu_put, 1)

            def turn_h(j, u):
                pe.wait_ge(e_mul, j + 1)
                if after(j, 2):
                    pe.wait_ge(h_copied, j - 1)
                for c in range(NJ):
                    last = pe.transpose(ps_u[u][0:FCH, c * P:c * P + P], h_sb[u][:, c * FCH:(c + 1) * FCH], core.ident[:, :])
                last.then_inc(h_turned, 1)

            def down(j, r):
                if not capacity:
                    e = pe.value_load(owner_i[0:1, bass.ds(j, 1)], min_val=0, max_val=E - 1)
                pe.wait_ge(h_copied, j + 1)
                if after(j, 1):
                    pe.wait_ge(y_copied, j)
                for c in range(NJ):
                    w = w_d[r][:, c, :] if capacity else w_d_all[:, bass.ds(e * (NJ * D) + c * D, D)]
                    last = pe.matmul(ps_l[:, 0:D], hT_sb[r % 2][:, c, :], w, start=(c == 0), stop=(c == NJ - 1))
                last.then_inc(yd_put, 1)

            def expert_tile(j, r):
                if ahead(j, 1, NT):
                    gate_up(j + 1, (r + 1) % RING)
                turn_h(j, r % 2)
                if ahead(j, 2, NT):
                    turn_in(j + 2, (r + 2) % RING)
                down(j, r)

            if not capacity:
                pe.wait_ge(owner_done, 1)
                pe.wait_ge(ew_in, 32)
            turn_in(0, 0)
            turn_in(1, 1)
            gate_up(0, 0)
            over_ring(pe, expert_tile, NT, RING)


STAGES = {
    "L1F": lambda core: moe_ffn(core, "l1f", 32, 4, 176, capacity=128, shared=704, rms=True),
    "L2F": lambda core: moe_ffn(core, "l2f", 16, 2, 128, shared=128, biased=True, renorm=True),
    "L3F": lambda core: moe_ffn(core, "l3f", 8, 2, 256, top_softmax=True),
    "L1A": lambda core: gated_long_conv(core, "l1a"),
    "L3A": lambda core: channel_attention(core, "l3a"),
    "L0F": lambda core: hadamard_ffn(core, "l0f"),
    "L0A": lambda core: gqa_attention(core, "l0a", dict(
        wq="l0a_wq", wk="l0a_wk", wv="l0a_wv", wo="l0a_wo", bq="l0a_bq", bk="l0a_bk", bv="l0a_bv", bo="l0a_bo"), True),
    "L2A": lambda core: gqa_attention(core, "l2a", dict(
        wq="l2a_wq", wk="l2a_wk", wv="l2a_wv", wo="l2a_wo", bo="l2a_bo"), False),
}


def build(nc, dram, out, stages):
    with ExitStack() as ctx:
        core = Core(nc, ctx, dram)
        load_inputs(core)
        for s in stages:
            STAGES[s](core)
        store_output(core, out)


def lay_out(np, a):
    def chunks(w, p=P):
        w = np.asarray(w)
        return w.reshape(w.shape[0] // p, p, -1).transpose(1, 0, 2)

    def per_head(w):
        w = np.asarray(w)
        return np.repeat(w.reshape(G, 1, HD, -1), R, axis=1).reshape(H * HD, -1)

    ctx = np.asarray(a["ctx_2048"])
    o = {
        "x": a["x"],
        "ctx": ctx,
        "ctxT": ctx.reshape(B, P, KC, P).transpose(0, 3, 2, 1),
        "pair_mask": np.asarray(a["mask_SxS2_bc0"]),
        "pad_mask": np.asarray(a["mask_BxS2_bk0"]).reshape(T),
    }
    for s, n in (("l0a", "L0_xattn_"), ("l2a", "L2_xattn_")):
        o[f"{s}_wq"] = chunks(np.asarray(a[n + "Wq"]).T)
        o[f"{s}_wk"] = chunks(per_head(a[n + "Wk"]).T)
        o[f"{s}_wv"] = chunks(np.asarray(a[n + "Wv"]).T)
    o["l0f_wg"] = chunks(np.asarray(a["L0_ffn_w_gate"]).T).reshape(P, -1)
    o["l0f_wu"] = chunks(np.asarray(a["L0_ffn_w_up"]).T).reshape(P, -1)
    o["l0f_wd"] = chunks(np.asarray(a["L0_ffn_w_down"]).T).reshape(P, -1)
    had = np.ones((1, 1), np.float32)
    while had.shape[0] < P:
        had = np.block([[had, had], [had, -had]])
    o["had"] = had
    o["skip"] = a["fside_S2_0"]
    k = np.concatenate([np.zeros((16, P), np.float32), np.asarray(a["L1_xattn_k"])], axis=1)
    o["l1a_taps"] = np.stack([k[:, P - m:P - m + D] for m in range(P)])
    def experts(g, u, d, fch):
        g, u, d = (np.asarray(w) for w in (g, u, d))
        gu = np.concatenate([g, u], axis=2)
        return (gu.reshape(len(gu), KC, P, -1).transpose(0, 2, 1, 3),
                d.reshape(len(d), -1, fch, D).transpose(0, 2, 1, 3))

    o["l1f_w_gu"], o["l1f_w_d"] = experts(a["L1_ffn_w_gate"], a["L1_ffn_w_up"], a["L1_ffn_w_down"], 88)
    o["l2f_w_gu"], o["l2f_w_d"] = experts(a["L2_ffn_Wg"], a["L2_ffn_Wu"], a["L2_ffn_Wd"], 128)
    o["l3f_w_gu"], o["l3f_w_d"] = experts(a["L3_ffn_wi_0"], a["L3_ffn_wi_1"], a["L3_ffn_wo"], 128)
    o["l1f_router"] = chunks(np.concatenate([np.asarray(a["L1_ffn_w_router"]), np.asarray(a["L1_ffn_w_shared_gate"])], axis=1))
    o["l2f_router"] = chunks(np.asarray(a["L2_ffn_Wr"]).T)
    o["l3f_router"] = chunks(a["L3_ffn_gate_kernel"])
    o["l1f_norm_w"] = a["L1_ffn_w_norm"]
    o["l2f_bias"] = a["L2_ffn_bias"]
    for s, n in (("l1f", ("L1_ffn_sw_gate", "L1_ffn_sw_up", "L1_ffn_sw_down")),
                 ("l2f", ("L2_ffn_sWg", "L2_ffn_sWu", "L2_ffn_sWd"))):
        o[f"{s}_sw_g"], o[f"{s}_sw_u"], o[f"{s}_sw_d"] = chunks(a[n[0]]), chunks(a[n[1]]), a[n[2]]
    o["l0a_wo"] = chunks(np.asarray(a["L0_xattn_Wo"]).T)
    o["l2a_wo"] = chunks(np.asarray(a["L2_xattn_Wfc"]).T)
    o["l0a_bq"] = np.asarray(a["L0_xattn_bq"]).reshape(KC, P).T
    o["l0a_bk"] = per_head(a["L0_xattn_bk"]).reshape(KC, P).T
    o["l0a_bv"] = a["L0_xattn_bv"]
    o["l0a_bo"] = a["L0_xattn_bo"]
    o["l2a_bo"] = a["L2_xattn_bfc"]
    return {k: np.ascontiguousarray(v) for k, v in o.items()}


ALL = ("L0A", "L0F", "L1A", "L1F", "L2A", "L2F", "L3A", "L3F")


def kernel(**inputs):
    import numpy as np
    import concourse.bacc as bacc
    from concourse.bass_utils import run_bass_kernel_spmd

    arrays = {f"in_{k}": v for k, v in lay_out(np, inputs).items()}
    nc = bacc.Bacc("TRN2", target_bir_lowering=False, num_devices=1)
    dram = {k[3:]: nc.dram_tensor(k, v.shape, mybir.dt.from_np(v.dtype), kind="ExternalInput").ap()
            for k, v in arrays.items()}
    out = nc.dram_tensor("out_x", (B, P, D), F32, kind="ExternalOutput").ap()
    build(nc, dram, out, ALL)
    return run_bass_kernel_spmd(nc, [arrays], core_ids=[0]).results[0]["out_x"]
```

```python
from contextlib import ExitStack, contextmanager

import numpy as np

import concourse.bass as bass
from concourse import mybir

P = 128
B = 16
T = B * P
D = 256
KC = D // P
H, HD = 32, 8
G = 8
R = H // G
W4 = 4 * P
LN_EPS = 1e-5
NEG = -1e30

F32 = mybir.dt.float32
BF16 = mybir.dt.bfloat16
U8 = mybir.dt.uint8
U32 = mybir.dt.uint32
I32 = mybir.dt.int32
ALU = mybir.AluOpType
ACT = mybir.ActivationFunctionType
AX = mybir.AxisListType


def over_batches(eng, body):
    body(0, 0, True, False)
    with eng.Fori(0, (B - 2) // 2) as i:
        body(i * 2 + 1, 1, False, False)
        body(i * 2 + 2, 0, False, False)
    body(B - 1, 1, False, True)


def over_tiles(eng, body, n=B):
    body(0, 0)
    body(1, 1)
    with eng.Fori(1, n // 2 - 1) as i:
        body(i * 2, 0)
        body(i * 2 + 1, 1)
    body(n - 2, 0)
    body(n - 1, 1)


def over_long_pipe(eng, body, n=B):
    body(0, 0)
    body(1, 1)
    with eng.Fori(1, n // 2 - 2) as i:
        body(i * 2, 0)
        body(i * 2 + 1, 1)
    for t in range(n - 4, n):
        body(t, t % 2)


def after(t, n):
    return not isinstance(t, int) or t >= n


def ahead(t, n, total=B):
    return not isinstance(t, int) or t + n < total


EPS_Q = float(np.float32(1e-5))
FF = 1024
NF = FF // P
MAX_SLOTS = 48 * P


class Core:

    def __init__(self, nc, ctx, dram):
        self.nc, self.ctx, self.dram = nc, ctx, dram
        self.x = self.sb("x_rows", [P, B * D])
        self.stats = self.sb("ln_mean_var", [P, B, 2])
        self.rstd = self.sb("ln_rstd", [P, B])
        self.slots = nc.dram_tensor("expert_slots", (MAX_SLOTS, D), F32, kind="Internal").ap()
        self.results = nc.dram_tensor("expert_results", (MAX_SLOTS, D), F32, kind="Internal").ap()
        self.ffn_raw = [self.sb(f"ffn_raw{n}", [P, KC * FF]) for n in range(3)]
        self.had = self.sb("had_matrix", [P, P])
        self.ffn_in = [ctx.enter_context(nc.semaphore(f"ffn_in{n}")) for n in range(3)]
        self.had_in = ctx.enter_context(nc.semaphore("had_in"))
        self.scattered = ctx.enter_context(nc.semaphore("scattered"))
        self.gathered = [ctx.enter_context(nc.semaphore(f"gathered{u}")) for u in range(2)]
        self.n_scattered, self.n_gathered = 0, 0
        self.minus_half = self.sb("minus_half", [P, B])
        self.ident = self.sb("ident", [P, P])
        self.identb = self.sb("identb", [P, P], BF16)
        self.head_of_row = self.sb("head_of_row", [P, R])
        self.chan_head_of_row = self.sb("chan_head_of_row", [P, P // 16])
        self.group_of_row = self.sb("group_of_row", [P, 4])

    def sb(self, name, shape, dt=F32, ctx=None):
        return (ctx or self.ctx).enter_context(self.nc.sbuf_tensor(name, shape, dt))

    def ps(self, name, shape, dt=F32, ctx=None):
        return (ctx or self.ctx).enter_context(self.nc.psum_tensor(name, shape, dt))

    def sem(self, name, ctx):
        s = ctx.enter_context(self.nc.semaphore(name))
        self.stage_sems.append(s.num)
        return s

    @contextmanager
    def stage(self):
        self.stage_sems = []
        with ExitStack() as st:
            yield st
        nums = sorted(self.stage_sems)
        first = nums[0]
        for n, following in zip(nums, nums[1:] + [-1]):
            if following != n + 1:
                self.nc.gpsimd.sem_clear(range(first, n + 1))
                first = following

    def xt(self, b):
        return self.x[:, bass.ds(b * D, D)]


def row_stats(dve, core, b, six):
    dve.bn_stats(six[:, :], core.xt(b))
    dve.drain()
    dve.bn_aggr(six[:, 0:2], six[:, :])
    dve.drain()
    dve.tensor_copy(core.stats[:, bass.ds(b, 1), :].rearrange("p a s -> p (a s)"), six[:, 0:2])


def all_rstd(pool, core, done):
    pool.tensor_scalar(core.rstd[:, :], core.stats[:, :, 1], LN_EPS, 1.0, ALU.add, ALU.mult)
    pool.drain()
    pool.tensor_tensor(core.rstd[:, :], core.rstd[:, :], core.minus_half[:, :], ALU.pow).then_inc(done, 1)


def normalise(dve, core, out, b):
    return dve.tensor_scalar(out, core.xt(b), core.stats[:, bass.ds(b, 1), 0], core.rstd[:, bass.ds(b, 1)],
                             ALU.subtract, ALU.mult)


def load_inputs(core):
    nc, dram = core.nc, core.dram
    with core.stage() as st:
        x_in, const, zeroed, zero_out = (core.sem(f"load_{n}", st) for n in ("x_in", "const", "zeroed", "zero_out"))
        zeros = core.sb("load_zeros", [P, D], F32, st)
        six = core.sb("load_six", [P, 6], F32, st)
        band = core.sb("load_band", [P, 4, R], F32, st)
        block = st.enter_context(nc.Block())

        @block.sync
        def _(sp):
            sp.dma_start(core.x[:, :].rearrange("p (b d) -> p b d", b=B),
                         dram["x"].rearrange("b p d -> p b d")).then_inc(x_in, 16)
            for n, key in enumerate(("l0f_wg", "l0f_wu", "l0f_wd")):
                sp.dma_start(core.ffn_raw[n][:, :], dram[key]).then_inc(core.ffn_in[n], 16)
            sp.dma_start(core.had[:, :], dram["had"]).then_inc(core.had_in, 16)
            sp.wait_ge(zeroed, 1)
            sp.dma_start(core.slots.rearrange("(n p) d -> p n d", p=P),
                         zeros[:, :].unsqueeze(1).broadcast_to([P, MAX_SLOTS // P, D])).then_inc(zero_out, 16)
            sp.wait_ge(zero_out, 16)

        @block.gpsimd
        def _(pool):
            pool.memset(zeros[:, :], 0.0).then_inc(zeroed, 1)
            pool.memset(core.minus_half[:, :], -0.5)
            pool.memset(core.ident[:, :], 0.0).then_inc(const, 1)
            pool.memset(core.identb[:, :], 0.0).then_inc(const, 1)
            pool.wait_ge(const, 2)
            for m in (core.ident, core.identb):
                pool.affine_select(out=m[:, :], in_=m[:, :], compare_op=ALU.not_equal, fill=1.0, base=0,
                                   pattern=[[-1, P]], channel_multiplier=1).then_inc(const, 1)
            pool.memset(band[:, :, :], 1.0).then_inc(const, 1)
            pool.wait_ge(const, 5)
            pool.affine_select(out=band[:, :, :].rearrange("p g r -> p (g r)"), in_=band[:, :, :].rearrange("p g r -> p (g r)"), compare_op=ALU.is_ge, fill=0.0, base=0,
                               pattern=[[-HD, P // HD]], channel_multiplier=1).then_inc(const, 1)
            pool.wait_ge(const, 6)
            pool.affine_select(out=band[:, :, :].rearrange("p g r -> p (g r)"), in_=band[:, :, :].rearrange("p g r -> p (g r)"), compare_op=ALU.is_ge, fill=0.0, base=HD - 1,
                               pattern=[[HD, P // HD]], channel_multiplier=-1).then_inc(const, 1)

        @block.vector
        def _(dve):
            dve.wait_ge(const, 7)
            dve.tensor_reduce(core.head_of_row[:, :], band[:, :, :].rearrange("p g r -> p r g"), AX.X, ALU.add)
            dve.tensor_reduce(core.group_of_row[:, :], band[:, :, :], AX.X, ALU.add)
            dve.tensor_reduce(core.chan_head_of_row[:, :], band[:, :, :].rearrange("p g (h two) -> p (g h) two", two=2),
                              AX.X, ALU.add)
            dve.drain()
            for rows, width in ((core.group_of_row, HD), (core.chan_head_of_row, 16)):
                dve.tensor_scalar(rows[:, :], rows[:, :], width ** -0.5, None, ALU.mult)
            dve.wait_ge(x_in, 16)
            for b in range(B):
                row_stats(dve, core, b, six)
                dve.drain()


def store_output(core, out):
    nc = core.nc
    with core.stage() as st:
        stored = core.sem("x_stored", st)
        block = st.enter_context(nc.Block())

        @block.sync
        def _(sp):
            sp.dma_start(out.rearrange("b p d -> p b d"),
                         core.x[:, :].rearrange("p (b d) -> p b d", b=B)).then_inc(stored, 16)
            sp.wait_ge(stored, 16)


def gqa_attention(core, name, w, masked):
    nc, dram = core.nc, core.dram
    with core.stage() as st:
        def sb(n, shape, dt=F32):
            return core.sb(f"{name}_{n}", shape, dt, st)

        def sem(n):
            return core.sem(f"{name}_{n}", st)

        wq, wk, wo = (sb(n, [P, KC, D]) for n in ("wq", "wk", "wo"))
        wv = sb("wv", [P, KC, G * HD])
        bias_o = sb("bias_o", [P, D])
        if masked:
            bias_q, bias_k = sb("bias_q", [P, KC]), sb("bias_k", [P, KC])
            bias_v = sb("bias_v", [P, G * HD])
            pad_u8, pair_u8 = sb("pad_u8", [P, T], U8), sb("pair_u8", [P, P], U8)
            pad_neg, pair_neg = sb("pad_neg", [P, T], BF16), sb("pair_neg", [P, P], BF16)
            mask = [sb(f"mask{u}", [P, P], BF16) for u in range(2)]
        ctxT = [sb(f"ctxT{u}", [P, KC, P]) for u in range(2)]
        xn = sb("xn", [P, D])
        xnT = sb("xnT", [P, KC, P])
        qT, kT = sb("qT", [P, KC, P]), sb("kT", [P, KC, P])
        q_group = [sb(f"q_group{u}", [P, G, P]) for u in range(2)]
        k_head = [sb(f"k_head{u}", [P, KC, R, P]) for u in range(2)]
        v_aug = [sb(f"v_aug{u}", [P, G, 32]) for u in range(2)]
        neg_max = sb("neg_max", [P, 4, R])
        prob = [sb(f"prob{s}", [P, W4]) for s in range(4)]
        probT = [sb(f"probT{s}", [P, W4]) for s in range(2)]
        o_sb = [sb(f"o_sb{c}", [P, W4]) for c in range(2)]
        recip = sb("recip", [P, R, 4])
        attn = sb("attn", [P, D])
        attnT = sb("attnT", [P, KC, P])
        y_sb = sb("y_sb", [P, D])
        six = sb("six", [P, 6])
        ps_s = [core.ps(f"{name}_ps_s{s}", [P, W4], F32, st) for s in range(2)]
        ps_t = [core.ps(f"{name}_ps_t{s}", [P, W4], F32, st) for s in range(2)]
        ps_o = [core.ps(f"{name}_ps_o{c}", [P, W4], F32, st) for c in range(2)]
        ps_in = core.ps(f"{name}_ps_in", [P, W4], F32, st)
        ps_out = core.ps(f"{name}_ps_out", [P, W4], F32, st)

        (w_in, const_done, mask_done, rstd_done, xn_done, xnT_put, xnT_done, qk_put, qk_done, q_spread,
         k_spread, v_put, v_done, s_put, max_done, exp_done, t_put, t_done, pv_put, o_done, r_put, attn_done,
         a_put, a_done, y_put, x_done) = (sem(n) for n in (
             "w_in", "const_done", "mask_done", "rstd_done", "xn_done", "xnT_put", "xnT_done", "qk_put",
             "qk_done", "q_spread", "k_spread", "v_put", "v_done", "s_put", "max_done", "exp_done", "t_put", "t_done",
             "pv_put", "o_done", "r_put", "attn_done", "a_put", "a_done", "y_put", "x_done"))
        ctx_in = [sem(f"ctx_in{u}") for u in range(2)]
        n_loads = 10 if masked else 5
        block = st.enter_context(nc.Block())

        @block.sync
        def _(sp):
            def load_ctx(b, u):
                sp.dma_start(ctxT[u][:, :, :], dram["ctxT"][bass.ds(b, 1)].rearrange("a p c t -> p (a c) t"))\
                  .then_inc(ctx_in[u], 16)

            load_ctx(0, 0)
            for buf, key in ((wq, "wq"), (wk, "wk"), (wv, "wv"), (wo, "wo")):
                sp.dma_start(buf[:, :, :], dram[w[key]]).then_inc(w_in, 16)
            sp.dma_start(bias_o[:, :], dram[w["bo"]].partition_broadcast(P)).then_inc(w_in, 16)
            if masked:
                sp.dma_start(bias_q[:, :], dram[w["bq"]]).then_inc(w_in, 16)
                sp.dma_start(bias_k[:, :], dram[w["bk"]]).then_inc(w_in, 16)
                sp.dma_start(bias_v[:, :], dram[w["bv"]].partition_broadcast(P)).then_inc(w_in, 16)
                sp.dma_start(pair_u8[:, :], dram["pair_mask"]).then_inc(w_in, 16)
                sp.dma_start(pad_u8[:, :], dram["pad_mask"].partition_broadcast(P)).then_inc(w_in, 16)
            load_ctx(1, 1)
            with sp.Fori(0, (B - 2) // 2) as i:
                for u in range(2):
                    sp.wait_ge(v_put, i * 2 + u + 1)
                    load_ctx(i * 2 + u + 2, u)

        @block.gpsimd
        def _(pool):
            all_rstd(pool, core, rstd_done)
            for u in range(2):
                pool.memset(q_group[u][:, :, :], 0.0).then_inc(const_done, 1)
                pool.memset(v_aug[u][:, :, :], 0.0).then_inc(const_done, 1)
            pool.wait_ge(const_done, 4)
            for u in range(2):
                pool.memset(v_aug[u][:, :, HD], 1.0).then_inc(const_done, 1)
            if masked:
                pool.wait_ge(w_in, 16 * n_loads)
                pool.tensor_scalar(pair_neg[:, :], pair_u8[:, :], NEG, 1.0, ALU.mult, ALU.mult)
                pool.tensor_scalar(pad_neg[:, :], pad_u8[:, :], NEG, 1.0, ALU.mult, ALU.mult)
                pool.drain()

            def spread(b, u):
                if masked:
                    pool.wait_ge(s_put, b * G - G) if not (isinstance(b, int) and b < 2) else None
                    pool.tensor_tensor(mask[u][:, :], pair_neg[:, :], pad_neg[:, bass.ds(b * P, P)], ALU.add)\
                        .then_inc(mask_done, 1)
                elif not (isinstance(b, int) and b < 2):
                    pool.wait_ge(s_put, b * G - G)
                pool.wait_ge(qk_done, b * 4 + 4)
                for c in range(KC):
                    pool.tensor_tensor(k_head[u][:, c, :, :],
                                       kT[:, c:c + 1, :].broadcast_to([P, R, P]),
                                       core.head_of_row[:, :].unsqueeze(2).broadcast_to([P, R, P]), ALU.mult)\
                        .then_inc(k_spread, 1)
                for c in range(KC):
                    pool.tensor_tensor(q_group[u][:, 4 * c:4 * c + 4, :],
                                       qT[:, c:c + 1, :].broadcast_to([P, 4, P]),
                                       core.group_of_row[:, :].unsqueeze(2).broadcast_to([P, 4, P]), ALU.mult)\
                        .then_inc(q_spread, 1)

            spread(0, 0)
            spread(1, 1)
            with pool.Fori(0, (B - 2) // 2) as i:
                for u in range(2):
                    spread(i * 2 + u + 2, u)

        @block.vector
        def _(dve):
            def xn_of(b):
                if not (isinstance(b, int) and b == 0):
                    dve.wait_ge(xnT_put, b)
                normalise(dve, core, xn[:, :], b).then_inc(xn_done, 1)

            def values(b, u):
                dve.wait_ge(v_put, b + 1)
                psv = ps_in[:, 0:G * HD].rearrange("p (g d) -> p g d", g=G)
                if not (isinstance(b, int) and b < 2):
                    dve.wait_ge(pv_put, b * G - G)
                if masked:
                    dve.tensor_tensor(v_aug[u][:, :, 0:HD], psv, bias_v[:, :].rearrange("p (g d) -> p g d", g=G),
                                      ALU.add).then_inc(v_done, 1)
                else:
                    dve.tensor_copy(v_aug[u][:, :, 0:HD], psv).then_inc(v_done, 1)

            def find_max(b, g):
                dve.wait_ge(s_put, b * G + g + 1)
                if after(b, 1) or g >= 4:
                    dve.wait_ge(exp_done, b * G + g - 3)
                dve.tensor_reduce(neg_max[:, g % 4, :], ps_s[g % 2][:, :].rearrange("p (r k) -> p r k", r=R),
                                  AX.X, ALU.max, negate=True).then_inc(max_done, 1)

            def copy_probT(b, g):
                dve.wait_ge(t_put, b * G + g + 1)
                if after(b, 1) or g >= 2:
                    dve.wait_ge(pv_put, b * G + g - 1)
                dve.tensor_copy(probT[g % 2][:, :], ps_t[g % 2][:, :]).then_inc(t_done, 1)

            def weigh(b, c):
                dve.wait_ge(r_put, b * 2 + c + 1)
                o = ps_out[:, :].rearrange("p (r g e) -> p r g e", r=R, g=4)
                dve.reciprocal(recip[:, :, :], o[:, :, :, HD])
                dve.drain()
                if c == 0 and not (isinstance(b, int) and b == 0):
                    dve.wait_ge(a_put, b)
                dve.tensor_tensor(attn[:, c * P:c * P + P].rearrange("p (g r d) -> p r g d", g=4, r=R),
                                  o[:, :, :, 0:HD], recip[:, :, :].unsqueeze(3).broadcast_to([P, R, 4, HD]),
                                  ALU.mult).then_inc(attn_done, 1)

            def add_to_x(b):
                dve.wait_ge(y_put, b + 1)
                dve.tensor_tensor(y_sb[:, :], ps_out[:, D:2 * D], bias_o[:, :], ALU.add)
                dve.drain()
                dve.tensor_tensor(core.xt(b), core.xt(b), y_sb[:, :], ALU.add).then_inc(x_done, 1)
                dve.drain()
                row_stats_late(dve, b)

            def row_stats_late(dve, b):
                row_stats(dve, core, b, six)

            def batch(b, u, first, last):
                for g in range(G):
                    find_max(b, g)
                    if g >= 2:
                        copy_probT(b, g - 2)
                    elif not first:
                        copy_probT(b - 1, G - 2 + g)
                    if g == 0 and not last:
                        xn_of(b + 1)
                    if g == 1 and not first:
                        weigh(b - 1, 0)
                    if g == 4 and not first:
                        weigh(b - 1, 1)
                    if g == 5 and not last:
                        values(b + 1, 1 - u)
                    if g == 7 and not first:
                        add_to_x(b - 1)

            dve.wait_ge(rstd_done, 1)
            xn_of(0)
            dve.wait_ge(w_in, 16 * n_loads)
            dve.wait_ge(const_done, 6)
            values(0, 0)
            over_batches(dve, batch)
            copy_probT(B - 1, G - 2)
            copy_probT(B - 1, G - 1)
            weigh(B - 1, 0)
            weigh(B - 1, 1)
            add_to_x(B - 1)

        @block.scalar
        def _(act):
            def copy_xnT(b):
                act.wait_ge(xnT_put, b + 1)
                if not (isinstance(b, int) and b == 0):
                    act.wait_ge(qk_put, b)
                act.activation(xnT[:, :, :].rearrange("p c t -> p (c t)"), ps_in[:, 0:D], ACT.Copy)\
                    .then_inc(xnT_done, 1)

            def copy_qk(b):
                act.wait_ge(qk_put, b + 1)
                if not (isinstance(b, int) and b == 0):
                    act.wait_ge(q_spread, b * 2)
                    act.wait_ge(k_spread, b * 2)
                for n, (to, bias) in enumerate(((qT, "q"), (kT, "k"))):
                    for c in range(KC):
                        src = ps_in[:, (n * KC + c) * P:(n * KC + c + 1) * P]
                        if masked:
                            act.activation(to[:, c, :], src, ACT.Identity,
                                           bias=(bias_q if bias == "q" else bias_k)[:, c:c + 1]).then_inc(qk_done, 1)
                        else:
                            act.activation(to[:, c, :], src, ACT.Copy).then_inc(qk_done, 1)

            def exps(b, g):
                act.wait_ge(max_done, b * G + g + 1)
                if after(b, 1) or g >= 4:
                    act.wait_ge(t_put, b * G + g - 3)
                for r in range(R):
                    last = act.activation(prob[g % 4][:, r * P:r * P + P], ps_s[g % 2][:, r * P:r * P + P], ACT.Exp,
                                          bias=neg_max[:, g % 4, r:r + 1])
                last.then_inc(exp_done, 1)

            def copy_o(b, c):
                act.wait_ge(pv_put, b * G + 4 * c + 4)
                if not (isinstance(b, int) and b == 0):
                    act.wait_ge(r_put, b * 2 + c - 1)
                act.activation(o_sb[c][:, :], ps_o[c][:, :], ACT.Copy).then_inc(o_done, 1)

            def copy_attnT(b):
                act.wait_ge(a_put, b + 1)
                if not (isinstance(b, int) and b == 0):
                    act.wait_ge(y_put, b)
                act.activation(attnT[:, :, :].rearrange("p c t -> p (c t)"), ps_out[:, 0:D], ACT.Copy)\
                    .then_inc(a_done, 1)

            def batch(b, u, first, last):
                for g in range(G):
                    exps(b, g)
                    if g == 1 and not last:
                        copy_xnT(b + 1)
                    if g == 2 and not first:
                        copy_o(b - 1, 1)
                    if g == 3 and not last:
                        copy_qk(b + 1)
                    if g == 5 and not first:
                        copy_attnT(b - 1)
                    if g == 6:
                        copy_o(b, 0)

            copy_xnT(0)
            act.wait_ge(w_in, 16 * n_loads)
            copy_qk(0)
            over_batches(act, batch)
            copy_o(B - 1, 1)
            copy_attnT(B - 1)

        @block.tensor
        def _(pe):
            def turn_xn(b):
                pe.wait_ge(xn_done, b + 1)
                if not (isinstance(b, int) and b == 0):
                    pe.wait_ge(v_done, b)
                for c in range(KC):
                    last = pe.transpose(ps_in[:, c * P:c * P + P], xn[:, c * P:c * P + P], core.ident[:, :])
                last.then_inc(xnT_put, 1)

            def project_qk(b, u):
                pe.wait_ge(xnT_done, b + 1)
                pe.wait_ge(ctx_in[u], (b - u) * 8 + 16)
                for n, (wt, src) in enumerate(((wq, xnT), (wk, ctxT[u]))):
                    for m in range(KC):
                        for c in range(KC):
                            last = pe.matmul(ps_in[:, (n * KC + m) * P:(n * KC + m + 1) * P],
                                             wt[:, c, m * P:m * P + P], src[:, c, :], start=(c == 0), stop=(c == KC - 1))
                last.then_inc(qk_put, 1)

            def project_v(b, u):
                pe.wait_ge(qk_done, b * 4 + 4)
                for c in range(KC):
                    last = pe.matmul(ps_in[:, 0:G * HD], ctxT[u][:, c, :], wv[:, c, :], start=(c == 0), stop=(c == KC - 1))
                last.then_inc(v_put, 1)

            def scores(b, g, u):
                if g == 0:
                    if masked:
                        pe.wait_ge(mask_done, b + 1)
                if g % 4 == 0:
                    pe.wait_ge(k_spread, b * 2 + g // 4 + 1)
                    pe.wait_ge(q_spread, b * 2 + g // 4 + 1)
                if not (isinstance(b, int) and b == 0 and g < 2):
                    pe.wait_ge(exp_done, b * G + g - 1)
                mm = pe.matmul(ps_s[g % 2][:, :], q_group[u][:, g, :],
                               k_head[u][:, g // 4, :, :].rearrange("p r k -> p (r k)"), start=True, stop=not masked)
                if masked:
                    mm = pe.matmul(ps_s[g % 2][:, :].rearrange("p (r k) -> p r k", r=R), core.identb[:, :],
                                   mask[u][:, :].unsqueeze(1).broadcast_to([P, R, P]), start=False, stop=True)
                mm.then_inc(s_put, 1)

            def turn_prob(b, g):
                pe.wait_ge(exp_done, b * G + g + 1)
                if not (isinstance(b, int) and b == 0 and g < 2):
                    pe.wait_ge(t_done, b * G + g - 1)
                for r in range(R):
                    last = pe.transpose(ps_t[g % 2][:, r * P:r * P + P], prob[g % 4][:, r * P:r * P + P], core.ident[:, :])
                last.then_inc(t_put, 1)

            def weigh_values(b, g, u):
                pe.wait_ge(t_done, b * G + g + 1)
                if g == 0:
                    pe.wait_ge(v_done, b + 1)
                if g % 4 == 0 and not (isinstance(b, int) and b == 0):
                    pe.wait_ge(o_done, b * 2 + g // 4 - 1)
                rows = slice(32 * (g % 4), 32 * (g % 4) + 32)
                pe.matmul(ps_o[g // 4][rows, :], v_aug[u][:, g, :], probT[g % 2][:, :], start=True, stop=True)\
                  .then_inc(pv_put, 1)

            def turn_o(b, c):
                pe.wait_ge(o_done, b * 2 + c + 1)
                if c == 1:
                    pe.wait_ge(attn_done, b * 2 + 1)
                elif not (isinstance(b, int) and b == 0):
                    pe.wait_ge(x_done, b)
                for r in range(R):
                    last = pe.transpose(ps_out[:, r * P:r * P + P], o_sb[c][:, r * P:r * P + P], core.ident[:, :])
                last.then_inc(r_put, 1)

            def turn_attn(b):
                pe.wait_ge(attn_done, b * 2 + 2)
                for c in range(KC):
                    last = pe.transpose(ps_out[:, c * P:c * P + P], attn[:, c * P:c * P + P], core.ident[:, :])
                last.then_inc(a_put, 1)

            def project_out(b):
                pe.wait_ge(a_done, b + 1)
                for c in range(KC):
                    last = pe.matmul(ps_out[:, D:2 * D], attnT[:, c, :], wo[:, c, :], start=(c == 0), stop=(c == KC - 1))
                last.then_inc(y_put, 1)

            def batch(b, u, first, last):
                for g in range(G):
                    scores(b, g, u)
                    if g >= 2:
                        turn_prob(b, g - 2)
                    elif not first:
                        turn_prob(b - 1, G - 2 + g)
                    if g >= 3:
                        weigh_values(b, g - 3, u)
                    elif not first:
                        weigh_values(b - 1, G - 3 + g, 1 - u)
                    if g == 0 and not first:
                        turn_o(b - 1, 0)
                    if g == 1 and not last:
                        turn_xn(b + 1)
                    if g == 3 and not first:
                        turn_o(b - 1, 1)
                    if g == 3 and not last:
                        project_qk(b + 1, 1 - u)
                    if g == 4 and not last:
                        project_v(b + 1, 1 - u)
                    if g == 5 and not first:
                        turn_attn(b - 1)
                    if g == 6 and not first:
                        project_out(b - 1)

            turn_xn(0)
            pe.wait_ge(w_in, 16 * n_loads)
            project_qk(0, 0)
            project_v(0, 0)
            over_batches(pe, batch)
            turn_prob(B - 1, G - 2)
            turn_prob(B - 1, G - 1)
            for g in range(G - 3, G):
                weigh_values(B - 1, g, 1)
            turn_o(B - 1, 0)
            turn_o(B - 1, 1)
            turn_attn(B - 1)
            project_out(B - 1)


def channel_attention(core, name):
    nc, dram = core.nc, core.dram
    CH, CD = 8, 16
    with core.stage() as st:
        def sb(n, shape, dt=F32):
            return core.sb(f"{name}_{n}", shape, dt, st)

        def sem(n):
            return core.sem(f"{name}_{n}", st)

        ctxT = [sb(f"ctxT{u}", [P, KC, P]) for u in range(2)]
        ctx = [sb(f"ctx{u}", [P, D]) for u in range(2)]
        xn = [sb(f"xn{u}", [P, D]) for u in range(2)]
        q_head = [sb(f"q_head{u}", [P, CH, D]) for u in range(2)]
        v_aug = [sb(f"v_aug{u}", [P, KC, CH, 32]) for u in range(2)]
        neg_max = sb("neg_max", [P, 4, 2])
        prob = [sb(f"prob{s}", [P, W4]) for s in range(4)]
        probT = [sb(f"probT{s}", [P, W4]) for s in range(2)]
        o_sb = [sb(f"o_sb{c}", [P, D]) for c in range(2)]
        recip = sb("recip", [P, 2, 4])
        attn = sb("attn", [P, 2, P])
        six = sb("six", [P, 6])
        ps_s = [core.ps(f"{name}_ps_s{s}", [P, W4], F32, st) for s in range(2)]
        ps_t = [core.ps(f"{name}_ps_t{s}", [P, W4], F32, st) for s in range(2)]
        ps_o = [core.ps(f"{name}_ps_o{c}", [P, D], F32, st) for c in range(2)]
        ps_out = core.ps(f"{name}_ps_out", [P, W4], F32, st)
        (const_done, rstd_done, xn_done, q_spread, v_done, s_put, max_done, exp_done, t_put, t_done, pv_put, o_done,
         r_put, attn_done, a_put, x_done) = (sem(n) for n in (
             "const_done", "rstd_done", "xn_done", "q_spread", "v_done", "s_put", "max_done", "exp_done", "t_put",
             "t_done", "pv_put", "o_done", "r_put", "attn_done", "a_put", "x_done"))
        ctx_in = [sem(f"ctx_in{u}") for u in range(2)]
        block = st.enter_context(nc.Block())

        def ctx_loaded(eng, b, u):
            eng.wait_ge(ctx_in[u], (b - u) * 16 + 32)

        @block.sync
        def _(sp):
            def load_ctx(b, u):
                sp.dma_start(ctxT[u][:, :, :], dram["ctxT"][bass.ds(b, 1)].rearrange("a p c t -> p (a c) t"))\
                  .then_inc(ctx_in[u], 16)
                sp.dma_start(ctx[u][:, :], dram["ctx"][bass.ds(b, 1)].rearrange("a p d -> p (a d)"))\
                  .then_inc(ctx_in[u], 16)

            load_ctx(0, 0)
            load_ctx(1, 1)
            with sp.Fori(0, (B - 2) // 2) as i:
                for u in range(2):
                    sp.wait_ge(s_put, i * (2 * CH) + (u + 1) * CH)
                    sp.wait_ge(v_done, i * 2 + u + 1)
                    load_ctx(i * 2 + u + 2, u)

        @block.gpsimd
        def _(pool):
            all_rstd(pool, core, rstd_done)
            for u in range(2):
                pool.memset(v_aug[u][:, :, :, :], 0.0).then_inc(const_done, 1)
            pool.wait_ge(const_done, 2)
            for u in range(2):
                pool.memset(v_aug[u][:, :, :, CD], 1.0).then_inc(const_done, 1)

            def spread(b, u):
                pool.wait_ge(xn_done, b + 1)
                if after(b, 2):
                    pool.wait_ge(s_put, b * CH - CH)
                pool.tensor_tensor(q_head[u][:, :, :], xn[u][:, :].unsqueeze(1).broadcast_to([P, CH, D]),
                                   core.chan_head_of_row[:, :].unsqueeze(2).broadcast_to([P, CH, D]), ALU.mult)\
                    .then_inc(q_spread, 1)

            over_tiles(pool, spread)

        @block.vector
        def _(dve):
            def xn_of(b, u):
                if after(b, 2):
                    dve.wait_ge(q_spread, b - 1)
                normalise(dve, core, xn[u][:, :], b).then_inc(xn_done, 1)

            def find_max(b, g):
                dve.wait_ge(s_put, b * CH + g + 1)
                if after(b, 1) or g >= 4:
                    dve.wait_ge(exp_done, b * CH + g - 3)
                dve.tensor_reduce(neg_max[:, g % 4, :], ps_s[g % 2][:, :].rearrange("p (r k) -> p r k", r=2),
                                  AX.X, ALU.max, negate=True).then_inc(max_done, 1)

            def weigh(b, c):
                dve.wait_ge(r_put, b * 2 + c + 1)
                o = ps_out[:, c * D:c * D + D].rearrange("p (m h e) -> p m h e", m=2, h=4)
                dve.reciprocal(recip[:, :, :], o[:, :, :, CD])
                dve.drain()
                if c == 0 and after(b, 1):
                    dve.wait_ge(a_put, b)
                dve.tensor_tensor(attn[:, :, c * 64:c * 64 + 64].rearrange("p m (h d) -> p m h d", h=4),
                                  o[:, :, :, 0:CD], recip[:, :, :].unsqueeze(3).broadcast_to([P, 2, 4, CD]),
                                  ALU.mult).then_inc(attn_done, 1)

            def add_to_x(b):
                dve.wait_ge(a_put, b + 1)
                dve.tensor_tensor(core.xt(b), core.xt(b), ps_out[:, 0:D], ALU.add).then_inc(x_done, 1)
                dve.drain()
                row_stats(dve, core, b, six)

            def batch(b, u):
                for g in range(CH):
                    find_max(b, g)
                    if g == 0 and ahead(b, 1):
                        xn_of(b + 1, 1 - u)
                    if g == 1 and after(b, 1):
                        weigh(b - 1, 0)
                    if g == 4 and after(b, 1):
                        weigh(b - 1, 1)
                    if g == 6 and after(b, 1):
                        add_to_x(b - 1)

            dve.wait_ge(rstd_done, 1)
            xn_of(0, 0)
            over_tiles(dve, batch)
            weigh(B - 1, 0)
            weigh(B - 1, 1)
            add_to_x(B - 1)

        @block.scalar
        def _(act):
            def values(b, u):
                ctx_loaded(act, b, u)
                if after(b, 2):
                    act.wait_ge(pv_put, b * CH - CH)
                act.activation(v_aug[u][:, :, :, 0:CD], ctxT[u][:, :, :].rearrange("p c (h d) -> p c h d", h=CH),
                               ACT.Copy).then_inc(v_done, 1)

            def exps(b, g):
                act.wait_ge(max_done, b * CH + g + 1)
                if after(b, 1) or g >= 4:
                    act.wait_ge(t_put, b * CH + g - 3)
                for m in range(2):
                    last = act.activation(prob[g % 4][:, m * D:m * D + D], ps_s[g % 2][:, m * D:m * D + D], ACT.Exp,
                                          bias=neg_max[:, g % 4, m:m + 1])
                last.then_inc(exp_done, 1)

            def copy_probT(b, g):
                act.wait_ge(t_put, b * CH + g + 1)
                if after(b, 1) or g >= 2:
                    act.wait_ge(pv_put, b * CH + g - 1)
                act.activation(probT[g % 2][:, :], ps_t[g % 2][:, :], ACT.Copy).then_inc(t_done, 1)

            def copy_o(b, c):
                act.wait_ge(pv_put, b * CH + 4 * c + 4)
                if after(b, 1):
                    act.wait_ge(r_put, b * 2 + c - 1)
                act.activation(o_sb[c][:, :], ps_o[c][:, :], ACT.Copy).then_inc(o_done, 1)

            def batch(b, u):
                for g in range(CH):
                    exps(b, g)
                    if g >= 2:
                        copy_probT(b, g - 2)
                    elif after(b, 1):
                        copy_probT(b - 1, CH - 2 + g)
                    if g == 2 and after(b, 1):
                        copy_o(b - 1, 1)
                    if g == 4 and ahead(b, 1):
                        values(b + 1, 1 - u)
                    if g == 6:
                        copy_o(b, 0)

            act.wait_ge(const_done, 4)
            values(0, 0)
            over_tiles(act, batch)
            copy_probT(B - 1, CH - 2)
            copy_probT(B - 1, CH - 1)
            copy_o(B - 1, 1)

        @block.tensor
        def _(pe):
            def scores(b, g, u):
                if g == 0:
                    ctx_loaded(pe, b, u)
                    pe.wait_ge(q_spread, b + 1)
                if after(b, 1) or g >= 2:
                    pe.wait_ge(exp_done, b * CH + g - 1)
                for m in range(2):
                    last = pe.matmul(ps_s[g % 2][:, m * D:m * D + D], q_head[u][:, g, m * P:m * P + P], ctx[u][:, :],
                                     start=True, stop=True)
                last.then_inc(s_put, 1)

            def turn_prob(b, g):
                pe.wait_ge(exp_done, b * CH + g + 1)
                if after(b, 1) or g >= 2:
                    pe.wait_ge(t_done, b * CH + g - 1)
                for m in range(2):
                    for n in range(2):
                        last = pe.transpose(ps_t[g % 2][:, n * D + m * P:n * D + m * P + P],
                                            prob[g % 4][:, m * D + n * P:m * D + n * P + P], core.ident[:, :])
                last.then_inc(t_put, 1)

            def weigh_values(b, g, u):
                pe.wait_ge(t_done, b * CH + g + 1)
                if g == 0:
                    pe.wait_ge(v_done, b + 1)
                if g % 4 == 0 and after(b, 1):
                    pe.wait_ge(o_done, b * 2 + g // 4 - 1)
                rows = slice(32 * (g % 4), 32 * (g % 4) + 32)
                for n in range(2):
                    last = pe.matmul(ps_o[g // 4][rows, :], v_aug[u][:, n, g, :], probT[g % 2][:, n * D:n * D + D],
                                     start=(n == 0), stop=(n == 1))
                last.then_inc(pv_put, 1)

            def turn_o(b, c):
                pe.wait_ge(o_done, b * 2 + c + 1)
                if c == 1:
                    pe.wait_ge(attn_done, b * 2 + 1)
                elif after(b, 1):
                    pe.wait_ge(x_done, b)
                for m in range(2):
                    last = pe.transpose(ps_out[:, c * D + m * P:c * D + m * P + P], o_sb[c][:, m * P:m * P + P],
                                        core.ident[:, :])
                last.then_inc(r_put, 1)

            def turn_attn(b):
                pe.wait_ge(attn_done, b * 2 + 2)
                for m in range(2):
                    last = pe.transpose(ps_out[:, m * P:m * P + P], attn[:, m, :], core.ident[:, :])
                last.then_inc(a_put, 1)

            def batch(b, u):
                for g in range(CH):
                    scores(b, g, u)
                    if g >= 2:
                        turn_prob(b, g - 2)
                    elif after(b, 1):
                        turn_prob(b - 1, CH - 2 + g)
                    if g >= 3:
                        weigh_values(b, g - 3, u)
                    elif after(b, 1):
                        weigh_values(b - 1, CH - 3 + g, 1 - u)
                    if g == 0 and after(b, 1):
                        turn_o(b - 1, 0)
                    if g == 3 and after(b, 1):
                        turn_o(b - 1, 1)
                    if g == 5 and after(b, 1):
                        turn_attn(b - 1)

            over_tiles(pe, batch)
            turn_prob(B - 1, CH - 2)
            turn_prob(B - 1, CH - 1)
            for g in range(CH - 3, CH):
                weigh_values(B - 1, g, 1)
            turn_o(B - 1, 0)
            turn_o(B - 1, 1)
            turn_attn(B - 1)


MAGIC = 1.5 * 2.0 ** 23


def hadamard_ffn(core, name):
    nc, dram = core.nc, core.dram
    with core.stage() as st:
        def sb(n, shape, dt=F32):
            return core.sb(f"{name}_{n}", shape, dt, st)

        def sem(n):
            return core.sem(f"{name}_{n}", st)

        raw = core.ffn_raw
        wq = [sb(f"w_int{n}", [P, KC * FF], BF16) for n in range(3)]
        gate_w, up_w = (wq[n][:, :].rearrange("p (c f) -> p c f", c=KC) for n in range(2))
        down_w = wq[2][:, :].rearrange("p (c f) -> p c f", c=NF)
        had = core.had
        ones = sb("ones", [P, P])
        magic = sb("magic", [P, 1])
        w_sum, w_mean, w_scale = sb("w_sum", [P, 3]), sb("w_mean", [P, 3]), sb("w_scale", [P, 3])
        xn = sb("xn", [P, D])
        xq = sb("xq", [P, D], BF16)
        xqT = [sb(f"xqT{u}", [P, KC, P], BF16) for u in range(2)]
        a_max, a_rec = sb("a_max", [P, 1]), sb("a_rec", [P, 1])
        deq = [sb(f"deq{u}", [P, 2]) for u in range(2)]
        b_max, b_rec = sb("b_max", [P, 1]), sb("b_rec", [P, 1])
        b_deq = [sb(f"b_deq{u}", [P, 1]) for u in range(2)]
        gate = sb("gate", [P, FF])
        prod = [sb(f"prod{u}", [P, FF]) for u in range(2)]
        fly = sb("fly", [P, FF])
        mixed = [sb(f"mixed{u}", [P, FF]) for u in range(2)]
        mixedT = sb("mixedT", [P, FF])
        rounded = sb("rounded", [P, FF])
        hq = sb("hq", [P, FF], BF16)
        hqT = sb("hqT", [P, FF], BF16)
        six = sb("six", [P, 6])
        ps_g = core.ps(f"{name}_ps_g", [P, FF], F32, st)
        ps_u = core.ps(f"{name}_ps_u", [P, FF], F32, st)
        ps_t = core.ps(f"{name}_ps_t", [P, W4], F32, st)
        ps_q = core.ps(f"{name}_ps_q", [P, W4], F32, st)
        ps_f = core.ps(f"{name}_ps_f", [P, FF], F32, st)
        ps_hqT = ps_q[:, 0:D].bitcast(BF16)
        ps_xqT = ps_q[:, 0:P].bitcast(BF16)
        ps_y = ps_q[:, D:2 * D]
        (const_done, rstd_done, sum_done, mean_put, scale_done, w_rounded, w_done, xq_done, deq_done, xqT_put, xqT_done, gate_put,
         up_put, silu_done, prod_done, mixed_done, mixT_put, mixT_done, had_put, b_scale, round_done, hq_done,
         hqT_put, hqT_done, y_put, x_done) = (sem(n) for n in (
             "const_done", "rstd_done", "sum_done", "mean_put", "scale_done", "w_rounded", "w_done", "xq_done", "deq_done", "xqT_put",
             "xqT_done", "gate_put", "up_put", "silu_done", "prod_done", "mixed_done", "mixT_put", "mixT_done",
             "had_put", "b_scale", "round_done", "hq_done", "hqT_put", "hqT_done", "y_put", "x_done"))
        block = st.enter_context(nc.Block())

        @block.gpsimd
        def _(pool):
            all_rstd(pool, core, rstd_done)
            pool.memset(ones[:, :], 1.0).then_inc(const_done, 1)
            pool.memset(magic[:, :], MAGIC).then_inc(const_done, 1)

            def butterflies(t, u):
                pool.wait_ge(prod_done, t + 1)
                if after(t, 2):
                    pool.wait_ge(mixT_put, t - 1)
                for n, (src, dst) in enumerate(((prod[u], fly), (fly, prod[u]), (prod[u], mixed[u]))):
                    v, o = (m[:, :].rearrange("p (a two c) -> p a two c", two=2, c=P << n) for m in (src, dst))
                    if n:
                        pool.drain()
                    pool.tensor_tensor(o[:, :, 0, :], v[:, :, 0, :], v[:, :, 1, :], ALU.add)
                    last = pool.tensor_tensor(o[:, :, 1, :], v[:, :, 0, :], v[:, :, 1, :], ALU.subtract)
                last.then_inc(mixed_done, 1)

            over_tiles(pool, butterflies)

        @block.vector
        def _(dve):
            def scale_weights():
                for n in range(3):
                    dve.wait_ge(core.ffn_in[n], 16)
                    dve.tensor_reduce(w_sum[:, n:n + 1], raw[n][:, :], AX.X, ALU.add, apply_absolute_value=True)\
                       .then_inc(sum_done, 1)
                dve.wait_ge(mean_put, 1)
                dve.tensor_scalar(w_mean[:, :], ps_f[:, 0:3], 1.0 / (D * FF), 1e-5, ALU.mult, ALU.max)
                dve.drain()
                dve.reciprocal(w_scale[:, :], w_mean[:, :]).then_inc(scale_done, 1)

            def clip_weights():
                for n in range(3):
                    dve.wait_ge(w_rounded, n + 1)
                    dve.tensor_scalar(raw[n][:, :], raw[n][:, :], MAGIC + 1.0, MAGIC - 1.0, ALU.min, ALU.max)
                    dve.drain()
                    dve.tensor_scalar(wq[n][:, :], raw[n][:, :], MAGIC, None, ALU.subtract).then_inc(w_done, 1)

            def quantise_x(t, u):
                dve.drain()
                normalise(dve, core, xn[:, :], t)
                dve.drain()
                dve.tensor_reduce(a_max[:, :], xn[:, :], AX.X, ALU.max, apply_absolute_value=True)
                dve.drain()
                dve.tensor_scalar(a_max[:, :], a_max[:, :], 1e-5, 1.0 / 128, ALU.max, ALU.mult)
                dve.drain()
                dve.reciprocal(a_rec[:, :], a_max[:, :])
                if after(t, 2):
                    dve.wait_ge(silu_done, t - 1)
                dve.tensor_scalar(deq[u][:, :], w_mean[:, 0:2], a_max[:, :], None, ALU.mult)\
                   .then_inc(deq_done, 1)
                dve.drain()
                dve.tensor_scalar(xn[:, :], xn[:, :], a_rec[:, :], MAGIC, ALU.mult, ALU.add)
                dve.drain()
                if after(t, 1):
                    dve.wait_ge(xqT_put, t)
                dve.tensor_scalar(xq[:, :], xn[:, :], MAGIC, 127.0, ALU.subtract, ALU.min).then_inc(xq_done, 1)

            def gate_times_up(t, u):
                dve.wait_ge(silu_done, t + 1)
                dve.wait_ge(up_put, t + 1)
                if after(t, 2):
                    dve.wait_ge(mixed_done, t - 1)
                dve.scalar_tensor_tensor(out=prod[u][:, :], in0=ps_u[:, :], scalar=deq[u][:, 1:2], in1=gate[:, :],
                                         op0=ALU.mult, op1=ALU.mult).then_inc(prod_done, 1)

            def scale_h(t, u):
                dve.wait_ge(had_put, t + 1)
                dve.tensor_reduce(b_max[:, :], ps_f[:, :], AX.X, ALU.max, apply_absolute_value=True)
                dve.drain()
                dve.tensor_scalar(b_max[:, :], b_max[:, :], 32 * EPS_Q, 1.0 / 128, ALU.max, ALU.mult)
                dve.drain()
                dve.tensor_scalar(b_deq[u][:, :], b_max[:, :], w_mean[:, 2:3], 1.0 / 32, ALU.mult, ALU.mult)
                dve.reciprocal(b_rec[:, :], b_max[:, :]).then_inc(b_scale, 1)

            def quantise_h(t):
                dve.wait_ge(round_done, t + 1)
                if after(t, 1):
                    dve.wait_ge(hqT_put, 2 * t)
                dve.tensor_scalar(hq[:, :], rounded[:, :], MAGIC, 127.0, ALU.subtract, ALU.min).then_inc(hq_done, 1)

            def add_to_x(t, u):
                dve.wait_ge(y_put, t + 1)
                dve.scalar_tensor_tensor(out=core.xt(t), in0=ps_y, scalar=b_deq[u][:, :], in1=core.xt(t),
                                         op0=ALU.mult, op1=ALU.add).then_inc(x_done, 1)
                dve.drain()
                row_stats(dve, core, t, six)

            def tile(t, u):
                if ahead(t, 3):
                    quantise_x(t + 3, 1 - u)
                if ahead(t, 2):
                    gate_times_up(t + 2, u)
                scale_h(t, u)
                if after(t, 1):
                    add_to_x(t - 1, 1 - u)
                quantise_h(t)

            scale_weights()
            dve.wait_ge(rstd_done, 1)
            quantise_x(0, 0)
            quantise_x(1, 1)
            clip_weights()
            gate_times_up(0, 0)
            quantise_x(2, 0)
            gate_times_up(1, 1)
            over_long_pipe(dve, tile)
            add_to_x(B - 1, 1)

        @block.scalar
        def _(act):
            def copy_xqT(t, u):
                act.wait_ge(xqT_put, t + 1)
                if after(t, 2):
                    act.wait_ge(up_put, t - 1)
                act.activation(xqT[u][:, :, :].rearrange("p c t -> p (c t)"), ps_xqT, ACT.Copy).then_inc(xqT_done, 1)

            def silu(t, u):
                act.wait_ge(gate_put, t + 1)
                act.wait_ge(deq_done, t + 1)
                if after(t, 1):
                    act.wait_ge(prod_done, t)
                act.activation(gate[:, :], ps_g[:, :], ACT.Silu, scale=deq[u][:, 0:1]).then_inc(silu_done, 1)

            def copy_mixedT(t, half):
                act.wait_ge(mixT_put, 2 * t + half + 1)
                if after(t, 1) and half == 0:
                    act.wait_ge(had_put, t)
                act.activation(mixedT[:, half * W4:half * W4 + W4], ps_t[:, :], ACT.Copy).then_inc(mixT_done, 1)

            def round_h(t):
                act.wait_ge(b_scale, t + 1)
                if after(t, 1):
                    act.wait_ge(hq_done, t)
                act.activation(rounded[:, :], ps_f[:, :], ACT.Identity, bias=magic[:, :], scale=b_rec[:, :])\
                    .then_inc(round_done, 1)

            def copy_hqT(t, half):
                act.wait_ge(hqT_put, 2 * t + half + 1)
                if after(t, 1) and half == 0:
                    act.wait_ge(y_put, t)
                act.activation(hqT[:, half * W4:half * W4 + W4], ps_hqT, ACT.Copy).then_inc(hqT_done, 1)

            def tile(t, u):
                copy_mixedT(t, 0)
                copy_mixedT(t, 1)
                if ahead(t, 2):
                    silu(t + 2, u)
                if after(t, 1):
                    copy_hqT(t - 1, 0)
                    copy_hqT(t - 1, 1)
                if ahead(t, 3):
                    copy_xqT(t + 3, 1 - u)
                round_h(t)

            act.wait_ge(const_done, 2)
            act.wait_ge(scale_done, 1)
            for n in range(3):
                act.activation(raw[n][:, :], raw[n][:, :], ACT.Identity, bias=magic[:, :], scale=w_scale[:, n:n + 1])\
                   .then_inc(w_rounded, 1)
            copy_xqT(0, 0)
            copy_xqT(1, 1)
            silu(0, 0)
            copy_xqT(2, 0)
            silu(1, 1)
            over_long_pipe(act, tile)
            copy_hqT(B - 1, 0)
            copy_hqT(B - 1, 1)

        @block.tensor
        def _(pe):
            def turn_xq(t, u):
                pe.wait_ge(xq_done, t + 1)
                if after(t, 1):
                    pe.wait_ge(xqT_done, t)
                if after(t, 4):
                    pe.wait_ge(hqT_done, 2 * t - 6)
                for c in range(KC):
                    last = pe.transpose(ps_xqT[:, c * P:c * P + P], xq[:, c * P:c * P + P], core.identb[:, :])
                last.then_inc(xqT_put, 1)

            def gate_up(t, u, which):
                if which == 0:
                    pe.wait_ge(xqT_done, t + 1)
                for ps, w, free, put in ((ps_g, gate_w, silu_done, gate_put), (ps_u, up_w, prod_done, up_put))[which:which + 1]:
                    if after(t, 1):
                        pe.wait_ge(free, t)
                    for h in range(2):
                        for c in range(KC):
                            last = pe.matmul(ps[:, h * W4:h * W4 + W4], xqT[u][:, c, :], w[:, c, h * W4:h * W4 + W4],
                                             start=(c == 0), stop=(c == KC - 1))
                    last.then_inc(put, 1)

            def turn_mixed(t, u, half):
                if half == 0:
                    pe.wait_ge(mixed_done, t + 1)
                if half or after(t, 1):
                    pe.wait_ge(mixT_done, 2 * t + half)
                for c in range(half * NF // 2, (half + 1) * NF // 2):
                    at = (c % (NF // 2)) * P
                    last = pe.transpose(ps_t[:, at:at + P], mixed[u][:, c * P:c * P + P], core.ident[:, :])
                last.then_inc(mixT_put, 1)

            def transform(t, half):
                if half == 0:
                    pe.wait_ge(mixT_done, 2 * t + 2)
                    if after(t, 1):
                        pe.wait_ge(round_done, t)
                for c in range(half * NF // 2, (half + 1) * NF // 2):
                    last = pe.matmul(ps_f[:, c * P:c * P + P], mixedT[:, c * P:c * P + P], had[:, :], start=True, stop=True)
                if half:
                    last.then_inc(had_put, 1)

            def turn_hq(t, half):
                if half == 0:
                    pe.wait_ge(hq_done, t + 1)
                    if after(t, 1):
                        pe.wait_ge(x_done, t)
                    if ahead(t, 3):
                        pe.wait_ge(xqT_done, t + 4)
                else:
                    pe.wait_ge(hqT_done, 2 * t + 1)
                for c in range(NF // 2):
                    at = half * W4 + c * P
                    last = pe.transpose(ps_hqT[:, c * P:c * P + P], hq[:, at:at + P], core.identb[:, :])
                last.then_inc(hqT_put, 1)

            def down(t):
                pe.wait_ge(hqT_done, 2 * t + 2)
                if ahead(t, 4):
                    pe.wait_ge(xqT_done, t + 5)
                for c in range(NF):
                    last = pe.matmul(ps_y, hqT[:, c * P:c * P + P], down_w[:, c, :], start=(c == 0), stop=(c == NF - 1))
                last.then_inc(y_put, 1)

            def tile(t, u):
                for half in range(2):
                    turn_mixed(t, u, half)
                    if ahead(t, 2):
                        gate_up(t + 2, u, half)
                for half in range(2):
                    transform(t, half)
                    if after(t, 1):
                        turn_hq(t - 1, half)
                if ahead(t, 3):
                    turn_xq(t + 3, 1 - u)
                if after(t, 1):
                    down(t - 1)

            pe.wait_ge(const_done, 2)
            pe.wait_ge(core.had_in, 16)
            pe.wait_ge(sum_done, 3)
            pe.matmul(ps_f[:, 0:3], ones[:, :], w_sum[:, :], start=True, stop=True).then_inc(mean_put, 1)
            turn_xq(0, 0)
            turn_xq(1, 1)
            pe.wait_ge(w_done, 3)
            gate_up(0, 0, 0)
            gate_up(0, 0, 1)
            turn_xq(2, 0)
            gate_up(1, 1, 0)
            gate_up(1, 1, 1)
            over_long_pipe(pe, tile)
            turn_hq(B - 1, 0)
            turn_hq(B - 1, 1)
            down(B - 1)


def gated_long_conv(core, name):
    nc, dram = core.nc, core.dram
    NH, N8 = 16, 8
    COLS = B * N8 * N8
    with core.stage() as st:
        def sb(n, shape, dt=F32, c=st):
            return core.sb(f"{name}_{n}", shape, dt, c)

        def sem(n):
            return core.sem(f"{name}_{n}", st)

        ctxT = sb("ctxT", [P, KC, B, P])
        vT = sb("vT", [P, KC, B, P])
        outT = sb("outT", [P, KC, B, P])
        xn = [sb(f"xn{u}", [P, D]) for u in range(2)]
        skip = sb("skip", [P, P])
        taps = sb("taps", [P, NH, D])
        six = sb("six", [P, 6])
        (ctx_in, taps_in, rstd_done, xn_done, xnT_put, xnT_done, kv_done, tap_done, y_put, z_done, fold_done,
         gated, skip_sum, skip_done, out_put, x_done) = (sem(n) for n in (
             "ctx_in", "taps_in", "rstd_done", "xn_done", "xnT_put", "xnT_done", "kv_done", "tap_done", "y_put",
             "z_done", "fold_done", "gated", "skip_sum", "skip_done", "out_put", "x_done"))

        with ExitStack() as ph:
            ps = [core.ps(f"{name}_ps_x{u}", [P, W4], F32, ph) for u in range(2)]
            block = ph.enter_context(nc.Block())

            @block.sync
            def _(sp):
                for c in range(KC):
                    sp.dma_start(ctxT[:, c, :, :], dram["ctxT"][:, :, c, :].rearrange("b p t -> p b t"))\
                      .then_inc(ctx_in, 16)
                sp.dma_start(skip[:, :], dram["skip"].partition_broadcast(P)).then_inc(ctx_in, 16)
                sp.dma_start(taps[:, :, :], dram["l1a_taps"]).then_inc(taps_in, 16)

            @block.gpsimd
            def _(pool):
                all_rstd(pool, core, rstd_done)

            @block.vector
            def _(dve):
                dve.wait_ge(rstd_done, 1)

                def tile(b, u):
                    if after(b, 2):
                        dve.wait_ge(xnT_put, b - 1)
                    normalise(dve, core, xn[u][:, :], b).then_inc(xn_done, 1)

                over_tiles(dve, tile)

            @block.scalar
            def _(act):
                def tile(b, u):
                    act.wait_ge(xnT_put, b + 1)
                    act.activation(vT[:, :, bass.ds(b, 1), :].rearrange("p c a t -> p c (a t)"),
                                   ps[u][:, 0:D].rearrange("p (c t) -> p c t", c=KC), ACT.Copy).then_inc(xnT_done, 1)

                over_tiles(act, tile)

            @block.tensor
            def _(pe):
                def tile(b, u):
                    pe.wait_ge(xn_done, b + 1)
                    if after(b, 2):
                        pe.wait_ge(xnT_done, b - 1)
                    for c in range(KC):
                        last = pe.transpose(ps[u][:, c * P:c * P + P], xn[u][:, c * P:c * P + P], core.ident[:, :])
                    last.then_inc(xnT_put, 1)

                over_tiles(pe, tile)

        with ExitStack() as ph:
            kv = [sb(f"kv{u}", [P, KC, COLS], F32, ph) for u in range(2)]
            tap = [sb(f"tap{u}", [P, D], F32, ph) for u in range(2)]
            z = [sb(f"z{c}", [P, COLS], F32, ph) for c in range(2)]
            ps = [[core.ps(f"{name}_ps_y{u}{c}", [P, COLS], F32, ph) for c in range(KC)] for u in range(2)]
            block = ph.enter_context(nc.Block())

            @block.gpsimd
            def _(pool):
                pool.wait_ge(ctx_in, 48)

                def outer(h, u):
                    for c in range(KC):
                        i_rows = vT[:, c, :, bass.ds(h * N8, N8)].unsqueeze(3).broadcast_to([P, B, N8, N8])
                        j_rows = ctxT[:, c, :, bass.ds(h * N8, N8)].unsqueeze(2).broadcast_to([P, B, N8, N8])
                        if c == 0 and after(h, 2):
                            pool.wait_ge(y_put, h * 2 - 2)
                        pool.tensor_tensor(kv[u][:, c, :].rearrange("p (b i j) -> p b i j", b=B, i=N8),
                                           i_rows, j_rows, ALU.mult).then_inc(kv_done, 1)

                over_tiles(pool, outer, NH)

            @block.scalar
            def _(act):
                act.wait_ge(taps_in, 16)

                def stage(h, u):
                    if after(h, 2):
                        act.wait_ge(y_put, h * 2 - 2)
                    act.activation(tap[u][:, :], taps[:, bass.ds(h, 1), :].rearrange("p a l -> p (a l)"), ACT.Copy)\
                        .then_inc(tap_done, 1)

                over_tiles(act, stage, NH)

            @block.tensor
            def _(pe):
                def conv(h, u):
                    pe.wait_ge(tap_done, h + 1)
                    for c in range(KC):
                        pe.wait_ge(kv_done, h * 2 + c + 1)
                        if after(h, 2):
                            pe.wait_ge(z_done, h * 2 - 3 + c)
                        for n in range(2):
                            cols = slice(n * W4, n * W4 + W4)
                            for m in range(c + 1):
                                last = pe.matmul(ps[u][c][:, cols], tap[u][:, (c - m) * P:(c - m) * P + P],
                                                 kv[u][:, m, cols], start=(m == 0), stop=(m == c))
                        last.then_inc(y_put, 1)

                over_tiles(pe, conv, NH)

            @block.vector
            def _(dve):
                dve.wait_ge(ctx_in, 48)

                def gate(h, u):
                    for c in range(KC):
                        dve.wait_ge(y_put, h * 2 + c + 1)
                        x1 = ctxT[:, c, :, bass.ds(h * N8, N8)].unsqueeze(3).broadcast_to([P, B, N8, N8])
                        if after(h, 1):
                            dve.wait_ge(fold_done, h * 2 - 1 + c)
                        dve.tensor_tensor(z[c][:, :].rearrange("p (b i j) -> p b i j", b=B, i=N8),
                                          ps[u][c][:, :].rearrange("p (b i j) -> p b i j", b=B, i=N8), x1, ALU.mult)\
                           .then_inc(z_done, 1)
                    for c in range(KC):
                        dve.wait_ge(z_done, h * 2 + c + 1)
                        dve.tensor_reduce(outT[:, c, :, bass.ds(h * N8, N8)],
                                          z[c][:, :].rearrange("p (b i j) -> p b j i", b=B, i=N8), AX.X, ALU.add)\
                           .then_inc(fold_done, 1)

                over_tiles(dve, gate, NH)

        with ExitStack() as ph:
            weight = sb("skip_weight", [P, KC, B, NH], F32, ph)
            ps = [core.ps(f"{name}_ps_o{u}", [P, W4], F32, ph) for u in range(2)]
            block = ph.enter_context(nc.Block())

            @block.gpsimd
            def _(pool):
                for c in range(KC):
                    pool.tensor_tensor(vT[:, c, :, :], vT[:, c, :, :], ctxT[:, c, :, :], ALU.mult)
                    pool.drain()
                    pool.tensor_tensor(vT[:, c, :, :], vT[:, c, :, :],
                                       skip[:, :].unsqueeze(1).broadcast_to([P, B, P]), ALU.mult).then_inc(gated, 1)

            @block.vector
            def _(dve):
                for c in range(KC):
                    dve.wait_ge(gated, c + 1)
                    dve.tensor_reduce(weight[:, c, :, :], vT[:, c, :, :].rearrange("p b (h i) -> p b h i", i=N8),
                                      AX.X, ALU.add)
                    dve.drain()
                    dve.tensor_tensor(vT[:, c, :, :].rearrange("p b (h j) -> p b h j", j=N8),
                                      weight[:, c, :, :].unsqueeze(3).broadcast_to([P, B, NH, N8]),
                                      ctxT[:, c, :, :].rearrange("p b (h j) -> p b h j", j=N8), ALU.mult)
                    dve.drain()
                    dve.tensor_tensor(outT[:, c, :, :], outT[:, c, :, :], vT[:, c, :, :], ALU.add)\
                       .then_inc(skip_done, 1)
                for b in range(B):
                    dve.wait_ge(out_put, b + 1)
                    dve.tensor_tensor(core.xt(b), core.xt(b), ps[b % 2][:, 0:D], ALU.add).then_inc(x_done, 1)
                    dve.drain()
                    row_stats(dve, core, b, six)

            @block.tensor
            def _(pe):
                pe.wait_ge(skip_done, KC)
                for b in range(B):
                    if b >= 2:
                        pe.wait_ge(x_done, b - 1)
                    for c in range(KC):
                        last = pe.transpose(ps[b % 2][:, c * P:c * P + P], outT[:, c, b, :], core.ident[:, :])
                    last.then_inc(out_put, 1)


def over_ring(eng, body, n, ring, lead=1):
    for j in range(lead * ring):
        body(j, j % ring)
    with eng.Fori(lead, n // ring - 1) as i:
        for r in range(ring):
            body(i * ring + r, r)
    for r in range(ring):
        body(n - ring + r, r)


LAG = 6
RING = 4


def moe_ffn(core, name, E, K, FE, capacity=None, shared=0, rms=False, biased=False, renorm=False, top_softmax=False):
    nc, dram = core.nc, core.dram
    NT = E * capacity // P if capacity else T * K // P + E
    NT += NT % RING and RING - NT % RING
    FCH = FE // 2 if FE > P else FE
    NJ = FE // FCH
    NL = E + (1 if rms else 0)
    FS = -(-shared // P)
    with core.stage() as st:
        def sb(n, shape, dt=F32):
            return core.sb(f"{name}_{n}", shape, dt, st)

        def sem(n):
            return core.sem(f"{name}_{n}", st)

        rows = sb("rows", [P, B, D])
        row1 = [sb(f"row1_{u}", [P, D]) for u in range(2)]
        xT1 = [sb(f"xT1_{u}", [P, KC, P]) for u in range(2)]
        router = sb("router", [P, KC, NL])
        logit = sb("logit", [P, B, NL])
        prob = sb("prob", [P, B, E])
        red = sb("red", [P, B])
        top, top_i = sb("top", [P, B, 8]), sb("top_i", [P, B, 8], U32)
        topf = sb("topf", [P, B, 8])
        expert = sb("expert", [P, E])
        onehot = sb("onehot", [P, B, K, E])
        chosen = sb("chosen", [P, 2 * B, E], BF16)
        before, onesb = sb("before", [P, P], BF16), sb("onesb", [P, P], BF16)
        place = sb("place", [P, B, E])
        spot = sb("spot", [P, B, K])
        spot2 = sb("spot2", [P, B, K])
        flag = sb("flag", [P, B, K])
        weight = sb("weight", [P, B, K])
        to_slot, from_slot = sb("to_slot", [P, B, K], U32), sb("from_slot", [P, B, K], U32)
        six = sb("six", [P, 6])
        xin = [sb(f"xin{r}", [P, D]) for r in range(RING)]
        xinT = [sb(f"xinT{u}", [P, KC, P]) for u in range(2)]
        act_sb = [sb(f"act_sb{u}", [P, FE]) for u in range(2)]
        h_sb = [sb(f"h_sb{u}", [P, FE]) for u in range(2)]
        hT_sb = [sb(f"hT_sb{u}", [FCH, NJ, P]) for u in range(2)]
        y_sb = [sb(f"y_sb{r}", [P, D]) for r in range(RING)]
        got = [sb(f"got{u}", [P, K, D]) for u in range(2)]
        if capacity:
            w_gu = [sb(f"w_gu{r}", [P, KC, 2 * FE]) for r in range(RING)]
            w_d = [sb(f"w_d{r}", [FCH, NJ, D]) for r in range(RING)]
        else:
            w_gu_all = sb("w_gu_all", [P, E * KC * 2 * FE])
            w_d_all = sb("w_d_all", [FCH, E * NJ * D])
            tiles, ends, base = sb("tiles", [P, E]), sb("ends", [P, E]), sb("base", [P, E])
            ones_e = sb("ones_e", [P, E])
            tile_no = sb("tile_no", [P, NT])
            past = sb("past", [P, NT, E])
            owner, owner_i = sb("owner", [P, NT]), sb("owner_i", [P, NT], I32)
        if biased:
            bias = sb("bias", [P, E])
        if rms:
            norm_w = sb("norm_w", [P, D])
            square, squares, rms_f = sb("square", [P, D]), sb("squares", [P, B]), sb("rms_f", [P, B])
            gate_f = sb("gate_f", [P, B])
        if shared:
            xT = sb("xT", [P, KC, T])
            sw_g, sw_u = sb("sw_g", [P, KC, shared]), sb("sw_u", [P, KC, shared])
            sw_d = sb("sw_d", [P, FS, D])
            s_act = [sb(f"s_act{u}", [P, W4]) for u in range(2)]
            s_hT = [sb(f"s_hT{u}", [P, FS, W4]) for u in range(2)]
        ps_x = [core.ps(f"{name}_ps_x{u}", [P, D], F32, st) for u in range(2)]
        ps_l = core.ps(f"{name}_ps_l", [P, W4], F32, st)
        ps_p = core.ps(f"{name}_ps_p", [P, W4], F32, st)
        ps_g = [core.ps(f"{name}_ps_g{u}", [P, W4], F32, st) for u in range(2)]
        ps_u = [core.ps(f"{name}_ps_u{u}", [P, W4], F32, st) for u in range(2)]
        (w_in, sw_in, ew_in, const_done, rstd_done, ln_done, sq_done, rms_done, row_done, row_kept, xT_put, xT_done,
         l_put, l_done, max_done, e_done, chosen_done, place_put, counted, owner_done, to_done, from_done, gate_e,
         sg_put, s_silu, s_mul, sd_put, sd_done, in_turned, in_copied, gu_put, e_silu, e_mul, h_turned,
         h_copied, yd_put, y_copied, added) = (sem(n) for n in (
             "w_in", "sw_in", "ew_in", "const_done", "rstd_done", "ln_done", "sq_done", "rms_done", "row_done",
             "row_kept", "xT_put", "xT_done", "l_put", "l_done", "max_done", "e_done", "chosen_done", "place_put",
             "counted", "owner_done", "to_done", "from_done", "gate_e", "sg_put", "s_silu", "s_mul",
             "sd_put", "sd_done", "in_turned", "in_copied", "gu_put", "e_silu", "e_mul", "h_turned", "h_copied",
             "yd_put", "y_copied", "added"))
        xin_in = [sem(f"xin_in{r}") for r in range(RING)]
        gu_in, down_in = ([sem(f"{n}{r}") for r in range(RING)] for n in ("gu_in", "down_in"))
        y_out = [sem(f"y_out{r}") for r in range(RING)]
        scattered, got_in = core.scattered, core.gathered
        scattered_before, got_before = core.n_scattered, core.n_gathered
        core.n_scattered += B * K * 16
        core.n_gathered += B // 2 * K * 16
        n_loads = 1 + rms + biased
        slots, results = core.slots[0:NT * P, :], core.results[0:NT * P, :]
        block = st.enter_context(nc.Block())

        def chunk_rows(f):
            return min(P, shared - f * P)

        @block.sync
        def _(sp):
            sp.dma_start(router[:, :, :], dram[f"{name}_router"]).then_inc(w_in, 16)
            if biased:
                sp.dma_start(bias[:, :], dram[f"{name}_bias"].partition_broadcast(P)).then_inc(w_in, 16)
            if rms:
                sp.dma_start(norm_w[:, :], dram[f"{name}_norm_w"].partition_broadcast(P)).then_inc(w_in, 16)
            if shared:
                sp.dma_start(sw_g[:, :, :], dram[f"{name}_sw_g"]).then_inc(sw_in, 16)
                sp.dma_start(sw_u[:, :, :], dram[f"{name}_sw_u"]).then_inc(sw_in, 16)
                whole = shared // P * P
                sp.dma_start(sw_d[:, 0:shared // P, :], dram[f"{name}_sw_d"][0:whole, :]
                             .rearrange("(f p) d -> p f d", p=P)).then_inc(sw_in, 16)
                if shared > whole:
                    sp.dma_start(sw_d[0:shared - whole, FS - 1, :], dram[f"{name}_sw_d"][whole:shared, :])\
                      .then_inc(sw_in, 16)
            if not capacity:
                sp.dma_start(w_gu_all[:, :].rearrange("p (e n) -> p e n", e=E), dram[f"{name}_w_gu"]
                             .rearrange("e p c n -> p e (c n)")).then_inc(ew_in, 16)
                sp.dma_start(w_d_all[:, :].rearrange("p (e n) -> p e n", e=E), dram[f"{name}_w_d"]
                             .rearrange("e p c n -> p e (c n)")).then_inc(ew_in, 16)

            def store(j, u):
                sp.wait_ge(y_copied, j + 1)
                sp.dma_start(results[bass.ds(j * P, P), :], y_sb[u][:, :]).then_inc(y_out[u], 16)

            def load_down(j, r):
                if after(j, RING):
                    sp.wait_ge(yd_put, j - (RING - 1))
                sp.dma_start(w_d[r][:, :, :], dram[f"{name}_w_d"][bass.ds(j, 1)]
                             .rearrange("e p c n -> p (e c) n")).then_inc(down_in[r], 16)

            def load(j, r):
                if capacity:
                    if after(j, RING):
                        sp.wait_ge(gu_put, j - (RING - 1))
                    sp.dma_start(w_gu[r][:, :, :], dram[f"{name}_w_gu"][bass.ds(j, 1)]
                                 .rearrange("e p c n -> p (e c) n")).then_inc(gu_in[r], 16)
                if isinstance(j, int) and j == 0:
                    sp.wait_ge(scattered, scattered_before + B * K * 16)
                if after(j, RING):
                    sp.wait_ge(in_turned, j - (RING - 1))
                sp.dma_start(xin[r][:, :], slots[bass.ds(j * P, P), :]).then_inc(xin_in[r], 16)
                if capacity and after(j, 1):
                    load_down(j - 1, (r - 1) % RING)
                if after(j, LAG):
                    store(j - LAG, (r - LAG) % RING)

            over_ring(sp, load, NT, RING, 2)
            if capacity:
                load_down(NT - 1, (NT - 1) % RING)
            for j in range(NT - LAG, NT):
                store(j, j % RING)

        @block.gpsimd
        def _(pool):
            all_rstd(pool, core, rstd_done)
            pool.iota(expert[:, :], [[1, E]], base=0, channel_multiplier=0, allow_small_or_imprecise_dtypes=True)\
                .then_inc(const_done, 1)
            pool.memset(before[:, :], 1.0).then_inc(const_done, 1)
            pool.memset(onesb[:, :], 1.0).then_inc(const_done, 1)
            pool.wait_ge(const_done, 3)
            pool.affine_select(out=before[:, :], in_=before[:, :], compare_op=ALU.is_gt, fill=0.0, base=0,
                               pattern=[[1, P]], channel_multiplier=-1).then_inc(const_done, 1)
            if not capacity:
                pool.memset(ones_e[:, :], 1.0).then_inc(const_done, 1)
                pool.iota(tile_no[:, :], [[1, NT]], base=0, channel_multiplier=0,
                          allow_small_or_imprecise_dtypes=True).then_inc(const_done, 1)
            if rms:
                pool.wait_ge(sq_done, B)
                pool.tensor_scalar(rms_f[:, :], squares[:, :], 1.0 / D, 1e-6, ALU.mult, ALU.add)
                pool.drain()
                pool.tensor_tensor(rms_f[:, :], rms_f[:, :], core.minus_half[:, :], ALU.pow).then_inc(rms_done, 1)
            pool.wait_ge(to_done, 1)
            pool.wait_ge(row_kept, B)
            for t in range(B):
                for k in range(K):
                    limit = dict(bounds_check=E * capacity - 1, oob_is_err=False) if capacity else {}
                    pool.indirect_dma_start(
                        out=slots, out_offset=bass.IndirectOffsetOnAxis(ap=to_slot[:, t, k:k + 1], axis=0),
                        in_=rows[:, t, :], in_offset=None, **limit).then_inc(scattered, 16)
            pool.wait_ge(from_done, 1)
            for r in range(RING):
                pool.wait_ge(y_out[r], NT // RING * 16)
            for t in range(B):
                if t >= 2:
                    pool.wait_ge(added, t - 1)
                for k in range(K):
                    pool.indirect_dma_start(
                        out=got[t % 2][:, k, :], out_offset=None, in_=results,
                        in_offset=bass.IndirectOffsetOnAxis(ap=from_slot[:, t, k:k + 1], axis=0))\
                        .then_inc(got_in[t % 2], 16)

        @block.vector
        def _(dve):
            dve.memset(chosen[:, 0:B, :], 0.0)
            dve.wait_ge(rstd_done, 1)
            if rms:
                def first(t, u):
                    normalise(dve, core, rows[:, bass.ds(t, 1), :].rearrange("p a d -> p (a d)"), t)
                    dve.drain()
                    dve.tensor_tensor(core.xt(t), core.xt(t), rows[:, bass.ds(t, 1), :].rearrange("p a d -> p (a d)"),
                                      ALU.add).then_inc(ln_done, 1)

                over_tiles(dve, first)
                dve.wait_ge(rms_done, 1)
            dve.wait_ge(w_in, 16 * n_loads)

            def row(t, u):
                if after(t, 2):
                    dve.wait_ge(row_kept, t - 1)
                    dve.wait_ge(xT_put, t - 1)
                if rms:
                    dve.scalar_tensor_tensor(out=row1[u][:, :], in0=rows[:, bass.ds(t, 1), :].rearrange("p a d -> p (a d)"),
                                             scalar=rms_f[:, bass.ds(t, 1)], in1=norm_w[:, :], op0=ALU.mult,
                                             op1=ALU.mult).then_inc(row_done, 1)
                else:
                    normalise(dve, core, row1[u][:, :], t).then_inc(row_done, 1)

            def keep_logits(t):
                dve.wait_ge(l_put, t + 1)
                out = logit[:, bass.ds(t, 1), :].rearrange("p a e -> p (a e)")
                if biased:
                    dve.tensor_tensor(out, ps_l[:, 0:NL], bias[:, :], ALU.add).then_inc(l_done, 1)
                else:
                    dve.tensor_copy(out, ps_l[:, 0:NL]).then_inc(l_done, 1)

            def tile(t, u):
                if ahead(t, 1):
                    row(t + 1, 1 - u)
                keep_logits(t)

            row(0, 0)
            over_tiles(dve, tile)
            dve.drain()

            logits = logit[:, :, 0:E]
            if top_softmax:
                ranked = logit
            else:
                ranked = prob
                dve.tensor_reduce(red[:, :], logits, AX.X, ALU.max)
                dve.drain()
                dve.tensor_tensor(prob[:, :, :], logits, red[:, :].unsqueeze(2).broadcast_to([P, B, E]), ALU.subtract)\
                   .then_inc(max_done, 1)
                dve.wait_ge(e_done, 1)
                dve.tensor_reduce(red[:, :], prob[:, :, :], AX.X, ALU.add)
                dve.drain()
                dve.reciprocal(red[:, :], red[:, :])
                dve.drain()
                dve.tensor_tensor(prob[:, :, :], prob[:, :, :], red[:, :].unsqueeze(2).broadcast_to([P, B, E]), ALU.mult)
                dve.drain()
            for t in range(B):
                dve.max(top[:, t, :], ranked[:, t, 0:E])
            dve.drain()
            for t in range(B):
                dve.max_index(top_i[:, t, :], top[:, t, :], ranked[:, t, 0:E])
            dve.drain()
            dve.tensor_copy(topf[:, :, :], top_i[:, :, :])
            dve.wait_ge(const_done, 4 if capacity else 6)
            dve.drain()
            for k in range(K):
                dve.tensor_tensor(onehot[:, :, k, :], expert[:, :].unsqueeze(1).broadcast_to([P, B, E]),
                                  topf[:, :, k:k + 1].broadcast_to([P, B, E]), ALU.is_equal)
            dve.drain()
            with nc.allow_low_precision(reason="zeros and ones"):
                dve.tensor_reduce(chosen[:, B:, :], onehot[:, :, :, :].rearrange("p t k e -> p t e k"), AX.X, ALU.add)\
                   .then_inc(chosen_done, 1)
            if top_softmax:
                dve.tensor_tensor(weight[:, :, :], top[:, :, 0:K], top[:, :, 0:1].broadcast_to([P, B, K]), ALU.subtract)\
                   .then_inc(max_done, 1)
                dve.wait_ge(e_done, 1)
                source = weight[:, :, :]
            else:
                source = top[:, :, 0:K]
            if top_softmax or renorm:
                dve.tensor_reduce(red[:, :], source, AX.X, ALU.add)
                dve.drain()
                if renorm:
                    dve.tensor_scalar(red[:, :], red[:, :], 1e-9, None, ALU.add)
                    dve.drain()
                dve.reciprocal(red[:, :], red[:, :])
                dve.drain()
                dve.tensor_tensor(weight[:, :, :], source, red[:, :].unsqueeze(2).broadcast_to([P, B, K]), ALU.mult)
            if rms:
                dve.wait_ge(gate_e, 1)
                dve.tensor_scalar(gate_f[:, :], gate_f[:, :], 1.0, None, ALU.add)
                dve.drain()
                dve.reciprocal(gate_f[:, :], gate_f[:, :])
            dve.wait_ge(place_put, 1)
            if capacity:
                dve.tensor_copy(place[:, :, :], ps_p[:, 0:B * E].rearrange("p (t e) -> p t e", t=B))
            else:
                dve.wait_ge(counted, 1)
                dve.tensor_scalar(tiles[:, :], ps_l[:, 0:E], 127.0, 1.0 / P, ALU.add, ALU.mult)
                dve.drain()
                dve.tensor_scalar(tiles[:, :], tiles[:, :], 1.0 / 256 - 0.5, MAGIC, ALU.add, ALU.add)
                dve.drain()
                dve.tensor_scalar(tiles[:, :], tiles[:, :], MAGIC, None, ALU.subtract)
                dve.drain()
                dve.tensor_tensor_scan(ends[:, :], ones_e[:, :], tiles[:, :], 0.0, ALU.mult, ALU.add)
                dve.drain()
                dve.tensor_tensor(base[:, :], ends[:, :], tiles[:, :], ALU.subtract)
                dve.tensor_tensor(past[:, :, :], tile_no[:, :].unsqueeze(2).broadcast_to([P, NT, E]),
                                  ends[:, :].unsqueeze(1).broadcast_to([P, NT, E]), ALU.is_ge)
                dve.drain()
                dve.tensor_scalar(base[:, :], base[:, :], float(P), None, ALU.mult)
                dve.tensor_reduce(owner[:, :], past[:, :, :], AX.X, ALU.add)
                dve.drain()
                dve.tensor_scalar(owner_i[:, :], owner[:, :], float(E - 1), None, ALU.min).then_inc(owner_done, 1)
                dve.tensor_tensor(place[:, :, :], ps_p[:, 0:B * E].rearrange("p (t e) -> p t e", t=B),
                                  base[:, :].unsqueeze(1).broadcast_to([P, B, E]), ALU.add)
            dve.drain()
            for k in range(K):
                dve.tensor_tensor(onehot[:, :, k, :], onehot[:, :, k, :], place[:, :, :], ALU.mult)
            dve.drain()
            dve.tensor_reduce(spot[:, :, :], onehot[:, :, :, :], AX.X, ALU.add)
            dve.drain()
            if capacity:
                dve.tensor_scalar(flag[:, :, :], spot[:, :, :], float(capacity), None, ALU.is_lt)
                dve.tensor_scalar(spot2[:, :, :], spot[:, :, :], float(capacity - 1), None, ALU.min)
                dve.drain()
                dve.tensor_tensor(weight[:, :, :], top[:, :, 0:K], flag[:, :, :], ALU.mult)
                dve.scalar_tensor_tensor(out=spot2[:, :, :], in0=topf[:, :, 0:K], scalar=float(capacity),
                                         in1=spot2[:, :, :], op0=ALU.mult, op1=ALU.add)
                dve.drain()
                dve.tensor_scalar(flag[:, :, :], flag[:, :, :], -float(2 * T * K), float(2 * T * K), ALU.mult, ALU.add)
                dve.tensor_copy(from_slot[:, :, :], spot2[:, :, :]).then_inc(from_done, 1)
                dve.drain()
                dve.tensor_tensor(to_slot[:, :, :], spot2[:, :, :], flag[:, :, :], ALU.add).then_inc(to_done, 1)
            else:
                dve.tensor_copy(to_slot[:, :, :], spot[:, :, :]).then_inc(to_done, 1)
                dve.tensor_copy(from_slot[:, :, :], spot[:, :, :]).then_inc(from_done, 1)

            def shared_mul(q, f):
                n, m = q * FS + f, chunk_rows(f)
                dve.wait_ge(s_silu, n + 1)
                if n - q % 2 >= 2 * FS and f == 0:
                    dve.wait_ge(sd_put, (q - 1) * 4)
                dve.tensor_tensor(s_hT[q % 2][0:m, f, :], ps_u[n % 2][0:m, :], s_act[n % 2][0:m, :], ALU.mult)\
                   .then_inc(s_mul, 1)

            def shared_add(q):
                for i in range(4):
                    t = 4 * q + i
                    dve.wait_ge(sd_put, t + 1)
                    if rms:
                        dve.scalar_tensor_tensor(out=core.xt(t), in0=ps_l[:, 0:D], scalar=gate_f[:, t:t + 1],
                                                 in1=core.xt(t), op0=ALU.mult, op1=ALU.add).then_inc(sd_done, 1)
                    else:
                        dve.tensor_tensor(core.xt(t), core.xt(t), ps_l[:, 0:D], ALU.add).then_inc(sd_done, 1)

            def shared_half(half, meanwhile):
                for i in range(2 * FS):
                    q, f = 2 * half + i // FS, i % FS
                    shared_mul(q, f)
                    if f == min(1, FS - 1) and q % 2:
                        shared_add(q - 1)
                    meanwhile(i)
                shared_add(2 * half + 1)

            if shared:
                shared_half(0, lambda i: None)

            def mul(j, u):
                dve.wait_ge(e_silu, j + 1)
                if after(j, 2):
                    dve.wait_ge(h_turned, j - 1)
                dve.tensor_tensor(h_sb[u][:, :], ps_g[u][:, FE:2 * FE], act_sb[u][:, :], ALU.mult).then_inc(e_mul, 1)

            def copy_y(j, r):
                dve.wait_ge(yd_put, j + 1)
                if after(j, RING):
                    dve.wait_ge(y_out[r], (j - r) * (16 // RING))
                dve.tensor_copy(y_sb[r][:, :], ps_l[:, 0:D]).then_inc(y_copied, 1)

            def expert_tile(j, r):
                if ahead(j, 1, NT):
                    mul(j + 1, (r + 1) % 2)
                if after(j, 1):
                    copy_y(j - 1, (r - 1) % RING)

            mul(0, 0)
            over_ring(dve, expert_tile, NT, RING)
            copy_y(NT - 1, (NT - 1) % RING)

            def add_results(t):
                dve.wait_ge(got_in[t % 2], got_before + (t // 2 + 1) * 16 * K)
                for k in range(K):
                    last = dve.scalar_tensor_tensor(out=core.xt(t), in0=got[t % 2][:, k, :], scalar=weight[:, t, k:k + 1],
                                                    in1=core.xt(t), op0=ALU.mult, op1=ALU.add)
                    if k < K - 1:
                        dve.drain()
                last.then_inc(added, 1)
                dve.drain()
                if not (shared and t >= 12):
                    row_stats(dve, core, t, six)

            so_far = 0

            def some_results(i):
                nonlocal so_far
                until = min((i + 1) * 4 // 3, 12 if i >= FS + min(1, FS - 1) else 8)
                for t in range(so_far, until):
                    add_results(t)
                so_far = max(so_far, until)

            if shared:
                shared_half(1, some_results)
            for t in range(so_far, B):
                add_results(t)
            if shared:
                for t in range(12, B):
                    dve.drain()
                    row_stats(dve, core, t, six)

        @block.scalar
        def _(act):
            if rms:
                def squares_of(t, u):
                    act.wait_ge(ln_done, t + 1)
                    act.activation(square[:, :], rows[:, bass.ds(t, 1), :].rearrange("p a d -> p (a d)"), ACT.Square,
                                   accum_out=squares[:, bass.ds(t, 1)]).then_inc(sq_done, 1)
                    act.drain()

                over_tiles(act, squares_of)

            def tile(t, u):
                act.wait_ge(row_done, t + 1)
                act.activation(rows[:, bass.ds(t, 1), :].rearrange("p a d -> p (a d)"), row1[u][:, :], ACT.Copy)\
                    .then_inc(row_kept, 1)
                act.wait_ge(xT_put, t + 1)
                if after(t, 2):
                    act.wait_ge(l_put, t - 1)
                if shared:
                    act.activation(xT[:, :, bass.ds(t * P, P)], ps_x[u][:, :].rearrange("p (c t) -> p c t", c=KC), ACT.Copy)
                act.activation(xT1[u][:, :, :], ps_x[u][:, :].rearrange("p (c t) -> p c t", c=KC), ACT.Copy)\
                    .then_inc(xT_done, 1)

            over_tiles(act, tile)
            act.wait_ge(max_done, 1)
            if top_softmax:
                act.activation(weight[:, :, :], weight[:, :, :], ACT.Exp).then_inc(e_done, 1)
            else:
                act.activation(prob[:, :, :], prob[:, :, :], ACT.Exp).then_inc(e_done, 1)
            if rms:
                act.activation(gate_f[:, :], logit[:, :, E], ACT.Exp, scale=-1.0).then_inc(gate_e, 1)

            def shared_half(half):
                for q in (2 * half, 2 * half + 1):
                    for f in range(FS):
                        n, m = q * FS + f, chunk_rows(f)
                        act.wait_ge(sg_put, n + 1)
                        if n >= 2:
                            act.wait_ge(s_mul, n - 1)
                        act.activation(s_act[n % 2][0:m, :], ps_g[n % 2][0:m, :], ACT.Silu).then_inc(s_silu, 1)

            if shared:
                shared_half(0)

            def copy_in(j, u):
                act.wait_ge(in_turned, j + 1)
                if after(j, 2):
                    act.wait_ge(gu_put, j - 1)
                act.activation(xinT[u][:, :, :].rearrange("p c t -> p (c t)"), ps_x[u][:, :], ACT.Copy)\
                    .then_inc(in_copied, 1)

            def silu(j, u):
                act.wait_ge(gu_put, j + 1)
                if after(j, 2):
                    act.wait_ge(e_mul, j - 1)
                act.activation(act_sb[u][:, :], ps_g[u][:, 0:FE], ACT.Silu).then_inc(e_silu, 1)

            def copy_h(j, u):
                act.wait_ge(h_turned, j + 1)
                if after(j, 2):
                    act.wait_ge(yd_put, j - 1)
                act.activation(hT_sb[u][:, :, :].rearrange("p c t -> p (c t)"), ps_u[u][0:FCH, 0:NJ * P], ACT.Copy)\
                    .then_inc(h_copied, 1)

            def expert_tile(j, r):
                if ahead(j, 1, NT):
                    silu(j + 1, (r + 1) % 2)
                copy_h(j, r % 2)
                if ahead(j, 2, NT):
                    copy_in(j + 2, r % 2)

            copy_in(0, 0)
            copy_in(1, 1)
            silu(0, 0)
            over_ring(act, expert_tile, NT, RING)
            if shared:
                shared_half(1)

        @block.tensor
        def _(pe):
            def turn_row(t, u):
                pe.wait_ge(row_done, t + 1)
                if after(t, 2):
                    pe.wait_ge(xT_done, t - 1)
                for c in range(KC):
                    last = pe.transpose(ps_x[u][:, c * P:c * P + P], row1[u][:, c * P:c * P + P], core.ident[:, :])
                last.then_inc(xT_put, 1)

            def route(t, u):
                pe.wait_ge(xT_done, t + 1)
                if after(t, 1):
                    pe.wait_ge(l_done, t)
                for c in range(KC):
                    last = pe.matmul(ps_l[:, 0:NL], xT1[u][:, c, :], router[:, c, :], start=(c == 0), stop=(c == KC - 1))
                last.then_inc(l_put, 1)

            def tile(t, u):
                if ahead(t, 1):
                    turn_row(t + 1, 1 - u)
                route(t, u)

            pe.wait_ge(w_in, 16 * n_loads)
            turn_row(0, 0)
            over_tiles(pe, tile)

            pe.wait_ge(const_done, 4 if capacity else 6)
            pe.wait_ge(chosen_done, 1)
            flat = chosen[:, :, :].rearrange("p t e -> p (t e)")
            for d in range(B):
                last = pe.matmul(ps_p[:, 0:B * E], onesb[:, :] if d else before[:, :], flat[:, (B - d) * E:(2 * B - d) * E],
                                 start=(d == 0), stop=(d == B - 1))
            last.then_inc(place_put, 1)
            if not capacity:
                pe.wait_ge(l_done, B)
                for t in range(B):
                    last = pe.matmul(ps_l[:, 0:E], onesb[:, :], chosen[:, B + t, :], start=(t == 0), stop=(t == B - 1))
                last.then_inc(counted, 1)

            def shared_gu(q, f):
                n, m = q * FS + f, chunk_rows(f)
                if n >= 2:
                    pe.wait_ge(s_mul, n - 1)
                for ps, w in ((ps_g, sw_g), (ps_u, sw_u)):
                    for c in range(KC):
                        last = pe.matmul(ps[n % 2][0:m, :], w[:, c, f * P:f * P + m], xT[:, c, q * W4:q * W4 + W4],
                                         start=(c == 0), stop=(c == KC - 1))
                last.then_inc(sg_put, 1)

            def shared_down(q):
                pe.wait_ge(s_mul, (q + 1) * FS)
                for i in range(4):
                    t = 4 * q + i
                    if t:
                        pe.wait_ge(sd_done, t)
                    elif not capacity:
                        pe.wait_ge(owner_done, 1)
                    for f in range(FS):
                        m = chunk_rows(f)
                        last = pe.matmul(ps_l[:, 0:D], s_hT[q % 2][0:m, f, i * P:i * P + P], sw_d[0:m, f, :],
                                         start=(f == 0), stop=(f == FS - 1))
                    last.then_inc(sd_put, 1)

            def shared_half(half):
                for q in (2 * half, 2 * half + 1):
                    for f in range(FS):
                        shared_gu(q, f)
                        if f == min(1, FS - 1) and q % 2:
                            shared_down(q - 1)
                shared_down(2 * half + 1)

            if shared:
                pe.wait_ge(sw_in, 16 * (3 + (shared % P > 0)))
                shared_half(0)
                pe.wait_ge(sd_done, B // 2)
                pe.wait_ge(s_mul, 2 * FS)

            def turn_in(j, r):
                pe.wait_ge(xin_in[r], (j - r) * (16 // RING) + 16)
                if after(j, 2):
                    pe.wait_ge(in_copied, j - 1)
                for c in range(KC):
                    last = pe.transpose(ps_x[r % 2][:, c * P:c * P + P], xin[r][:, c * P:c * P + P], core.ident[:, :])
                last.then_inc(in_turned, 1)

            def gate_up(j, r):
                if not capacity:
                    e = pe.value_load(owner_i[0:1, bass.ds(j, 1)], min_val=0, max_val=E - 1)
                if capacity:
                    pe.wait_ge(gu_in[r], (j - r) * (16 // RING) + 16)
                pe.wait_ge(in_copied, j + 1)
                if after(j, 2):
                    pe.wait_ge(e_mul, j - 1)
                for c in range(KC):
                    w = w_gu[r][:, c, :] if capacity else w_gu_all[:, bass.ds(e * (KC * 2 * FE) + c * 2 * FE, 2 * FE)]
                    last = pe.matmul(ps_g[r % 2][:, 0:2 * FE], xinT[r % 2][:, c, :], w, start=(c == 0), stop=(c == KC - 1))
                last.then_inc(gu_put, 1)

            def turn_h(j, u):
                pe.wait_ge(e_mul, j + 1)
                if after(j, 2):
                    pe.wait_ge(h_copied, j - 1)
                for c in range(NJ):
                    last = pe.transpose(ps_u[u][0:FCH, c * P:c * P + P], h_sb[u][:, c * FCH:(c + 1) * FCH], core.ident[:, :])
                last.then_inc(h_turned, 1)

            def down(j, r):
                if not capacity:
                    e = pe.value_load(owner_i[0:1, bass.ds(j, 1)], min_val=0, max_val=E - 1)
                if capacity:
                    pe.wait_ge(down_in[r], (j - r) * (16 // RING) + 16)
                pe.wait_ge(h_copied, j + 1)
                if after(j, 1):
                    pe.wait_ge(y_copied, j)
                for c in range(NJ):
                    w = w_d[r][:, c, :] if capacity else w_d_all[:, bass.ds(e * (NJ * D) + c * D, D)]
                    last = pe.matmul(ps_l[:, 0:D], hT_sb[r % 2][:, c, :], w, start=(c == 0), stop=(c == NJ - 1))
                last.then_inc(yd_put, 1)

            def expert_tile(j, r):
                if ahead(j, 1, NT):
                    gate_up(j + 1, (r + 1) % RING)
                turn_h(j, r % 2)
                if ahead(j, 2, NT):
                    turn_in(j + 2, (r + 2) % RING)
                if after(j, 1):
                    down(j - 1, (r - 1) % RING)

            if not capacity:
                pe.wait_ge(owner_done, 1)
                pe.wait_ge(ew_in, 32)
            turn_in(0, 0)
            turn_in(1, 1)
            gate_up(0, 0)
            over_ring(pe, expert_tile, NT, RING)
            down(NT - 1, (NT - 1) % RING)
            if shared:
                pe.wait_ge(e_mul, NT)
                pe.wait_ge(h_copied, NT)
                pe.wait_ge(y_copied, NT)
                shared_half(1)


STAGES = {
    "L1F": lambda core: moe_ffn(core, "l1f", 32, 4, 176, capacity=128, shared=704, rms=True),
    "L2F": lambda core: moe_ffn(core, "l2f", 16, 2, 128, shared=128, biased=True, renorm=True),
    "L3F": lambda core: moe_ffn(core, "l3f", 8, 2, 256, top_softmax=True),
    "L1A": lambda core: gated_long_conv(core, "l1a"),
    "L3A": lambda core: channel_attention(core, "l3a"),
    "L0F": lambda core: hadamard_ffn(core, "l0f"),
    "L0A": lambda core: gqa_attention(core, "l0a", dict(
        wq="l0a_wq", wk="l0a_wk", wv="l0a_wv", wo="l0a_wo", bq="l0a_bq", bk="l0a_bk", bv="l0a_bv", bo="l0a_bo"), True),
    "L2A": lambda core: gqa_attention(core, "l2a", dict(
        wq="l2a_wq", wk="l2a_wk", wv="l2a_wv", wo="l2a_wo", bo="l2a_bo"), False),
}


def build(nc, dram, out, stages):
    with ExitStack() as ctx:
        core = Core(nc, ctx, dram)
        load_inputs(core)
        for s in stages:
            STAGES[s](core)
        store_output(core, out)


def lay_out(np, a):
    def chunks(w, p=P):
        w = np.asarray(w)
        return w.reshape(w.shape[0] // p, p, -1).transpose(1, 0, 2)

    def per_head(w):
        w = np.asarray(w)
        return np.repeat(w.reshape(G, 1, HD, -1), R, axis=1).reshape(H * HD, -1)

    ctx = np.asarray(a["ctx_2048"])
    o = {
        "x": a["x"],
        "ctx": ctx,
        "ctxT": ctx.reshape(B, P, KC, P).transpose(0, 3, 2, 1),
        "pair_mask": np.asarray(a["mask_SxS2_bc0"]),
        "pad_mask": np.asarray(a["mask_BxS2_bk0"]).reshape(T),
    }
    for s, n in (("l0a", "L0_xattn_"), ("l2a", "L2_xattn_")):
        o[f"{s}_wq"] = chunks(np.asarray(a[n + "Wq"]).T)
        o[f"{s}_wk"] = chunks(per_head(a[n + "Wk"]).T)
        o[f"{s}_wv"] = chunks(np.asarray(a[n + "Wv"]).T)
    o["l0f_wg"] = chunks(np.asarray(a["L0_ffn_w_gate"]).T).reshape(P, -1)
    o["l0f_wu"] = chunks(np.asarray(a["L0_ffn_w_up"]).T).reshape(P, -1)
    o["l0f_wd"] = chunks(np.asarray(a["L0_ffn_w_down"]).T).reshape(P, -1)
    had = np.ones((1, 1), np.float32)
    while had.shape[0] < P:
        had = np.block([[had, had], [had, -had]])
    o["had"] = had
    o["skip"] = a["fside_S2_0"]
    k = np.concatenate([np.zeros((16, P), np.float32), np.asarray(a["L1_xattn_k"])], axis=1)
    o["l1a_taps"] = np.stack([k[:, P - m:P - m + D] for m in range(P)])
    def experts(g, u, d, fch):
        g, u, d = (np.asarray(w) for w in (g, u, d))
        gu = np.concatenate([g, u], axis=2)
        return (gu.reshape(len(gu), KC, P, -1).transpose(0, 2, 1, 3),
                d.reshape(len(d), -1, fch, D).transpose(0, 2, 1, 3))

    o["l1f_w_gu"], o["l1f_w_d"] = experts(a["L1_ffn_w_gate"], a["L1_ffn_w_up"], a["L1_ffn_w_down"], 88)
    o["l2f_w_gu"], o["l2f_w_d"] = experts(a["L2_ffn_Wg"], a["L2_ffn_Wu"], a["L2_ffn_Wd"], 128)
    o["l3f_w_gu"], o["l3f_w_d"] = experts(a["L3_ffn_wi_0"], a["L3_ffn_wi_1"], a["L3_ffn_wo"], 128)
    o["l1f_router"] = chunks(np.concatenate([np.asarray(a["L1_ffn_w_router"]), np.asarray(a["L1_ffn_w_shared_gate"])], axis=1))
    o["l2f_router"] = chunks(np.asarray(a["L2_ffn_Wr"]).T)
    o["l3f_router"] = chunks(a["L3_ffn_gate_kernel"])
    o["l1f_norm_w"] = a["L1_ffn_w_norm"]
    o["l2f_bias"] = a["L2_ffn_bias"]
    for s, n in (("l1f", ("L1_ffn_sw_gate", "L1_ffn_sw_up", "L1_ffn_sw_down")),
                 ("l2f", ("L2_ffn_sWg", "L2_ffn_sWu", "L2_ffn_sWd"))):
        o[f"{s}_sw_g"], o[f"{s}_sw_u"], o[f"{s}_sw_d"] = chunks(a[n[0]]), chunks(a[n[1]]), a[n[2]]
    o["l0a_wo"] = chunks(np.asarray(a["L0_xattn_Wo"]).T)
    o["l2a_wo"] = chunks(np.asarray(a["L2_xattn_Wfc"]).T)
    o["l0a_bq"] = np.asarray(a["L0_xattn_bq"]).reshape(KC, P).T
    o["l0a_bk"] = per_head(a["L0_xattn_bk"]).reshape(KC, P).T
    o["l0a_bv"] = a["L0_xattn_bv"]
    o["l0a_bo"] = a["L0_xattn_bo"]
    o["l2a_bo"] = a["L2_xattn_bfc"]
    return {k: np.ascontiguousarray(v) for k, v in o.items()}


ALL = ("L0A", "L0F", "L1A", "L1F", "L2A", "L2F", "L3A", "L3F")


def kernel(**inputs):
    import numpy as np
    import concourse.bacc as bacc
    from concourse.bass_utils import run_bass_kernel_spmd

    arrays = {f"in_{k}": v for k, v in lay_out(np, inputs).items()}
    nc = bacc.Bacc("TRN2", target_bir_lowering=False, num_devices=1)
    dram = {k[3:]: nc.dram_tensor(k, v.shape, mybir.dt.from_np(v.dtype), kind="ExternalInput").ap()
            for k, v in arrays.items()}
    out = nc.dram_tensor("out_x", (B, P, D), F32, kind="ExternalOutput").ap()
    build(nc, dram, out, ALL)
    return run_bass_kernel_spmd(nc, [arrays], core_ids=[0]).results[0]["out_x"]
```

```python
from contextlib import ExitStack, contextmanager

import numpy as np

import concourse.bass as bass
from concourse import mybir

P = 128
B = 16
T = B * P
D = 256
KC = D // P
H, HD = 32, 8
G = 8
R = H // G
W4 = 4 * P
LN_EPS = 1e-5
NEG = -1e30

F32 = mybir.dt.float32
BF16 = mybir.dt.bfloat16
U8 = mybir.dt.uint8
U32 = mybir.dt.uint32
I32 = mybir.dt.int32
ALU = mybir.AluOpType
ACT = mybir.ActivationFunctionType
AX = mybir.AxisListType


def over_batches(eng, body):
    body(0, 0, True, False)
    with eng.Fori(0, (B - 2) // 2) as i:
        body(i * 2 + 1, 1, False, False)
        body(i * 2 + 2, 0, False, False)
    body(B - 1, 1, False, True)


def over_tiles(eng, body, n=B):
    body(0, 0)
    body(1, 1)
    with eng.Fori(1, n // 2 - 1) as i:
        body(i * 2, 0)
        body(i * 2 + 1, 1)
    body(n - 2, 0)
    body(n - 1, 1)


def over_long_pipe(eng, body, n=B):
    body(0, 0)
    body(1, 1)
    with eng.Fori(1, n // 2 - 2) as i:
        body(i * 2, 0)
        body(i * 2 + 1, 1)
    for t in range(n - 4, n):
        body(t, t % 2)


def over_ring(eng, body, n, ring, lead=1):
    for j in range(lead * ring):
        body(j, j % ring)
    with eng.Fori(lead, n // ring - 1) as i:
        for r in range(ring):
            body(i * ring + r, r)
    for r in range(ring):
        body(n - ring + r, r)


def after(t, n):
    return not isinstance(t, int) or t >= n


def ahead(t, n, total=B):
    return not isinstance(t, int) or t + n < total


EPS_Q = float(np.float32(1e-5))
FF = 1024
NF = FF // P
MAX_SLOTS = 48 * P
RING = 4
X_PART = 2


class Core:

    def __init__(self, nc, ctx, dram):
        self.nc, self.ctx, self.dram = nc, ctx, dram
        self.x = self.sb("x_rows", [P, B * D])
        self.stats = self.sb("ln_mean_var", [P, B, 2])
        self.var_eps = self.sb("ln_var_eps", [P, B])
        self.minus_half = self.sb("minus_half", [P, B])
        self.six = self.sb("ln_partial", [P, B, 6])
        self.rstd = self.sb("ln_rstd", [P, B])
        self.rows = nc.dram_tensor("expert_rows", (T, D), F32, kind="Internal").ap()
        self.results = nc.dram_tensor("expert_results", (MAX_SLOTS, D), F32, kind="Internal").ap()
        self.ffn_in = [ctx.enter_context(nc.semaphore(f"ffn_in{n}")) for n in range(3)]
        self.had_in = ctx.enter_context(nc.semaphore("had_in"))
        self.xin_in = [ctx.enter_context(nc.semaphore(f"xin_in{r}")) for r in range(RING)]
        self.gathered = [ctx.enter_context(nc.semaphore(f"gathered{r}")) for r in range(RING)]
        self.n_xin_in, self.n_gathered = 0, 0
        self.conv_in = ctx.enter_context(nc.semaphore("conv_in"))
        self.x_out = ctx.enter_context(nc.semaphore("x_out"))
        self.ident = self.sb("ident", [P, P])
        self.identb = self.sb("identb", [P, P], BF16)
        self.head_of_row = self.sb("head_of_row", [P, R])
        self.chan_head_of_row = self.sb("chan_head_of_row", [P, P // 16])
        self.group_of_row = self.sb("group_of_row", [P, 4])
        self.early = ctx.enter_context(ExitStack())
        self.ffn_raw = [self.sb(f"ffn_raw{n}", [P, KC * FF], F32, self.early) for n in range(3)]
        self.had = self.sb("had_matrix", [P, P], F32, self.early)
        self.ctxT = self.sb("ctxT_all", [P, KC, B, P], F32, self.early)
        self.taps = self.sb("taps", [P, 16, D], F32, self.early)
        self.skip = self.sb("skip", [P, 1], F32, self.early)
        self.same_block = self.sb("same_block", [P, P], F32, self.early)

    def sb(self, name, shape, dt=F32, ctx=None):
        return (ctx or self.ctx).enter_context(self.nc.sbuf_tensor(name, shape, dt))

    def ps(self, name, shape, dt=F32, ctx=None):
        return (ctx or self.ctx).enter_context(self.nc.psum_tensor(name, shape, dt))

    def sem(self, name, ctx):
        s = ctx.enter_context(self.nc.semaphore(name))
        self.stage_sems.append(s.num)
        return s

    @contextmanager
    def stage(self):
        self.stage_sems = []
        with ExitStack() as st:
            yield st
        nums = sorted(self.stage_sems)
        first = nums[0]
        for n, following in zip(nums, nums[1:] + [-1]):
            if following != n + 1:
                self.nc.gpsimd.sem_clear(range(first, n + 1))
                first = following

    def xt(self, b):
        return self.x[:, bass.ds(b * D, D)]


def row_stats(dve, core, b):
    dve.bn_stats(core.six[:, bass.ds(b, 1), :].rearrange("p a s -> p (a s)"), core.xt(b))


def finish_stats(dve, core):
    dve.drain()
    for b in range(B):
        dve.bn_aggr(core.stats[:, b, :], core.six[:, b, :])
    dve.drain()
    dve.tensor_scalar(core.var_eps[:, :], core.stats[:, :, 1], LN_EPS, None, ALU.add)


def all_rstd(pool, core, done):
    pool.tensor_tensor(core.rstd[:, :], core.var_eps[:, :], core.minus_half[:, :], ALU.pow).then_inc(done, 1)


def normalise(dve, core, out, b):
    return dve.tensor_scalar(out, core.xt(b), core.stats[:, bass.ds(b, 1), 0], core.rstd[:, bass.ds(b, 1)],
                             ALU.subtract, ALU.mult)


def load_inputs(core):
    nc, dram = core.nc, core.dram
    with core.stage() as st:
        const = core.sem("load_const", st)
        x_in = [core.sem(f"x_in{n}", st) for n in range(B // X_PART)]
        band = core.sb("load_band", [P, 4, R], F32, st)
        block = st.enter_context(nc.Block())

        @block.sync
        def _(sp):
            for n in range(B // X_PART):
                tiles = slice(n * X_PART, (n + 1) * X_PART)
                sp.dma_start(core.x[:, n * X_PART * D:(n + 1) * X_PART * D].rearrange("p (b d) -> p b d", b=X_PART),
                             dram["x"][tiles].rearrange("b p d -> p b d")).then_inc(x_in[n], 16)

        @block.gpsimd
        def _(pool):
            pool.memset(core.minus_half[:, :], -0.5).then_inc(const, 1)
            pool.memset(core.ident[:, :], 0.0).then_inc(const, 1)
            pool.memset(core.identb[:, :], 0.0).then_inc(const, 1)
            pool.wait_ge(const, 3)
            for m in (core.ident, core.identb):
                pool.affine_select(out=m[:, :], in_=m[:, :], compare_op=ALU.not_equal, fill=1.0, base=0,
                                   pattern=[[-1, P]], channel_multiplier=1).then_inc(const, 1)
            pool.memset(band[:, :, :], 1.0).then_inc(const, 1)
            pool.wait_ge(const, 6)
            pool.affine_select(out=band[:, :, :].rearrange("p g r -> p (g r)"), in_=band[:, :, :].rearrange("p g r -> p (g r)"), compare_op=ALU.is_ge, fill=0.0, base=0,
                               pattern=[[-HD, P // HD]], channel_multiplier=1).then_inc(const, 1)
            pool.wait_ge(const, 7)
            pool.affine_select(out=band[:, :, :].rearrange("p g r -> p (g r)"), in_=band[:, :, :].rearrange("p g r -> p (g r)"), compare_op=ALU.is_ge, fill=0.0, base=HD - 1,
                               pattern=[[HD, P // HD]], channel_multiplier=-1).then_inc(const, 1)

        @block.vector
        def _(dve):
            dve.wait_ge(const, 8)
            dve.tensor_reduce(core.head_of_row[:, :], band[:, :, :].rearrange("p g r -> p r g"), AX.X, ALU.add)
            dve.tensor_reduce(core.group_of_row[:, :], band[:, :, :], AX.X, ALU.add)
            dve.tensor_reduce(core.chan_head_of_row[:, :], band[:, :, :].rearrange("p g (h two) -> p (g h) two", two=2),
                              AX.X, ALU.add)
            dve.tensor_copy(core.same_block[:, :].rearrange("p (h i) -> p h i", i=HD),
                            band[:, :, :].rearrange("p g r -> p (g r)").unsqueeze(2).broadcast_to([P, P // HD, HD]))
            dve.drain()
            for rows, width in ((core.group_of_row, HD), (core.chan_head_of_row, 16)):
                dve.tensor_scalar(rows[:, :], rows[:, :], width ** -0.5, None, ALU.mult)
            for b in range(B):
                if b % X_PART == 0:
                    dve.wait_ge(x_in[b // X_PART], 16)
                row_stats(dve, core, b)
            finish_stats(dve, core)


def load_ahead(core, sp):
    for n, key in enumerate(("l0f_wg", "l0f_wu", "l0f_wd")):
        sp.dma_start(core.ffn_raw[n][:, :], core.dram[key]).then_inc(core.ffn_in[n], 16)
    sp.dma_start(core.had[:, :], core.dram["had"]).then_inc(core.had_in, 16)
    for c in range(KC):
        sp.dma_start(core.ctxT[:, c, :, :], core.dram["ctxT"][:, :, c, :].rearrange("b p t -> p b t"))\
          .then_inc(core.conv_in, 16)
    sp.dma_start(core.taps[:, :, :], core.dram["l1a_taps"]).then_inc(core.conv_in, 16)
    sp.dma_start(core.skip[:, :], core.dram["skip"].rearrange("(p a) -> p a", a=1)).then_inc(core.conv_in, 16)



def gqa_attention(core, name, w, masked):
    nc, dram = core.nc, core.dram
    with core.stage() as st:
        def sb(n, shape, dt=F32):
            return core.sb(f"{name}_{n}", shape, dt, st)

        def sem(n):
            return core.sem(f"{name}_{n}", st)

        wq, wk, wo = (sb(n, [P, KC, D]) for n in ("wq", "wk", "wo"))
        wv = sb("wv", [P, KC, G * HD])
        bias_o = sb("bias_o", [P, D])
        if masked:
            bias_q, bias_k = sb("bias_q", [P, KC]), sb("bias_k", [P, KC])
            bias_v = sb("bias_v", [P, G * HD])
            pad_u8, pair_u8 = sb("pad_u8", [P, T], U8), sb("pair_u8", [P, P], U8)
            pad_neg, pair_neg = sb("pad_neg", [P, T], BF16), sb("pair_neg", [P, P], BF16)
            mask = [sb(f"mask{u}", [P, P], BF16) for u in range(2)]
        ctxT = [sb(f"ctxT{u}", [P, KC, P]) for u in range(2)]
        xn = sb("xn", [P, D])
        xnT = sb("xnT", [P, KC, P])
        qT, kT = sb("qT", [P, KC, P]), sb("kT", [P, KC, P])
        q_group = [sb(f"q_group{u}", [P, G, P]) for u in range(2)]
        k_head = [sb(f"k_head{u}", [P, KC, R, P]) for u in range(2)]
        v_aug = [sb(f"v_aug{u}", [P, G, 32]) for u in range(2)]
        neg_max = sb("neg_max", [P, 4, R])
        prob = [sb(f"prob{s}", [P, W4]) for s in range(4)]
        probT = [sb(f"probT{s}", [P, W4]) for s in range(2)]
        o_sb = [sb(f"o_sb{c}", [P, W4]) for c in range(2)]
        recip = sb("recip", [P, R, 4])
        attn = sb("attn", [P, D])
        attnT = sb("attnT", [P, KC, P])
        y_sb = sb("y_sb", [P, D])
        ps_s = [core.ps(f"{name}_ps_s{s}", [P, W4], F32, st) for s in range(2)]
        ps_t = [core.ps(f"{name}_ps_t{s}", [P, W4], F32, st) for s in range(2)]
        ps_o = [core.ps(f"{name}_ps_o{c}", [P, W4], F32, st) for c in range(2)]
        ps_in = core.ps(f"{name}_ps_in", [P, W4], F32, st)
        ps_out = core.ps(f"{name}_ps_out", [P, W4], F32, st)

        (w_in, const_done, mask_done, xn_done, xnT_put, xnT_done, qk_put, qk_done, q_spread,
         k_spread, v_put, v_done, s_put, max_done, exp_done, t_put, t_done, pv_put, o_done, r_put, attn_done,
         a_put, a_done, y_put, x_done) = (sem(n) for n in (
             "w_in", "const_done", "mask_done", "xn_done", "xnT_put", "xnT_done", "qk_put",
             "qk_done", "q_spread", "k_spread", "v_put", "v_done", "s_put", "max_done", "exp_done", "t_put", "t_done",
             "pv_put", "o_done", "r_put", "attn_done", "a_put", "a_done", "y_put", "x_done"))
        ctx_in = [sem(f"ctx_in{u}") for u in range(2)]
        n_loads = 10 if masked else 5
        rstd_done = sem("rstd_done")
        block = st.enter_context(nc.Block())

        @block.sync
        def _(sp):
            def load_ctx(b, u):
                sp.dma_start(ctxT[u][:, :, :], dram["ctxT"][bass.ds(b, 1)].rearrange("a p c t -> p (a c) t"))\
                  .then_inc(ctx_in[u], 16)

            load_ctx(0, 0)
            for buf, key in ((wq, "wq"), (wk, "wk"), (wv, "wv"), (wo, "wo")):
                sp.dma_start(buf[:, :, :], dram[w[key]]).then_inc(w_in, 16)
            sp.dma_start(bias_o[:, :], dram[w["bo"]].partition_broadcast(P)).then_inc(w_in, 16)
            if masked:
                sp.dma_start(bias_q[:, :], dram[w["bq"]]).then_inc(w_in, 16)
                sp.dma_start(bias_k[:, :], dram[w["bk"]]).then_inc(w_in, 16)
                sp.dma_start(bias_v[:, :], dram[w["bv"]].partition_broadcast(P)).then_inc(w_in, 16)
                sp.dma_start(pair_u8[:, :], dram["pair_mask"]).then_inc(w_in, 16)
                sp.dma_start(pad_u8[:, :], dram["pad_mask"].partition_broadcast(P)).then_inc(w_in, 16)
            load_ctx(1, 1)
            if masked:
                load_ahead(core, sp)
            with sp.Fori(0, (B - 2) // 2) as i:
                for u in range(2):
                    sp.wait_ge(v_put, i * 2 + u + 1)
                    load_ctx(i * 2 + u + 2, u)

        @block.gpsimd
        def _(pool):
            all_rstd(pool, core, rstd_done)
            for u in range(2):
                pool.memset(q_group[u][:, :, :], 0.0).then_inc(const_done, 1)
                pool.memset(v_aug[u][:, :, :], 0.0).then_inc(const_done, 1)
            pool.wait_ge(const_done, 4)
            for u in range(2):
                pool.memset(v_aug[u][:, :, HD], 1.0).then_inc(const_done, 1)
            if masked:
                pool.wait_ge(w_in, 16 * n_loads)
                pool.tensor_scalar(pair_neg[:, :], pair_u8[:, :], NEG, 1.0, ALU.mult, ALU.mult)
                pool.tensor_scalar(pad_neg[:, :], pad_u8[:, :], NEG, 1.0, ALU.mult, ALU.mult)
                pool.drain()

            def spread(b, u):
                if masked:
                    pool.wait_ge(s_put, b * G - G) if not (isinstance(b, int) and b < 2) else None
                    pool.tensor_tensor(mask[u][:, :], pair_neg[:, :], pad_neg[:, bass.ds(b * P, P)], ALU.add)\
                        .then_inc(mask_done, 1)
                elif not (isinstance(b, int) and b < 2):
                    pool.wait_ge(s_put, b * G - G)
                pool.wait_ge(qk_done, b * 4 + 4)
                for c in range(KC):
                    pool.tensor_tensor(k_head[u][:, c, :, :],
                                       kT[:, c:c + 1, :].broadcast_to([P, R, P]),
                                       core.head_of_row[:, :].unsqueeze(2).broadcast_to([P, R, P]), ALU.mult)\
                        .then_inc(k_spread, 1)
                for c in range(KC):
                    pool.tensor_tensor(q_group[u][:, 4 * c:4 * c + 4, :],
                                       qT[:, c:c + 1, :].broadcast_to([P, 4, P]),
                                       core.group_of_row[:, :].unsqueeze(2).broadcast_to([P, 4, P]), ALU.mult)\
                        .then_inc(q_spread, 1)

            spread(0, 0)
            spread(1, 1)
            with pool.Fori(0, (B - 2) // 2) as i:
                for u in range(2):
                    spread(i * 2 + u + 2, u)

        @block.vector
        def _(dve):
            def xn_of(b):
                if not (isinstance(b, int) and b == 0):
                    dve.wait_ge(xnT_put, b)
                normalise(dve, core, xn[:, :], b).then_inc(xn_done, 1)

            def values(b, u):
                dve.wait_ge(v_put, b + 1)
                psv = ps_in[:, 0:G * HD].rearrange("p (g d) -> p g d", g=G)
                if not (isinstance(b, int) and b < 2):
                    dve.wait_ge(pv_put, b * G - G)
                if masked:
                    dve.tensor_tensor(v_aug[u][:, :, 0:HD], psv, bias_v[:, :].rearrange("p (g d) -> p g d", g=G),
                                      ALU.add).then_inc(v_done, 1)
                else:
                    dve.tensor_copy(v_aug[u][:, :, 0:HD], psv).then_inc(v_done, 1)

            def find_max(b, g):
                dve.wait_ge(s_put, b * G + g + 1)
                if after(b, 1) or g >= 4:
                    dve.wait_ge(exp_done, b * G + g - 3)
                dve.tensor_reduce(neg_max[:, g % 4, :], ps_s[g % 2][:, :].rearrange("p (r k) -> p r k", r=R),
                                  AX.X, ALU.max, negate=True).then_inc(max_done, 1)

            def copy_probT(b, g):
                dve.wait_ge(t_put, b * G + g + 1)
                if after(b, 1) or g >= 2:
                    dve.wait_ge(pv_put, b * G + g - 1)
                dve.tensor_copy(probT[g % 2][:, :], ps_t[g % 2][:, :]).then_inc(t_done, 1)

            def weigh(b, c):
                dve.wait_ge(r_put, b * 2 + c + 1)
                o = ps_out[:, :].rearrange("p (r g e) -> p r g e", r=R, g=4)
                dve.reciprocal(recip[:, :, :], o[:, :, :, HD])
                dve.drain()
                if c == 0 and not (isinstance(b, int) and b == 0):
                    dve.wait_ge(a_put, b)
                dve.tensor_tensor(attn[:, c * P:c * P + P].rearrange("p (g r d) -> p r g d", g=4, r=R),
                                  o[:, :, :, 0:HD], recip[:, :, :].unsqueeze(3).broadcast_to([P, R, 4, HD]),
                                  ALU.mult).then_inc(attn_done, 1)

            def add_to_x(b):
                dve.wait_ge(y_put, b + 1)
                dve.tensor_tensor(y_sb[:, :], ps_out[:, D:2 * D], bias_o[:, :], ALU.add)
                dve.drain()
                dve.tensor_tensor(core.xt(b), core.xt(b), y_sb[:, :], ALU.add).then_inc(x_done, 1)
                dve.drain()
                row_stats(dve, core, b)

            def batch(b, u, first, last):
                for g in range(G):
                    find_max(b, g)
                    if g >= 2:
                        copy_probT(b, g - 2)
                    elif not first:
                        copy_probT(b - 1, G - 2 + g)
                    if g == 0 and not last:
                        xn_of(b + 1)
                    if g == 1 and not first:
                        weigh(b - 1, 0)
                    if g == 4 and not first:
                        weigh(b - 1, 1)
                    if g == 5 and not last:
                        values(b + 1, 1 - u)
                    if g == 7 and not first:
                        add_to_x(b - 1)

            dve.wait_ge(rstd_done, 1)
            xn_of(0)
            dve.wait_ge(w_in, 16 * n_loads)
            dve.wait_ge(const_done, 6)
            values(0, 0)
            over_batches(dve, batch)
            copy_probT(B - 1, G - 2)
            copy_probT(B - 1, G - 1)
            weigh(B - 1, 0)
            weigh(B - 1, 1)
            add_to_x(B - 1)
            finish_stats(dve, core)

        @block.scalar
        def _(act):
            def copy_xnT(b):
                act.wait_ge(xnT_put, b + 1)
                if not (isinstance(b, int) and b == 0):
                    act.wait_ge(qk_put, b)
                act.activation(xnT[:, :, :].rearrange("p c t -> p (c t)"), ps_in[:, 0:D], ACT.Copy)\
                    .then_inc(xnT_done, 1)

            def copy_qk(b):
                act.wait_ge(qk_put, b + 1)
                if not (isinstance(b, int) and b == 0):
                    act.wait_ge(q_spread, b * 2)
                    act.wait_ge(k_spread, b * 2)
                for n, (to, bias) in enumerate(((qT, "q"), (kT, "k"))):
                    for c in range(KC):
                        src = ps_in[:, (n * KC + c) * P:(n * KC + c + 1) * P]
                        if masked:
                            act.activation(to[:, c, :], src, ACT.Identity,
                                           bias=(bias_q if bias == "q" else bias_k)[:, c:c + 1]).then_inc(qk_done, 1)
                        else:
                            act.activation(to[:, c, :], src, ACT.Copy).then_inc(qk_done, 1)

            def exps(b, g):
                act.wait_ge(max_done, b * G + g + 1)
                if after(b, 1) or g >= 4:
                    act.wait_ge(t_put, b * G + g - 3)
                for r in range(R):
                    last = act.activation(prob[g % 4][:, r * P:r * P + P], ps_s[g % 2][:, r * P:r * P + P], ACT.Exp,
                                          bias=neg_max[:, g % 4, r:r + 1])
                last.then_inc(exp_done, 1)

            def copy_o(b, c):
                act.wait_ge(pv_put, b * G + 4 * c + 4)
                if not (isinstance(b, int) and b == 0):
                    act.wait_ge(r_put, b * 2 + c - 1)
                act.activation(o_sb[c][:, :], ps_o[c][:, :], ACT.Copy).then_inc(o_done, 1)

            def copy_attnT(b):
                act.wait_ge(a_put, b + 1)
                if not (isinstance(b, int) and b == 0):
                    act.wait_ge(y_put, b)
                act.activation(attnT[:, :, :].rearrange("p c t -> p (c t)"), ps_out[:, 0:D], ACT.Copy)\
                    .then_inc(a_done, 1)

            def batch(b, u, first, last):
                for g in range(G):
                    exps(b, g)
                    if g == 1 and not last:
                        copy_xnT(b + 1)
                    if g == 2 and not first:
                        copy_o(b - 1, 1)
                    if g == 3 and not last:
                        copy_qk(b + 1)
                    if g == 5 and not first:
                        copy_attnT(b - 1)
                    if g == 6:
                        copy_o(b, 0)

            copy_xnT(0)
            act.wait_ge(w_in, 16 * n_loads)
            copy_qk(0)
            over_batches(act, batch)
            copy_o(B - 1, 1)
            copy_attnT(B - 1)

        @block.tensor
        def _(pe):
            def turn_xn(b):
                pe.wait_ge(xn_done, b + 1)
                if not (isinstance(b, int) and b == 0):
                    pe.wait_ge(v_done, b)
                for c in range(KC):
                    last = pe.transpose(ps_in[:, c * P:c * P + P], xn[:, c * P:c * P + P], core.ident[:, :])
                last.then_inc(xnT_put, 1)

            def project_qk(b, u):
                pe.wait_ge(xnT_done, b + 1)
                pe.wait_ge(ctx_in[u], (b - u) * 8 + 16)
                for n, (wt, src) in enumerate(((wq, xnT), (wk, ctxT[u]))):
                    for m in range(KC):
                        for c in range(KC):
                            last = pe.matmul(ps_in[:, (n * KC + m) * P:(n * KC + m + 1) * P],
                                             wt[:, c, m * P:m * P + P], src[:, c, :], start=(c == 0), stop=(c == KC - 1))
                last.then_inc(qk_put, 1)

            def project_v(b, u):
                pe.wait_ge(qk_done, b * 4 + 4)
                for c in range(KC):
                    last = pe.matmul(ps_in[:, 0:G * HD], ctxT[u][:, c, :], wv[:, c, :], start=(c == 0), stop=(c == KC - 1))
                last.then_inc(v_put, 1)

            def scores(b, g, u):
                if g == 0:
                    if masked:
                        pe.wait_ge(mask_done, b + 1)
                if g % 4 == 0:
                    pe.wait_ge(k_spread, b * 2 + g // 4 + 1)
                    pe.wait_ge(q_spread, b * 2 + g // 4 + 1)
                if not (isinstance(b, int) and b == 0 and g < 2):
                    pe.wait_ge(exp_done, b * G + g - 1)
                mm = pe.matmul(ps_s[g % 2][:, :], q_group[u][:, g, :],
                               k_head[u][:, g // 4, :, :].rearrange("p r k -> p (r k)"), start=True, stop=not masked)
                if masked:
                    mm = pe.matmul(ps_s[g % 2][:, :].rearrange("p (r k) -> p r k", r=R), core.identb[:, :],
                                   mask[u][:, :].unsqueeze(1).broadcast_to([P, R, P]), start=False, stop=True)
                mm.then_inc(s_put, 1)

            def turn_prob(b, g):
                pe.wait_ge(exp_done, b * G + g + 1)
                if not (isinstance(b, int) and b == 0 and g < 2):
                    pe.wait_ge(t_done, b * G + g - 1)
                for r in range(R):
                    last = pe.transpose(ps_t[g % 2][:, r * P:r * P + P], prob[g % 4][:, r * P:r * P + P], core.ident[:, :])
                last.then_inc(t_put, 1)

            def weigh_values(b, g, u):
                pe.wait_ge(t_done, b * G + g + 1)
                if g == 0:
                    pe.wait_ge(v_done, b + 1)
                if g % 4 == 0 and not (isinstance(b, int) and b == 0):
                    pe.wait_ge(o_done, b * 2 + g // 4 - 1)
                rows = slice(32 * (g % 4), 32 * (g % 4) + 32)
                pe.matmul(ps_o[g // 4][rows, :], v_aug[u][:, g, :], probT[g % 2][:, :], start=True, stop=True)\
                  .then_inc(pv_put, 1)

            def turn_o(b, c):
                pe.wait_ge(o_done, b * 2 + c + 1)
                if c == 1:
                    pe.wait_ge(attn_done, b * 2 + 1)
                elif not (isinstance(b, int) and b == 0):
                    pe.wait_ge(x_done, b)
                for r in range(R):
                    last = pe.transpose(ps_out[:, r * P:r * P + P], o_sb[c][:, r * P:r * P + P], core.ident[:, :])
                last.then_inc(r_put, 1)

            def turn_attn(b):
                pe.wait_ge(attn_done, b * 2 + 2)
                for c in range(KC):
                    last = pe.transpose(ps_out[:, c * P:c * P + P], attn[:, c * P:c * P + P], core.ident[:, :])
                last.then_inc(a_put, 1)

            def project_out(b):
                pe.wait_ge(a_done, b + 1)
                for c in range(KC):
                    last = pe.matmul(ps_out[:, D:2 * D], attnT[:, c, :], wo[:, c, :], start=(c == 0), stop=(c == KC - 1))
                last.then_inc(y_put, 1)

            def batch(b, u, first, last):
                for g in range(G):
                    scores(b, g, u)
                    if g >= 2:
                        turn_prob(b, g - 2)
                    elif not first:
                        turn_prob(b - 1, G - 2 + g)
                    if g >= 3:
                        weigh_values(b, g - 3, u)
                    elif not first:
                        weigh_values(b - 1, G - 3 + g, 1 - u)
                    if g == 0 and not first:
                        turn_o(b - 1, 0)
                    if g == 1 and not last:
                        turn_xn(b + 1)
                    if g == 3 and not first:
                        turn_o(b - 1, 1)
                    if g == 3 and not last:
                        project_qk(b + 1, 1 - u)
                    if g == 4 and not last:
                        project_v(b + 1, 1 - u)
                    if g == 5 and not first:
                        turn_attn(b - 1)
                    if g == 6 and not first:
                        project_out(b - 1)

            turn_xn(0)
            pe.wait_ge(w_in, 16 * n_loads)
            project_qk(0, 0)
            project_v(0, 0)
            over_batches(pe, batch)
            turn_prob(B - 1, G - 2)
            turn_prob(B - 1, G - 1)
            for g in range(G - 3, G):
                weigh_values(B - 1, g, 1)
            turn_o(B - 1, 0)
            turn_o(B - 1, 1)
            turn_attn(B - 1)
            project_out(B - 1)


def channel_attention(core, name):
    nc, dram = core.nc, core.dram
    CH, CD = 8, 16
    with core.stage() as st:
        def sb(n, shape, dt=F32):
            return core.sb(f"{name}_{n}", shape, dt, st)

        def sem(n):
            return core.sem(f"{name}_{n}", st)

        ctxT = [sb(f"ctxT{u}", [P, KC, P]) for u in range(2)]
        ctx = [sb(f"ctx{u}", [P, D]) for u in range(2)]
        xn = [sb(f"xn{u}", [P, D]) for u in range(2)]
        q_head = [sb(f"q_head{u}", [P, CH, D]) for u in range(2)]
        v_aug = [sb(f"v_aug{u}", [P, KC, CH, 32]) for u in range(2)]
        neg_max = sb("neg_max", [P, 4, 2])
        prob = [sb(f"prob{s}", [P, W4]) for s in range(4)]
        probT = [sb(f"probT{s}", [P, W4]) for s in range(2)]
        o_sb = [sb(f"o_sb{c}", [P, D]) for c in range(2)]
        recip = sb("recip", [P, 2, 4])
        attn = sb("attn", [P, 2, P])
        ps_s = [core.ps(f"{name}_ps_s{s}", [P, W4], F32, st) for s in range(2)]
        ps_t = [core.ps(f"{name}_ps_t{s}", [P, W4], F32, st) for s in range(2)]
        ps_o = [core.ps(f"{name}_ps_o{c}", [P, D], F32, st) for c in range(2)]
        ps_out = core.ps(f"{name}_ps_out", [P, W4], F32, st)
        (const_done, xn_done, q_spread, v_done, s_put, max_done, exp_done, t_put, t_done, pv_put, o_done,
         r_put, attn_done, a_put, x_done) = (sem(n) for n in (
             "const_done", "xn_done", "q_spread", "v_done", "s_put", "max_done", "exp_done", "t_put",
             "t_done", "pv_put", "o_done", "r_put", "attn_done", "a_put", "x_done"))
        ctx_in = [sem(f"ctx_in{u}") for u in range(2)]
        rstd_done = sem("rstd_done")
        block = st.enter_context(nc.Block())

        def ctx_loaded(eng, b, u):
            eng.wait_ge(ctx_in[u], (b - u) * 16 + 32)

        @block.sync
        def _(sp):
            def load_ctx(b, u):
                sp.dma_start(ctxT[u][:, :, :], dram["ctxT"][bass.ds(b, 1)].rearrange("a p c t -> p (a c) t"))\
                  .then_inc(ctx_in[u], 16)
                sp.dma_start(ctx[u][:, :], dram["ctx"][bass.ds(b, 1)].rearrange("a p d -> p (a d)"))\
                  .then_inc(ctx_in[u], 16)

            load_ctx(0, 0)
            load_ctx(1, 1)
            with sp.Fori(0, (B - 2) // 2) as i:
                for u in range(2):
                    sp.wait_ge(s_put, i * (2 * CH) + (u + 1) * CH)
                    sp.wait_ge(v_done, i * 2 + u + 1)
                    load_ctx(i * 2 + u + 2, u)

        @block.gpsimd
        def _(pool):
            all_rstd(pool, core, rstd_done)
            for u in range(2):
                pool.memset(v_aug[u][:, :, :, :], 0.0).then_inc(const_done, 1)
            pool.wait_ge(const_done, 2)
            for u in range(2):
                pool.memset(v_aug[u][:, :, :, CD], 1.0).then_inc(const_done, 1)

            def spread(b, u):
                pool.wait_ge(xn_done, b + 1)
                if after(b, 2):
                    pool.wait_ge(s_put, b * CH - CH)
                pool.tensor_tensor(q_head[u][:, :, :], xn[u][:, :].unsqueeze(1).broadcast_to([P, CH, D]),
                                   core.chan_head_of_row[:, :].unsqueeze(2).broadcast_to([P, CH, D]), ALU.mult)\
                    .then_inc(q_spread, 1)

            over_tiles(pool, spread)

        @block.vector
        def _(dve):
            def xn_of(b, u):
                if after(b, 2):
                    dve.wait_ge(q_spread, b - 1)
                normalise(dve, core, xn[u][:, :], b).then_inc(xn_done, 1)

            def find_max(b, g):
                dve.wait_ge(s_put, b * CH + g + 1)
                if after(b, 1) or g >= 4:
                    dve.wait_ge(exp_done, b * CH + g - 3)
                dve.tensor_reduce(neg_max[:, g % 4, :], ps_s[g % 2][:, :].rearrange("p (r k) -> p r k", r=2),
                                  AX.X, ALU.max, negate=True).then_inc(max_done, 1)

            def weigh(b, c):
                dve.wait_ge(r_put, b * 2 + c + 1)
                o = ps_out[:, c * D:c * D + D].rearrange("p (m h e) -> p m h e", m=2, h=4)
                dve.reciprocal(recip[:, :, :], o[:, :, :, CD])
                dve.drain()
                if c == 0 and after(b, 1):
                    dve.wait_ge(a_put, b)
                dve.tensor_tensor(attn[:, :, c * 64:c * 64 + 64].rearrange("p m (h d) -> p m h d", h=4),
                                  o[:, :, :, 0:CD], recip[:, :, :].unsqueeze(3).broadcast_to([P, 2, 4, CD]),
                                  ALU.mult).then_inc(attn_done, 1)

            def add_to_x(b):
                dve.wait_ge(a_put, b + 1)
                dve.tensor_tensor(core.xt(b), core.xt(b), ps_out[:, 0:D], ALU.add).then_inc(x_done, 1)
                dve.drain()
                row_stats(dve, core, b)

            def batch(b, u):
                for g in range(CH):
                    find_max(b, g)
                    if g == 0 and ahead(b, 1):
                        xn_of(b + 1, 1 - u)
                    if g == 1 and after(b, 1):
                        weigh(b - 1, 0)
                    if g == 4 and after(b, 1):
                        weigh(b - 1, 1)
                    if g == 6 and after(b, 1):
                        add_to_x(b - 1)

            dve.wait_ge(rstd_done, 1)
            xn_of(0, 0)
            over_tiles(dve, batch)
            weigh(B - 1, 0)
            weigh(B - 1, 1)
            add_to_x(B - 1)
            finish_stats(dve, core)

        @block.scalar
        def _(act):
            def values(b, u):
                ctx_loaded(act, b, u)
                if after(b, 2):
                    act.wait_ge(pv_put, b * CH - CH)
                act.activation(v_aug[u][:, :, :, 0:CD], ctxT[u][:, :, :].rearrange("p c (h d) -> p c h d", h=CH),
                               ACT.Copy).then_inc(v_done, 1)

            def exps(b, g):
                act.wait_ge(max_done, b * CH + g + 1)
                if after(b, 1) or g >= 4:
                    act.wait_ge(t_put, b * CH + g - 3)
                for m in range(2):
                    last = act.activation(prob[g % 4][:, m * D:m * D + D], ps_s[g % 2][:, m * D:m * D + D], ACT.Exp,
                                          bias=neg_max[:, g % 4, m:m + 1])
                last.then_inc(exp_done, 1)

            def copy_probT(b, g):
                act.wait_ge(t_put, b * CH + g + 1)
                if after(b, 1) or g >= 2:
                    act.wait_ge(pv_put, b * CH + g - 1)
                act.activation(probT[g % 2][:, :], ps_t[g % 2][:, :], ACT.Copy).then_inc(t_done, 1)

            def copy_o(b, c):
                act.wait_ge(pv_put, b * CH + 4 * c + 4)
                if after(b, 1):
                    act.wait_ge(r_put, b * 2 + c - 1)
                act.activation(o_sb[c][:, :], ps_o[c][:, :], ACT.Copy).then_inc(o_done, 1)

            def batch(b, u):
                for g in range(CH):
                    exps(b, g)
                    if g >= 2:
                        copy_probT(b, g - 2)
                    elif after(b, 1):
                        copy_probT(b - 1, CH - 2 + g)
                    if g == 2 and after(b, 1):
                        copy_o(b - 1, 1)
                    if g == 4 and ahead(b, 1):
                        values(b + 1, 1 - u)
                    if g == 6:
                        copy_o(b, 0)

            act.wait_ge(const_done, 4)
            values(0, 0)
            over_tiles(act, batch)
            copy_probT(B - 1, CH - 2)
            copy_probT(B - 1, CH - 1)
            copy_o(B - 1, 1)

        @block.tensor
        def _(pe):
            def scores(b, g, u):
                if g == 0:
                    ctx_loaded(pe, b, u)
                    pe.wait_ge(q_spread, b + 1)
                if after(b, 1) or g >= 2:
                    pe.wait_ge(exp_done, b * CH + g - 1)
                for m in range(2):
                    last = pe.matmul(ps_s[g % 2][:, m * D:m * D + D], q_head[u][:, g, m * P:m * P + P], ctx[u][:, :],
                                     start=True, stop=True)
                last.then_inc(s_put, 1)

            def turn_prob(b, g):
                pe.wait_ge(exp_done, b * CH + g + 1)
                if after(b, 1) or g >= 2:
                    pe.wait_ge(t_done, b * CH + g - 1)
                for m in range(2):
                    for n in range(2):
                        last = pe.transpose(ps_t[g % 2][:, n * D + m * P:n * D + m * P + P],
                                            prob[g % 4][:, m * D + n * P:m * D + n * P + P], core.ident[:, :])
                last.then_inc(t_put, 1)

            def weigh_values(b, g, u):
                pe.wait_ge(t_done, b * CH + g + 1)
                if g == 0:
                    pe.wait_ge(v_done, b + 1)
                if g % 4 == 0 and after(b, 1):
                    pe.wait_ge(o_done, b * 2 + g // 4 - 1)
                rows = slice(32 * (g % 4), 32 * (g % 4) + 32)
                for n in range(2):
                    last = pe.matmul(ps_o[g // 4][rows, :], v_aug[u][:, n, g, :], probT[g % 2][:, n * D:n * D + D],
                                     start=(n == 0), stop=(n == 1))
                last.then_inc(pv_put, 1)

            def turn_o(b, c):
                pe.wait_ge(o_done, b * 2 + c + 1)
                if c == 1:
                    pe.wait_ge(attn_done, b * 2 + 1)
                elif after(b, 1):
                    pe.wait_ge(x_done, b)
                for m in range(2):
                    last = pe.transpose(ps_out[:, c * D + m * P:c * D + m * P + P], o_sb[c][:, m * P:m * P + P],
                                        core.ident[:, :])
                last.then_inc(r_put, 1)

            def turn_attn(b):
                pe.wait_ge(attn_done, b * 2 + 2)
                for m in range(2):
                    last = pe.transpose(ps_out[:, m * P:m * P + P], attn[:, m, :], core.ident[:, :])
                last.then_inc(a_put, 1)

            def batch(b, u):
                for g in range(CH):
                    scores(b, g, u)
                    if g >= 2:
                        turn_prob(b, g - 2)
                    elif after(b, 1):
                        turn_prob(b - 1, CH - 2 + g)
                    if g >= 3:
                        weigh_values(b, g - 3, u)
                    elif after(b, 1):
                        weigh_values(b - 1, CH - 3 + g, 1 - u)
                    if g == 0 and after(b, 1):
                        turn_o(b - 1, 0)
                    if g == 3 and after(b, 1):
                        turn_o(b - 1, 1)
                    if g == 5 and after(b, 1):
                        turn_attn(b - 1)

            over_tiles(pe, batch)
            turn_prob(B - 1, CH - 2)
            turn_prob(B - 1, CH - 1)
            for g in range(CH - 3, CH):
                weigh_values(B - 1, g, 1)
            turn_o(B - 1, 0)
            turn_o(B - 1, 1)
            turn_attn(B - 1)


MAGIC = 1.5 * 2.0 ** 23


def hadamard_ffn(core, name):
    nc, dram = core.nc, core.dram
    with core.stage() as st:
        def sb(n, shape, dt=F32):
            return core.sb(f"{name}_{n}", shape, dt, st)

        def sem(n):
            return core.sem(f"{name}_{n}", st)

        raw = core.ffn_raw
        wq = [sb(f"w_int{n}", [P, KC * FF], BF16) for n in range(3)]
        gate_w, up_w = (wq[n][:, :].rearrange("p (c f) -> p c f", c=KC) for n in range(2))
        down_w = wq[2][:, :].rearrange("p (c f) -> p c f", c=NF)
        had = core.had
        ones = sb("ones", [P, P])
        magic = sb("magic", [P, 1])
        w_sum, w_mean, w_scale = sb("w_sum", [P, 3]), sb("w_mean", [P, 3]), sb("w_scale", [P, 3])
        xn = sb("xn", [P, D])
        xq = sb("xq", [P, D], BF16)
        xqT = [sb(f"xqT{u}", [P, KC, P], BF16) for u in range(2)]
        a_max, a_rec = sb("a_max", [P, 1]), sb("a_rec", [P, 1])
        deq = [sb(f"deq{u}", [P, 2]) for u in range(2)]
        b_max, b_rec = sb("b_max", [P, 1]), sb("b_rec", [P, 1])
        b_deq = [sb(f"b_deq{u}", [P, 1]) for u in range(2)]
        gate = sb("gate", [P, FF])
        prod = [sb(f"prod{u}", [P, FF]) for u in range(2)]
        fly = sb("fly", [P, FF])
        mixed = [sb(f"mixed{u}", [P, FF]) for u in range(2)]
        mixedT = sb("mixedT", [P, FF])
        rounded = sb("rounded", [P, FF])
        hq = sb("hq", [P, FF], BF16)
        hqT = sb("hqT", [P, FF], BF16)
        ps_g = core.ps(f"{name}_ps_g", [P, FF], F32, st)
        ps_u = core.ps(f"{name}_ps_u", [P, FF], F32, st)
        ps_t = core.ps(f"{name}_ps_t", [P, W4], F32, st)
        ps_q = core.ps(f"{name}_ps_q", [P, W4], F32, st)
        ps_f = core.ps(f"{name}_ps_f", [P, FF], F32, st)
        ps_hqT = ps_q[:, 0:D].bitcast(BF16)
        ps_xqT = ps_q[:, 0:P].bitcast(BF16)
        ps_y = ps_q[:, D:2 * D]
        (const_done, sum_done, mean_put, scale_done, w_rounded, w_done, xq_done, deq_done, xqT_put, xqT_done, gate_put,
         up_put, silu_done, prod_done, mixed_done, mixT_put, mixT_done, had_put, b_scale, round_done, hq_done,
         hqT_put, hqT_done, y_put, x_done) = (sem(n) for n in (
             "const_done", "sum_done", "mean_put", "scale_done", "w_rounded", "w_done", "xq_done", "deq_done", "xqT_put",
             "xqT_done", "gate_put", "up_put", "silu_done", "prod_done", "mixed_done", "mixT_put", "mixT_done",
             "had_put", "b_scale", "round_done", "hq_done", "hqT_put", "hqT_done", "y_put", "x_done"))
        rstd_done = sem("rstd_done")
        block = st.enter_context(nc.Block())

        @block.gpsimd
        def _(pool):
            all_rstd(pool, core, rstd_done)
            pool.memset(ones[:, :], 1.0).then_inc(const_done, 1)
            pool.memset(magic[:, :], MAGIC).then_inc(const_done, 1)

            def butterflies(t, u):
                pool.wait_ge(prod_done, t + 1)
                if after(t, 2):
                    pool.wait_ge(mixT_put, t - 1)
                for n, (src, dst) in enumerate(((prod[u], fly), (fly, prod[u]), (prod[u], mixed[u]))):
                    v, o = (m[:, :].rearrange("p (a two c) -> p a two c", two=2, c=P << n) for m in (src, dst))
                    if n:
                        pool.drain()
                    pool.tensor_tensor(o[:, :, 0, :], v[:, :, 0, :], v[:, :, 1, :], ALU.add)
                    last = pool.tensor_tensor(o[:, :, 1, :], v[:, :, 0, :], v[:, :, 1, :], ALU.subtract)
                last.then_inc(mixed_done, 1)

            over_tiles(pool, butterflies)

        @block.vector
        def _(dve):
            def scale_weights():
                for n in range(3):
                    dve.wait_ge(core.ffn_in[n], 16)
                    dve.tensor_reduce(w_sum[:, n:n + 1], raw[n][:, :], AX.X, ALU.add, apply_absolute_value=True)\
                       .then_inc(sum_done, 1)
                dve.wait_ge(mean_put, 1)
                dve.tensor_scalar(w_mean[:, :], ps_f[:, 0:3], 1.0 / (D * FF), 1e-5, ALU.mult, ALU.max)
                dve.drain()
                dve.reciprocal(w_scale[:, :], w_mean[:, :]).then_inc(scale_done, 1)

            def clip_weights():
                for n in range(3):
                    dve.wait_ge(w_rounded, n + 1)
                    dve.tensor_scalar(raw[n][:, :], raw[n][:, :], MAGIC + 1.0, MAGIC - 1.0, ALU.min, ALU.max)
                    dve.drain()
                    dve.tensor_scalar(wq[n][:, :], raw[n][:, :], MAGIC, None, ALU.subtract).then_inc(w_done, 1)

            def quantise_x(t, u):
                dve.drain()
                normalise(dve, core, xn[:, :], t)
                dve.drain()
                dve.tensor_reduce(a_max[:, :], xn[:, :], AX.X, ALU.max, apply_absolute_value=True)
                dve.drain()
                dve.tensor_scalar(a_max[:, :], a_max[:, :], 1e-5, 1.0 / 128, ALU.max, ALU.mult)
                dve.drain()
                dve.reciprocal(a_rec[:, :], a_max[:, :])
                if after(t, 2):
                    dve.wait_ge(silu_done, t - 1)
                dve.tensor_scalar(deq[u][:, :], w_mean[:, 0:2], a_max[:, :], None, ALU.mult)\
                   .then_inc(deq_done, 1)
                dve.drain()
                dve.tensor_scalar(xn[:, :], xn[:, :], a_rec[:, :], MAGIC, ALU.mult, ALU.add)
                dve.drain()
                if after(t, 1):
                    dve.wait_ge(xqT_put, t)
                dve.tensor_scalar(xq[:, :], xn[:, :], MAGIC, 127.0, ALU.subtract, ALU.min).then_inc(xq_done, 1)

            def gate_times_up(t, u):
                dve.wait_ge(silu_done, t + 1)
                dve.wait_ge(up_put, t + 1)
                if after(t, 2):
                    dve.wait_ge(mixed_done, t - 1)
                dve.scalar_tensor_tensor(out=prod[u][:, :], in0=ps_u[:, :], scalar=deq[u][:, 1:2], in1=gate[:, :],
                                         op0=ALU.mult, op1=ALU.mult).then_inc(prod_done, 1)

            def scale_h(t, u):
                dve.wait_ge(had_put, t + 1)
                dve.tensor_reduce(b_max[:, :], ps_f[:, :], AX.X, ALU.max, apply_absolute_value=True)
                dve.drain()
                dve.tensor_scalar(b_max[:, :], b_max[:, :], 32 * EPS_Q, 1.0 / 128, ALU.max, ALU.mult)
                dve.drain()
                dve.tensor_scalar(b_deq[u][:, :], b_max[:, :], w_mean[:, 2:3], 1.0 / 32, ALU.mult, ALU.mult)
                dve.reciprocal(b_rec[:, :], b_max[:, :]).then_inc(b_scale, 1)

            def quantise_h(t):
                dve.wait_ge(round_done, t + 1)
                if after(t, 1):
                    dve.wait_ge(hqT_put, 2 * t)
                dve.tensor_scalar(hq[:, :], rounded[:, :], MAGIC, 127.0, ALU.subtract, ALU.min).then_inc(hq_done, 1)

            def add_to_x(t, u):
                dve.wait_ge(y_put, t + 1)
                dve.scalar_tensor_tensor(out=core.xt(t), in0=ps_y, scalar=b_deq[u][:, :], in1=core.xt(t),
                                         op0=ALU.mult, op1=ALU.add).then_inc(x_done, 1)
                dve.drain()
                row_stats(dve, core, t)

            def tile(t, u):
                if ahead(t, 3):
                    quantise_x(t + 3, 1 - u)
                if ahead(t, 2):
                    gate_times_up(t + 2, u)
                scale_h(t, u)
                if after(t, 1):
                    add_to_x(t - 1, 1 - u)
                quantise_h(t)

            scale_weights()
            dve.wait_ge(rstd_done, 1)
            quantise_x(0, 0)
            quantise_x(1, 1)
            clip_weights()
            gate_times_up(0, 0)
            quantise_x(2, 0)
            gate_times_up(1, 1)
            over_long_pipe(dve, tile)
            add_to_x(B - 1, 1)
            finish_stats(dve, core)

        @block.scalar
        def _(act):
            def copy_xqT(t, u):
                act.wait_ge(xqT_put, t + 1)
                if after(t, 2):
                    act.wait_ge(up_put, t - 1)
                act.activation(xqT[u][:, :, :].rearrange("p c t -> p (c t)"), ps_xqT, ACT.Copy).then_inc(xqT_done, 1)

            def silu(t, u):
                act.wait_ge(gate_put, t + 1)
                act.wait_ge(deq_done, t + 1)
                if after(t, 1):
                    act.wait_ge(prod_done, t)
                act.activation(gate[:, :], ps_g[:, :], ACT.Silu, scale=deq[u][:, 0:1]).then_inc(silu_done, 1)

            def copy_mixedT(t, half):
                act.wait_ge(mixT_put, 2 * t + half + 1)
                if after(t, 1) and half == 0:
                    act.wait_ge(had_put, t)
                act.activation(mixedT[:, half * W4:half * W4 + W4], ps_t[:, :], ACT.Copy).then_inc(mixT_done, 1)

            def round_h(t):
                act.wait_ge(b_scale, t + 1)
                if after(t, 1):
                    act.wait_ge(hq_done, t)
                act.activation(rounded[:, :], ps_f[:, :], ACT.Identity, bias=magic[:, :], scale=b_rec[:, :])\
                    .then_inc(round_done, 1)

            def copy_hqT(t, half):
                act.wait_ge(hqT_put, 2 * t + half + 1)
                if after(t, 1) and half == 0:
                    act.wait_ge(y_put, t)
                act.activation(hqT[:, half * W4:half * W4 + W4], ps_hqT, ACT.Copy).then_inc(hqT_done, 1)

            def tile(t, u):
                copy_mixedT(t, 0)
                copy_mixedT(t, 1)
                if ahead(t, 2):
                    silu(t + 2, u)
                if after(t, 1):
                    copy_hqT(t - 1, 0)
                    copy_hqT(t - 1, 1)
                if ahead(t, 3):
                    copy_xqT(t + 3, 1 - u)
                round_h(t)

            act.wait_ge(const_done, 2)
            act.wait_ge(scale_done, 1)
            for n in range(3):
                act.activation(raw[n][:, :], raw[n][:, :], ACT.Identity, bias=magic[:, :], scale=w_scale[:, n:n + 1])\
                   .then_inc(w_rounded, 1)
            copy_xqT(0, 0)
            copy_xqT(1, 1)
            silu(0, 0)
            copy_xqT(2, 0)
            silu(1, 1)
            over_long_pipe(act, tile)
            copy_hqT(B - 1, 0)
            copy_hqT(B - 1, 1)

        @block.tensor
        def _(pe):
            def turn_xq(t, u):
                pe.wait_ge(xq_done, t + 1)
                if after(t, 1):
                    pe.wait_ge(xqT_done, t)
                if after(t, 4):
                    pe.wait_ge(hqT_done, 2 * t - 6)
                for c in range(KC):
                    last = pe.transpose(ps_xqT[:, c * P:c * P + P], xq[:, c * P:c * P + P], core.identb[:, :])
                last.then_inc(xqT_put, 1)

            def gate_up(t, u, which):
                if which == 0:
                    pe.wait_ge(xqT_done, t + 1)
                for ps, w, free, put in ((ps_g, gate_w, silu_done, gate_put), (ps_u, up_w, prod_done, up_put))[which:which + 1]:
                    if after(t, 1):
                        pe.wait_ge(free, t)
                    for h in range(2):
                        for c in range(KC):
                            last = pe.matmul(ps[:, h * W4:h * W4 + W4], xqT[u][:, c, :], w[:, c, h * W4:h * W4 + W4],
                                             start=(c == 0), stop=(c == KC - 1))
                    last.then_inc(put, 1)

            def turn_mixed(t, u, half):
                if half == 0:
                    pe.wait_ge(mixed_done, t + 1)
                if half or after(t, 1):
                    pe.wait_ge(mixT_done, 2 * t + half)
                for c in range(half * NF // 2, (half + 1) * NF // 2):
                    at = (c % (NF // 2)) * P
                    last = pe.transpose(ps_t[:, at:at + P], mixed[u][:, c * P:c * P + P], core.ident[:, :])
                last.then_inc(mixT_put, 1)

            def transform(t, half):
                if half == 0:
                    pe.wait_ge(mixT_done, 2 * t + 2)
                    if after(t, 1):
                        pe.wait_ge(round_done, t)
                for c in range(half * NF // 2, (half + 1) * NF // 2):
                    last = pe.matmul(ps_f[:, c * P:c * P + P], mixedT[:, c * P:c * P + P], had[:, :], start=True, stop=True)
                if half:
                    last.then_inc(had_put, 1)

            def turn_hq(t, half):
                if half == 0:
                    pe.wait_ge(hq_done, t + 1)
                    if after(t, 1):
                        pe.wait_ge(x_done, t)
                    if ahead(t, 3):
                        pe.wait_ge(xqT_done, t + 4)
                else:
                    pe.wait_ge(hqT_done, 2 * t + 1)
                for c in range(NF // 2):
                    at = half * W4 + c * P
                    last = pe.transpose(ps_hqT[:, c * P:c * P + P], hq[:, at:at + P], core.identb[:, :])
                last.then_inc(hqT_put, 1)

            def down(t):
                pe.wait_ge(hqT_done, 2 * t + 2)
                if ahead(t, 4):
                    pe.wait_ge(xqT_done, t + 5)
                for c in range(NF):
                    last = pe.matmul(ps_y, hqT[:, c * P:c * P + P], down_w[:, c, :], start=(c == 0), stop=(c == NF - 1))
                last.then_inc(y_put, 1)

            def tile(t, u):
                for half in range(2):
                    turn_mixed(t, u, half)
                    if ahead(t, 2):
                        gate_up(t + 2, u, half)
                for half in range(2):
                    transform(t, half)
                    if after(t, 1):
                        turn_hq(t - 1, half)
                if ahead(t, 3):
                    turn_xq(t + 3, 1 - u)
                if after(t, 1):
                    down(t - 1)

            pe.wait_ge(const_done, 2)
            pe.wait_ge(core.had_in, 16)
            pe.wait_ge(sum_done, 3)
            pe.matmul(ps_f[:, 0:3], ones[:, :], w_sum[:, :], start=True, stop=True).then_inc(mean_put, 1)
            turn_xq(0, 0)
            turn_xq(1, 1)
            pe.wait_ge(w_done, 3)
            gate_up(0, 0, 0)
            gate_up(0, 0, 1)
            turn_xq(2, 0)
            gate_up(1, 1, 0)
            gate_up(1, 1, 1)
            over_long_pipe(pe, tile)
            turn_hq(B - 1, 0)
            turn_hq(B - 1, 1)
            down(B - 1)


def gated_long_conv(core, name):
    nc, dram = core.nc, core.dram
    NH, N8 = 16, 8
    COLS = B * N8 * N8
    with core.stage() as st:
        def sb(n, shape, dt=F32, c=st):
            return core.sb(f"{name}_{n}", shape, dt, c)

        def sem(n):
            return core.sem(f"{name}_{n}", st)

        ctxT, taps = core.ctxT, core.taps
        vT = sb("vT", [P, KC, B, P])
        outT = sb("outT", [P, KC, B, P])
        (xn_done, xnT_put, xnT_done, kv_done, tap_done, y_put, z_done, fold_done, gated, sum_put, skipped,
         out_put, x_done) = (sem(n) for n in (
             "xn_done", "xnT_put", "xnT_done", "kv_done", "tap_done", "y_put", "z_done", "fold_done",
             "gated", "sum_put", "skipped", "out_put", "x_done"))
        ctx_in = [sem(f"ctx_in{r}") for r in range(RING)]

        rstd_done = sem("rstd_done")

        with ExitStack() as ph:
            xn = [sb(f"xn{u}", [P, D], F32, ph) for u in range(2)]
            ctx = [sb(f"ctx{r}", [P, D], F32, ph) for r in range(RING)]
            part = [sb(f"part{u}", [P, D], F32, ph) for u in range(2)]
            ps = [core.ps(f"{name}_ps_x{u}", [P, W4], F32, ph) for u in range(2)]
            ps_sum = [core.ps(f"{name}_ps_sum{u}", [P, W4], F32, ph) for u in range(2)]
            block = ph.enter_context(nc.Block())

            @block.sync
            def _(sp):
                def load(b, r):
                    if after(b, RING):
                        sp.wait_ge(skipped, b - (RING - 1))
                    sp.dma_start(ctx[r][:, :], dram["ctx"][bass.ds(b, 1)].rearrange("a p d -> p (a d)"))\
                      .then_inc(ctx_in[r], 16)

                over_ring(sp, load, B, RING)

            @block.gpsimd
            def _(pool):
                all_rstd(pool, core, rstd_done)

            @block.vector
            def _(dve):
                dve.wait_ge(rstd_done, 1)
                dve.wait_ge(core.conv_in, 64)

                def gate(b, r):
                    u = r % 2
                    if after(b, 2):
                        dve.wait_ge(xnT_put, b - 1)
                    normalise(dve, core, xn[u][:, :], b).then_inc(xn_done, 1)
                    dve.drain()
                    dve.wait_ge(ctx_in[r], (b - r) * (16 // RING) + 16)
                    dve.scalar_tensor_tensor(out=part[u][:, :], in0=xn[u][:, :], scalar=core.skip[:, :],
                                             in1=ctx[r][:, :], op0=ALU.mult, op1=ALU.mult).then_inc(gated, 1)

                def add_skip(b, r):
                    u = r % 2
                    dve.wait_ge(sum_put, b + 1)
                    dve.tensor_tensor(part[u][:, :], ps_sum[u][:, 0:D], ctx[r][:, :], ALU.mult)
                    dve.drain()
                    dve.tensor_tensor(core.xt(b), core.xt(b), part[u][:, :], ALU.add).then_inc(skipped, 1)
                    dve.drain()

                def tile(b, r):
                    if ahead(b, 1):
                        gate(b + 1, (r + 1) % RING)
                    add_skip(b, r)

                gate(0, 0)
                over_ring(dve, tile, B, RING)

            @block.scalar
            def _(act):
                def tile(b, u):
                    act.wait_ge(xnT_put, b + 1)
                    act.activation(vT[:, :, bass.ds(b, 1), :].rearrange("p c a t -> p c (a t)"),
                                   ps[u][:, 0:D].rearrange("p (c t) -> p c t", c=KC), ACT.Copy).then_inc(xnT_done, 1)

                over_tiles(act, tile)

            @block.tensor
            def _(pe):
                def tile(b, u):
                    pe.wait_ge(xn_done, b + 1)
                    if after(b, 2):
                        pe.wait_ge(xnT_done, b - 1)
                    for c in range(KC):
                        last = pe.transpose(ps[u][:, c * P:c * P + P], xn[u][:, c * P:c * P + P], core.ident[:, :])
                    last.then_inc(xnT_put, 1)
                    pe.wait_ge(gated, b + 1)
                    if after(b, 2):
                        pe.wait_ge(skipped, b - 1)
                    pe.matmul(ps_sum[u][:, 0:D], core.same_block[:, :], part[u][:, :], start=True, stop=True)\
                      .then_inc(sum_put, 1)

                over_tiles(pe, tile)

        with ExitStack() as ph:
            kv = [sb(f"kv{u}", [P, KC, COLS], F32, ph) for u in range(2)]
            tap = [sb(f"tap{u}", [P, D], F32, ph) for u in range(2)]
            z = [sb(f"z{c}", [P, COLS], F32, ph) for c in range(2)]
            ps = [[core.ps(f"{name}_ps_y{u}{c}", [P, COLS], F32, ph) for c in range(KC)] for u in range(2)]
            block = ph.enter_context(nc.Block())

            @block.gpsimd
            def _(pool):
                pool.wait_ge(core.conv_in, 64)

                def outer(h, u):
                    for c in range(KC):
                        i_rows = vT[:, c, :, bass.ds(h * N8, N8)].unsqueeze(3).broadcast_to([P, B, N8, N8])
                        j_rows = ctxT[:, c, :, bass.ds(h * N8, N8)].unsqueeze(2).broadcast_to([P, B, N8, N8])
                        if c == 0 and after(h, 2):
                            pool.wait_ge(y_put, h * 2 - 2)
                        pool.tensor_tensor(kv[u][:, c, :].rearrange("p (b i j) -> p b i j", b=B, i=N8),
                                           i_rows, j_rows, ALU.mult).then_inc(kv_done, 1)

                over_tiles(pool, outer, NH)

            @block.scalar
            def _(act):
                act.wait_ge(core.conv_in, 64)

                def stage(h, u):
                    if after(h, 2):
                        act.wait_ge(y_put, h * 2 - 2)
                    act.activation(tap[u][:, :], taps[:, bass.ds(h, 1), :].rearrange("p a l -> p (a l)"), ACT.Copy)\
                        .then_inc(tap_done, 1)

                over_tiles(act, stage, NH)

            @block.tensor
            def _(pe):
                def conv(h, u):
                    pe.wait_ge(tap_done, h + 1)
                    for c in range(KC):
                        pe.wait_ge(kv_done, h * 2 + c + 1)
                        if after(h, 2):
                            pe.wait_ge(z_done, h * 2 - 3 + c)
                        for n in range(2):
                            cols = slice(n * W4, n * W4 + W4)
                            for m in range(c + 1):
                                last = pe.matmul(ps[u][c][:, cols], tap[u][:, (c - m) * P:(c - m) * P + P],
                                                 kv[u][:, m, cols], start=(m == 0), stop=(m == c))
                        last.then_inc(y_put, 1)

                over_tiles(pe, conv, NH)

            @block.vector
            def _(dve):
                dve.wait_ge(core.conv_in, 64)

                def gate(h, u):
                    for c in range(KC):
                        dve.wait_ge(y_put, h * 2 + c + 1)
                        x1 = ctxT[:, c, :, bass.ds(h * N8, N8)].unsqueeze(3).broadcast_to([P, B, N8, N8])
                        if after(h, 1):
                            dve.wait_ge(fold_done, h * 2 - 1 + c)
                        dve.tensor_tensor(z[c][:, :].rearrange("p (b i j) -> p b i j", b=B, i=N8),
                                          ps[u][c][:, :].rearrange("p (b i j) -> p b i j", b=B, i=N8), x1, ALU.mult)\
                           .then_inc(z_done, 1)
                    for c in range(KC):
                        dve.wait_ge(z_done, h * 2 + c + 1)
                        dve.tensor_reduce(outT[:, c, :, bass.ds(h * N8, N8)],
                                          z[c][:, :].rearrange("p (b i j) -> p b j i", b=B, i=N8), AX.X, ALU.add)\
                           .then_inc(fold_done, 1)

                over_tiles(dve, gate, NH)

        with ExitStack() as ph:
            ps = [core.ps(f"{name}_ps_o{u}", [P, W4], F32, ph) for u in range(2)]
            block = ph.enter_context(nc.Block())

            @block.vector
            def _(dve):
                for b in range(B):
                    dve.wait_ge(out_put, b + 1)
                    dve.tensor_tensor(core.xt(b), core.xt(b), ps[b % 2][:, 0:D], ALU.add).then_inc(x_done, 1)
                    dve.drain()
                    row_stats(dve, core, b)
                finish_stats(dve, core)

            @block.tensor
            def _(pe):
                for b in range(B):
                    if b >= 2:
                        pe.wait_ge(x_done, b - 1)
                    for c in range(KC):
                        last = pe.transpose(ps[b % 2][:, c * P:c * P + P], outT[:, c, b, :], core.ident[:, :])
                    last.then_inc(out_put, 1)


LAG = 6


def moe_ffn(core, name, E, K, FE, capacity=None, shared=0, rms=False, biased=False, renorm=False, top_softmax=False,
            final=False):
    nc, dram = core.nc, core.dram
    NT = E * capacity // P if capacity else T * K // P + E
    NT += NT % RING and RING - NT % RING
    FCH = FE // 2 if FE > P else FE
    NJ = FE // FCH
    NL = E + (1 if rms else 0)
    FS = -(-shared // P)
    with core.stage() as st:
        def sb(n, shape, dt=F32):
            return core.sb(f"{name}_{n}", shape, dt, st)

        def sem(n):
            return core.sem(f"{name}_{n}", st)

        row1 = [sb(f"row1_{r}", [P, D]) for r in range(RING)]
        xT1 = [sb(f"xT1_{u}", [P, KC, P]) for u in range(2)]
        router = sb("router", [P, KC, NL])
        logit = sb("logit", [P, B, NL])
        prob = sb("prob", [P, B, E])
        red = sb("red", [P, B])
        top, top_i = sb("top", [P, B, 8]), sb("top_i", [P, B, 8], U32)
        topf = sb("topf", [P, B, 8])
        expert = sb("expert", [P, E])
        onehot = sb("onehot", [P, B, K, E])
        chosen = sb("chosen", [P, 2 * B, E], BF16)
        before, onesb = sb("before", [P, P], BF16), sb("onesb", [P, P], BF16)
        place = sb("place", [P, B, E])
        spot = sb("spot", [P, B, K])
        spot2 = sb("spot2", [P, B, K])
        flag = sb("flag", [P, B, K])
        weight = sb("weight", [P, B, K])
        from_slot = sb("from_slot", [P, B, K], U32)
        slot_tile, slot_row = sb("slot_tile", [P, B, K]), sb("slot_row", [P, B, K])
        lane, tile_of, row_of = sb("lane", [P, P], BF16), sb("tile_of", [P, B]), sb("row_of", [P, 1])
        tile_no = sb("tile_no", [P, NT])
        in_row = [sb(f"in_row{u}", [P, K, P], BF16) for u in range(2)]
        in_tile = sb("in_tile", [P, 2, B * K, NT], BF16)
        token_f, tokens = sb("token_f", [P, 2, NT]), sb("tokens", [P, NT], U32)
        xin = [sb(f"xin{r}", [P, D]) for r in range(RING)]
        xinT = [sb(f"xinT{u}", [P, KC, P]) for u in range(2)]
        act_sb = [sb(f"act_sb{u}", [P, FE]) for u in range(2)]
        h_sb = [sb(f"h_sb{u}", [P, FE]) for u in range(2)]
        hT_sb = [sb(f"hT_sb{u}", [FCH, NJ, P]) for u in range(2)]
        y_sb = [sb(f"y_sb{r}", [P, D]) for r in range(RING)]
        got = [sb(f"got{r}", [P, K, D]) for r in range(RING)]
        if capacity:
            w_gu = [sb(f"w_gu{r}", [P, KC, 2 * FE]) for r in range(RING)]
            w_d = [sb(f"w_d{r}", [FCH, NJ, D]) for r in range(RING)]
        else:
            w_gu_all = sb("w_gu_all", [P, E * KC * 2 * FE])
            w_d_all = sb("w_d_all", [FCH, E * NJ * D])
            tiles, ends, base = sb("tiles", [P, E]), sb("ends", [P, E]), sb("base", [P, E])
            ones_e = sb("ones_e", [P, E])
            past = sb("past", [P, NT, E])
            owner, owner_i = sb("owner", [P, NT]), sb("owner_i", [P, NT], I32)
        if biased:
            bias = sb("bias", [P, E])
        if rms:
            norm_w = sb("norm_w", [P, D])
            xn, rms_f = sb("xn", [P, D]), sb("rms_f", [P, B])
            gate_f = sb("gate_f", [P, B])
        if shared:
            xT = sb("xT", [P, KC, T])
            sw_g, sw_u = sb("sw_g", [P, KC, shared]), sb("sw_u", [P, KC, shared])
            sw_d = sb("sw_d", [P, FS, D])
            s_up = [sb(f"s_up{u}", [P, W4]) for u in range(2)]
            s_act = [sb(f"s_act{u}", [P, W4]) for u in range(2)]
            s_hT = [sb(f"s_hT{u}", [P, FS, W4]) for u in range(2)]
        ps_x = [core.ps(f"{name}_ps_x{u}", [P, D], F32, st) for u in range(2)]
        ps_l = core.ps(f"{name}_ps_l", [P, W4], F32, st)
        ps_p = core.ps(f"{name}_ps_p", [P, W4], F32, st)
        ps_r = (ps_l, ps_p)
        ps_g = [core.ps(f"{name}_ps_g{u}", [P, W4], F32, st) for u in range(2)]
        ps_u = [core.ps(f"{name}_ps_u{u}", [P, W4], F32, st) for u in range(2)]
        (w_in, sw_in, ew_in, const_done, row_done, xT_put, xT_done,
         l_put, l_done, max_done, e_done, chosen_done, place_put, counted, owner_done, tile_marked, row_marked, tokens_put, tokens_done, from_done, gate_e,
         sg_put, s_silu, s_early_mul, s_mul, sd_put, sd_done, in_turned, in_copied, gu_put, e_silu, e_mul, h_turned,
         h_copied, yd_put, y_copied, added) = (sem(n) for n in (
             "w_in", "sw_in", "ew_in", "const_done", "row_done",
             "xT_put", "xT_done", "l_put", "l_done", "max_done", "e_done", "chosen_done", "place_put",
             "counted", "owner_done", "tile_marked", "row_marked", "tokens_put", "tokens_done", "from_done", "gate_e", "sg_put", "s_silu",
             "s_early_mul", "s_mul",
             "sd_put", "sd_done", "in_turned", "in_copied", "gu_put", "e_silu", "e_mul", "h_turned", "h_copied",
             "yd_put", "y_copied", "added"))
        row_out = [sem(f"row_out{r}") for r in range(RING)]
        gu_in, down_in = ([sem(f"{n}{r}") for r in range(RING)] for n in ("gu_in", "down_in"))
        y_out = [sem(f"y_out{r}") for r in range(RING)]
        xin_in, got_in = core.xin_in, core.gathered
        xin_before, got_before = core.n_xin_in, core.n_gathered
        core.n_xin_in += NT // RING * 16
        core.n_gathered += B // RING * K * 16
        n_loads = 1 + rms + biased
        results = core.results[0:NT * P, :]
        n_const = 8 if capacity else 9
        rstd_done = sem("rstd_done")
        block = st.enter_context(nc.Block())

        early_steps = 2 * FS
        bounds = (0, (early_steps + 2) // 3, max(3 * FS // 2, min(2, early_steps)), early_steps)

        def chunk_rows(f):
            return min(P, shared - f * P)

        @block.sync
        def _(sp):
            sp.dma_start(router[:, :, :], dram[f"{name}_router"]).then_inc(w_in, 16)
            if biased:
                sp.dma_start(bias[:, :], dram[f"{name}_bias"].partition_broadcast(P)).then_inc(w_in, 16)
            if rms:
                sp.dma_start(norm_w[:, :], dram[f"{name}_norm_w"].partition_broadcast(P)).then_inc(w_in, 16)
            if shared:
                sp.dma_start(sw_g[:, :, :], dram[f"{name}_sw_g"]).then_inc(sw_in, 16)
                sp.dma_start(sw_u[:, :, :], dram[f"{name}_sw_u"]).then_inc(sw_in, 16)
                whole = shared // P * P
                sp.dma_start(sw_d[:, 0:shared // P, :], dram[f"{name}_sw_d"][0:whole, :]
                             .rearrange("(f p) d -> p f d", p=P)).then_inc(sw_in, 16)
                if shared > whole:
                    sp.dma_start(sw_d[0:shared - whole, FS - 1, :], dram[f"{name}_sw_d"][whole:shared, :])\
                      .then_inc(sw_in, 16)
            if not capacity:
                sp.dma_start(w_gu_all[:, :].rearrange("p (e n) -> p e n", e=E), dram[f"{name}_w_gu"]
                             .rearrange("e p c n -> p e (c n)")).then_inc(ew_in, 16)
                sp.dma_start(w_d_all[:, :].rearrange("p (e n) -> p e n", e=E), dram[f"{name}_w_d"]
                             .rearrange("e p c n -> p e (c n)")).then_inc(ew_in, 16)

            def store(j, u):
                sp.wait_ge(y_copied, j + 1)
                sp.dma_start(results[bass.ds(j * P, P), :], y_sb[u][:, :]).then_inc(y_out[u], 16)

            def load_down(j, r):
                if after(j, RING):
                    sp.wait_ge(yd_put, j - (RING - 1))
                sp.dma_start(w_d[r][:, :, :], dram[f"{name}_w_d"][bass.ds(j, 1)]
                             .rearrange("e p c n -> p (e c) n")).then_inc(down_in[r], 16)

            def load(j, r):
                if capacity:
                    if after(j, RING):
                        sp.wait_ge(gu_put, j - (RING - 1))
                    sp.dma_start(w_gu[r][:, :, :], dram[f"{name}_w_gu"][bass.ds(j, 1)]
                                 .rearrange("e p c n -> p (e c) n")).then_inc(gu_in[r], 16)
                if capacity and after(j, 1):
                    load_down(j - 1, (r - 1) % RING)
                if after(j, LAG):
                    store(j - LAG, (r - LAG) % RING)

            def store_row(t, r):
                sp.wait_ge(row_done, t + 1)
                sp.dma_start(core.rows[bass.ds(t * P, P), :], row1[r][:, :]).then_inc(row_out[r], 16)

            over_ring(sp, store_row, B, RING)
            over_ring(sp, load, NT, RING, 2)
            if capacity:
                load_down(NT - 1, (NT - 1) % RING)
            for j in range(NT - LAG, NT):
                store(j, j % RING)
            if final:
                for t in range(B):
                    sp.wait_ge(added, t + 1)
                    sp.dma_start(core.out[t], core.xt(t)).then_inc(core.x_out, 16)
                sp.wait_ge(core.x_out, B * 16)

        @block.gpsimd
        def _(pool):
            all_rstd(pool, core, rstd_done)
            if rms:
                pool.wait_ge(rstd_done, 1)
                pool.tensor_tensor(rms_f[:, :], core.stats[:, :, 1], core.rstd[:, :], ALU.mult)
                pool.drain()
                pool.tensor_tensor(rms_f[:, :], rms_f[:, :], core.rstd[:, :], ALU.mult)
                pool.drain()
                pool.tensor_scalar(rms_f[:, :], rms_f[:, :], 1e-6, 1.0, ALU.add, ALU.mult)
                pool.drain()
                pool.tensor_tensor(rms_f[:, :], rms_f[:, :], core.minus_half[:, :], ALU.pow).then_inc(rstd_done, 1)
            pool.iota(expert[:, :], [[1, E]], base=0, channel_multiplier=0, allow_small_or_imprecise_dtypes=True)\
                .then_inc(const_done, 1)
            pool.memset(before[:, :], 1.0).then_inc(const_done, 1)
            pool.memset(onesb[:, :], 1.0).then_inc(const_done, 1)
            pool.wait_ge(const_done, 3)
            pool.affine_select(out=before[:, :], in_=before[:, :], compare_op=ALU.is_gt, fill=0.0, base=0,
                               pattern=[[1, P]], channel_multiplier=-1).then_inc(const_done, 1)
            for out, pattern, rowwise in ((tile_no, [[1, NT]], 0), (lane, [[1, P]], 0), (tile_of, [[1, B]], 0),
                                          (row_of, [[0, 1]], 1)):
                pool.iota(out[:, :], pattern, base=0, channel_multiplier=rowwise,
                          allow_small_or_imprecise_dtypes=True).then_inc(const_done, 1)
            if not capacity:
                pool.memset(ones_e[:, :], 1.0).then_inc(const_done, 1)
            def shared_mul(n):
                q, f = n // FS, n % FS
                m = chunk_rows(f)
                pool.wait_ge(s_silu, n + 1)
                pool.tensor_tensor(s_hT[q][0:m, f, :], s_up[n % 2][0:m, :], s_act[n % 2][0:m, :], ALU.mult)\
                    .then_inc(s_early_mul, 1)

            for n in range(bounds[2]):
                shared_mul(n)
            for r in range(RING):
                pool.wait_ge(row_out[r], B // RING * 16)
            pool.wait_ge(tokens_done, 1)
            for j in range(NT):
                if j == RING:
                    for n in range(bounds[2], early_steps):
                        shared_mul(n)
                if j >= RING:
                    pool.wait_ge(in_turned, j - (RING - 1))
                pool.indirect_dma_start(
                    out=xin[j % RING][:, :], out_offset=None, in_=core.rows,
                    in_offset=bass.IndirectOffsetOnAxis(ap=tokens[:, j:j + 1], axis=0)).then_inc(xin_in[j % RING], 16)
            pool.wait_ge(from_done, 1)
            for r in range(RING):
                pool.wait_ge(y_out[r], NT // RING * 16)
            for t in range(B):
                if t >= RING:
                    pool.wait_ge(added, t - (RING - 1))
                for k in range(K):
                    pool.indirect_dma_start(
                        out=got[t % RING][:, k, :], out_offset=None, in_=results,
                        in_offset=bass.IndirectOffsetOnAxis(ap=from_slot[:, t, k:k + 1], axis=0))\
                        .then_inc(got_in[t % RING], 16)

        @block.vector
        def _(dve):
            dve.memset(chosen[:, 0:B, :], 0.0)
            dve.wait_ge(rstd_done, 2 if rms else 1)
            dve.wait_ge(w_in, 16 * n_loads)

            def row(t, r):
                if rms:
                    dve.drain()
                if after(t, RING):
                    dve.wait_ge(row_out[r], (t - r) * (16 // RING))
                    dve.wait_ge(xT_put, t - (RING - 1))
                if rms:
                    normalise(dve, core, xn[:, :], t)
                    dve.drain()
                    dve.tensor_tensor(core.xt(t), core.xt(t), xn[:, :], ALU.add)
                    dve.scalar_tensor_tensor(out=row1[r][:, :], in0=xn[:, :], scalar=rms_f[:, bass.ds(t, 1)],
                                             in1=norm_w[:, :], op0=ALU.mult, op1=ALU.mult).then_inc(row_done, 1)
                else:
                    normalise(dve, core, row1[r][:, :], t).then_inc(row_done, 1)

            def keep_logits(t, r):
                dve.wait_ge(l_put, t + 1)
                out = logit[:, bass.ds(t, 1), :].rearrange("p a e -> p (a e)")
                if biased:
                    dve.tensor_tensor(out, ps_r[r % 2][:, 0:NL], bias[:, :], ALU.add).then_inc(l_done, 1)
                else:
                    dve.tensor_copy(out, ps_r[r % 2][:, 0:NL]).then_inc(l_done, 1)

            def tile(t, r):
                if ahead(t, 2):
                    row(t + 2, (r + 2) % RING)
                keep_logits(t, r)

            row(0, 0)
            row(1, 1)
            over_ring(dve, tile, B, RING)
            dve.drain()

            logits = logit[:, :, 0:E]
            if top_softmax:
                ranked = logit
            else:
                ranked = prob
                dve.tensor_reduce(red[:, :], logits, AX.X, ALU.max)
                dve.drain()
                dve.tensor_tensor(prob[:, :, :], logits, red[:, :].unsqueeze(2).broadcast_to([P, B, E]), ALU.subtract)\
                   .then_inc(max_done, 1)
                dve.wait_ge(e_done, 1)
                dve.tensor_reduce(red[:, :], prob[:, :, :], AX.X, ALU.add)
                dve.drain()
                dve.reciprocal(red[:, :], red[:, :])
                dve.drain()
                dve.tensor_tensor(prob[:, :, :], prob[:, :, :], red[:, :].unsqueeze(2).broadcast_to([P, B, E]), ALU.mult)
                dve.drain()
            for t in range(B):
                dve.max(top[:, t, :], ranked[:, t, 0:E])
            dve.drain()
            for t in range(B):
                dve.max_index(top_i[:, t, :], top[:, t, :], ranked[:, t, 0:E])
            dve.drain()
            dve.tensor_copy(topf[:, :, :], top_i[:, :, :])
            dve.wait_ge(const_done, n_const)
            dve.drain()
            for k in range(K):
                dve.tensor_tensor(onehot[:, :, k, :], expert[:, :].unsqueeze(1).broadcast_to([P, B, E]),
                                  topf[:, :, k:k + 1].broadcast_to([P, B, E]), ALU.is_equal)
            dve.drain()
            with nc.allow_low_precision(reason="zeros and ones"):
                dve.tensor_reduce(chosen[:, B:, :], onehot[:, :, :, :].rearrange("p t k e -> p t e k"), AX.X, ALU.add)\
                   .then_inc(chosen_done, 1)
            if top_softmax:
                dve.tensor_tensor(weight[:, :, :], top[:, :, 0:K], top[:, :, 0:1].broadcast_to([P, B, K]), ALU.subtract)\
                   .then_inc(max_done, 1)
                dve.wait_ge(e_done, 1)
                source = weight[:, :, :]
            else:
                source = top[:, :, 0:K]
            if top_softmax or renorm:
                dve.tensor_reduce(red[:, :], source, AX.X, ALU.add)
                dve.drain()
                if renorm:
                    dve.tensor_scalar(red[:, :], red[:, :], 1e-9, None, ALU.add)
                    dve.drain()
                dve.reciprocal(red[:, :], red[:, :])
                dve.drain()
                dve.tensor_tensor(weight[:, :, :], source, red[:, :].unsqueeze(2).broadcast_to([P, B, K]), ALU.mult)
            if rms:
                dve.wait_ge(gate_e, 1)
                dve.tensor_scalar(gate_f[:, :], gate_f[:, :], 1.0, None, ALU.add)
                dve.drain()
                dve.reciprocal(gate_f[:, :], gate_f[:, :])
            dve.wait_ge(place_put, 1)
            if capacity:
                dve.tensor_copy(place[:, :, :], ps_p[:, 0:B * E].rearrange("p (t e) -> p t e", t=B))
            else:
                dve.wait_ge(counted, 1)
                dve.tensor_scalar(tiles[:, :], ps_l[:, 0:E], 127.0, 1.0 / P, ALU.add, ALU.mult)
                dve.drain()
                dve.tensor_scalar(tiles[:, :], tiles[:, :], 1.0 / 256 - 0.5, MAGIC, ALU.add, ALU.add)
                dve.drain()
                dve.tensor_scalar(tiles[:, :], tiles[:, :], MAGIC, None, ALU.subtract)
                dve.drain()
                dve.tensor_tensor_scan(ends[:, :], ones_e[:, :], tiles[:, :], 0.0, ALU.mult, ALU.add)
                dve.drain()
                dve.tensor_tensor(base[:, :], ends[:, :], tiles[:, :], ALU.subtract)
                dve.tensor_tensor(past[:, :, :], tile_no[:, :].unsqueeze(2).broadcast_to([P, NT, E]),
                                  ends[:, :].unsqueeze(1).broadcast_to([P, NT, E]), ALU.is_ge)
                dve.drain()
                dve.tensor_scalar(base[:, :], base[:, :], float(P), None, ALU.mult)
                dve.tensor_reduce(owner[:, :], past[:, :, :], AX.X, ALU.add)
                dve.drain()
                dve.tensor_scalar(owner_i[:, :], owner[:, :], float(E - 1), None, ALU.min).then_inc(owner_done, 1)
                dve.tensor_tensor(place[:, :, :], ps_p[:, 0:B * E].rearrange("p (t e) -> p t e", t=B),
                                  base[:, :].unsqueeze(1).broadcast_to([P, B, E]), ALU.add)
            dve.drain()
            for k in range(K):
                dve.tensor_tensor(onehot[:, :, k, :], onehot[:, :, k, :], place[:, :, :], ALU.mult)
            dve.drain()
            dve.tensor_reduce(spot[:, :, :], onehot[:, :, :, :], AX.X, ALU.add)
            dve.drain()
            if capacity:
                dve.tensor_scalar(flag[:, :, :], spot[:, :, :], float(capacity), None, ALU.is_lt)
                dve.tensor_scalar(spot2[:, :, :], spot[:, :, :], float(capacity - 1), None, ALU.min)
                dve.drain()
                dve.tensor_tensor(weight[:, :, :], top[:, :, 0:K], flag[:, :, :], ALU.mult)
                dve.scalar_tensor_tensor(out=spot[:, :, :], in0=topf[:, :, 0:K], scalar=float(capacity),
                                         in1=spot2[:, :, :], op0=ALU.mult, op1=ALU.add)
                dve.drain()
                dve.tensor_scalar(flag[:, :, :], flag[:, :, :], -float(NT * P), float(NT * P), ALU.mult, ALU.add)
                dve.drain()
            dve.tensor_copy(from_slot[:, :, :], spot[:, :, :]).then_inc(from_done, 1)
            if capacity:
                dve.drain()
                dve.tensor_tensor(spot[:, :, :], spot[:, :, :], flag[:, :, :], ALU.add)
                dve.drain()
            dve.tensor_scalar(slot_tile[:, :, :], spot[:, :, :], 0.5 - P / 2, 1.0 / P, ALU.add, ALU.mult)
            dve.drain()
            dve.tensor_scalar(slot_tile[:, :, :], slot_tile[:, :, :], MAGIC, MAGIC, ALU.add, ALU.subtract)
            dve.drain()
            dve.scalar_tensor_tensor(out=slot_row[:, :, :], in0=slot_tile[:, :, :], scalar=-float(P),
                                     in1=spot[:, :, :], op0=ALU.mult, op1=ALU.add)
            with nc.allow_low_precision(reason="whole numbers under 256"):
                dve.tensor_tensor(in_tile[:, 0, :, :], tile_no[:, :].unsqueeze(1).broadcast_to([P, B * K, NT]),
                                  slot_tile[:, :, :].rearrange("p t k -> p (t k)").unsqueeze(2)
                                  .broadcast_to([P, B * K, NT]), ALU.is_equal)
                dve.drain()
                dve.tensor_scalar(in_tile[:, 1, :, :], in_tile[:, 0, :, :], row_of[:, :], None, ALU.mult)
                dve.drain()
                marks = in_tile[:, 0, :, :].rearrange("p (t k) j -> p t (k j)", k=K)
                dve.tensor_tensor(marks, marks, tile_of[:, :].unsqueeze(2).broadcast_to([P, B, K * NT]), ALU.mult)\
                   .then_inc(tile_marked, 1)

            def mark_rows(t, u):
                if after(t, 2):
                    dve.wait_ge(tokens_put, t - 1)
                dve.tensor_tensor(in_row[u][:, :, :], lane[:, :].unsqueeze(1).broadcast_to([P, K, P]),
                                  slot_row[:, t, :].unsqueeze(2).broadcast_to([P, K, P]), ALU.is_equal)\
                   .then_inc(row_marked, 1)

            for t in range(B):
                mark_rows(t, t % 2)
            dve.wait_ge(tokens_put, B)
            dve.tensor_copy(token_f[:, :, :], ps_p[:, 0:2 * NT].rearrange("p (s j) -> p s j", s=2))
            dve.drain()
            dve.scalar_tensor_tensor(out=tokens[:, :], in0=token_f[:, 0, :], scalar=float(P), in1=token_f[:, 1, :],
                                     op0=ALU.mult, op1=ALU.add).then_inc(tokens_done, 1)

            def shared_mul(q, f):
                n, m = q * FS + f, chunk_rows(f)
                dve.wait_ge(s_silu, n + 1)
                if n - q % 2 >= 2 * FS and f == 0:
                    dve.wait_ge(sd_put, (q - 1) * 4)
                dve.tensor_tensor(s_hT[q % 2][0:m, f, :], ps_u[n % 2][0:m, :], s_act[n % 2][0:m, :], ALU.mult)\
                   .then_inc(s_mul, 1)

            def shared_add(t):
                dve.wait_ge(sd_put, t + 1)
                if rms:
                    dve.scalar_tensor_tensor(out=core.xt(t), in0=ps_r[t % 2][:, 0:D], scalar=gate_f[:, t:t + 1],
                                             in1=core.xt(t), op0=ALU.mult, op1=ALU.add).then_inc(sd_done, 1)
                else:
                    dve.tensor_tensor(core.xt(t), core.xt(t), ps_r[t % 2][:, 0:D], ALU.add).then_inc(sd_done, 1)

            def mul(j, u):
                dve.wait_ge(e_silu, j + 1)
                if after(j, 2):
                    dve.wait_ge(h_turned, j - 1)
                dve.tensor_tensor(h_sb[u][:, :], ps_g[u][:, FE:2 * FE], act_sb[u][:, :], ALU.mult).then_inc(e_mul, 1)

            def copy_y(j, r):
                dve.wait_ge(yd_put, j + 1)
                if after(j, RING):
                    dve.wait_ge(y_out[r], (j - r) * (16 // RING))
                dve.tensor_copy(y_sb[r][:, :], ps_l[:, 0:D]).then_inc(y_copied, 1)

            def expert_tile(j, r):
                if ahead(j, 1, NT):
                    mul(j + 1, (r + 1) % 2)
                if after(j, 1):
                    copy_y(j - 1, (r - 1) % RING)

            mul(0, 0)
            over_ring(dve, expert_tile, NT, RING)
            copy_y(NT - 1, (NT - 1) % RING)

            with_shared, with_results = 0, 0

            def stats_of(t):
                if not final and t < with_results and (not shared or t < with_shared):
                    dve.drain()
                    row_stats(dve, core, t)

            def add_results(until):
                nonlocal with_results
                for t in range(with_results, until):
                    dve.wait_ge(got_in[t % RING], got_before + (t // RING + 1) * 16 * K)
                    for k in range(K):
                        last = dve.scalar_tensor_tensor(out=core.xt(t), in0=got[t % RING][:, k, :], scalar=weight[:, t, k:k + 1],
                                                        in1=core.xt(t), op0=ALU.mult, op1=ALU.add)
                        if k < K - 1:
                            dve.drain()
                    last.then_inc(added, 1)
                    with_results = t + 1
                    stats_of(t)

            columns = 0

            def results_by_now(more):
                nonlocal columns
                columns += more
                dve.drain()
                add_results(max(with_results, min(B, columns // (K * 640) - 1)))

            def add_shared(q):
                nonlocal with_shared
                for t in range(4 * q, 4 * q + 4):
                    dve.drain()
                    shared_add(t)
                    with_shared = t + 1
                    stats_of(t)
                    results_by_now(FS * D)

            if shared:
                add_shared(0)
            for n in range(early_steps, 4 * FS):
                if n == 3 * FS:
                    add_shared(1)
                shared_mul(n // FS, n % FS)
                results_by_now(4 * W4)
            if shared:
                add_shared(2)
                add_shared(3)
            dve.drain()
            add_results(B)
            if not final:
                finish_stats(dve, core)

        @block.scalar
        def _(act):
            def tile(t, r):
                act.wait_ge(xT_put, t + 1)
                if after(t, 2):
                    act.wait_ge(l_put, t - 1)
                if shared:
                    act.activation(xT[:, :, bass.ds(t * P, P)], ps_x[r % 2][:, :].rearrange("p (c t) -> p c t", c=KC),
                                   ACT.Copy)
                act.activation(xT1[r % 2][:, :, :], ps_x[r % 2][:, :].rearrange("p (c t) -> p c t", c=KC), ACT.Copy)\
                    .then_inc(xT_done, 1)

            over_ring(act, tile, B, RING)
            act.wait_ge(max_done, 1)
            if top_softmax:
                act.activation(weight[:, :, :], weight[:, :, :], ACT.Exp).then_inc(e_done, 1)
            else:
                act.activation(prob[:, :, :], prob[:, :, :], ACT.Exp).then_inc(e_done, 1)
            if rms:
                act.activation(gate_f[:, :], logit[:, :, E], ACT.Exp, scale=-1.0).then_inc(gate_e, 1)

            for n in range(early_steps):
                m = chunk_rows(n % FS)
                act.wait_ge(sg_put, n + 1)
                if n >= 2:
                    act.wait_ge(s_early_mul, n - 1)
                act.activation(s_act[n % 2][0:m, :], ps_g[n % 2][0:m, :], ACT.Silu)
                act.activation(s_up[n % 2][0:m, :], ps_u[n % 2][0:m, :], ACT.Copy).then_inc(s_silu, 1)

            def copy_in(j, u):
                act.wait_ge(in_turned, j + 1)
                if after(j, 2):
                    act.wait_ge(gu_put, j - 1)
                act.activation(xinT[u][:, :, :].rearrange("p c t -> p (c t)"), ps_x[u][:, :], ACT.Copy)\
                    .then_inc(in_copied, 1)

            def silu(j, u):
                act.wait_ge(gu_put, j + 1)
                if after(j, 2):
                    act.wait_ge(e_mul, j - 1)
                act.activation(act_sb[u][:, :], ps_g[u][:, 0:FE], ACT.Silu).then_inc(e_silu, 1)

            def copy_h(j, u):
                act.wait_ge(h_turned, j + 1)
                if after(j, 2):
                    act.wait_ge(yd_put, j - 1)
                act.activation(hT_sb[u][:, :, :].rearrange("p c t -> p (c t)"), ps_u[u][0:FCH, 0:NJ * P], ACT.Copy)\
                    .then_inc(h_copied, 1)

            def expert_tile(j, r):
                if ahead(j, 1, NT):
                    silu(j + 1, (r + 1) % 2)
                copy_h(j, r % 2)
                if ahead(j, 2, NT):
                    copy_in(j + 2, r % 2)

            copy_in(0, 0)
            copy_in(1, 1)
            silu(0, 0)
            over_ring(act, expert_tile, NT, RING)
            for n in range(early_steps, 4 * FS):
                m = chunk_rows(n % FS)
                act.wait_ge(sg_put, n + 1)
                if n < early_steps + 2:
                    act.wait_ge(s_early_mul, early_steps)
                else:
                    act.wait_ge(s_mul, n - 1 - early_steps)
                act.activation(s_act[n % 2][0:m, :], ps_g[n % 2][0:m, :], ACT.Silu).then_inc(s_silu, 1)

        @block.tensor
        def _(pe):
            def turn_row(t, r):
                pe.wait_ge(row_done, t + 1)
                if after(t, 2):
                    pe.wait_ge(xT_done, t - 1)
                for c in range(KC):
                    last = pe.transpose(ps_x[r % 2][:, c * P:c * P + P], row1[r][:, c * P:c * P + P], core.ident[:, :])
                last.then_inc(xT_put, 1)

            def route(t, r):
                pe.wait_ge(xT_done, t + 1)
                if after(t, 2):
                    pe.wait_ge(l_done, t - 1)
                for c in range(KC):
                    last = pe.matmul(ps_r[r % 2][:, 0:NL], xT1[r % 2][:, c, :], router[:, c, :],
                                     start=(c == 0), stop=(c == KC - 1))
                last.then_inc(l_put, 1)

            def tile(t, r):
                if ahead(t, 1):
                    turn_row(t + 1, (r + 1) % RING)
                route(t, r)

            pe.wait_ge(w_in, 16 * n_loads)
            turn_row(0, 0)
            over_ring(pe, tile, B, RING)

            def shared_gu(n):
                q, f = n // FS, n % FS
                m = chunk_rows(f)
                if n >= early_steps + 2:
                    pe.wait_ge(s_mul, n - 1 - early_steps)
                elif n >= 2:
                    pe.wait_ge(s_silu, min(n - 1, early_steps))
                for ps, w in ((ps_g, sw_g), (ps_u, sw_u)):
                    for c in range(KC):
                        last = pe.matmul(ps[n % 2][0:m, :], w[:, c, f * P:f * P + m], xT[:, c, q * W4:q * W4 + W4],
                                         start=(c == 0), stop=(c == KC - 1))
                last.then_inc(sg_put, 1)

            def shared_down(q):
                pe.wait_ge(s_early_mul if q < 2 else s_mul, (q % 2 + 1) * FS)
                for i in range(4):
                    t = 4 * q + i
                    if t >= 2:
                        pe.wait_ge(sd_done, t - 1)
                    for f in range(FS):
                        m = chunk_rows(f)
                        last = pe.matmul(ps_r[t % 2][:, 0:D], s_hT[q % 2][0:m, f, i * P:i * P + P], sw_d[0:m, f, :],
                                         start=(f == 0), stop=(f == FS - 1))
                    last.then_inc(sd_put, 1)

            if shared:
                pe.wait_ge(sw_in, 16 * (3 + (shared % P > 0)))
            for n in range(bounds[0], bounds[1]):
                shared_gu(n)

            pe.wait_ge(const_done, n_const)
            pe.wait_ge(chosen_done, 1)
            flat = chosen[:, :, :].rearrange("p t e -> p (t e)")
            for d in range(B):
                last = pe.matmul(ps_p[:, 0:B * E], onesb[:, :] if d else before[:, :], flat[:, (B - d) * E:(2 * B - d) * E],
                                 start=(d == 0), stop=(d == B - 1))
            last.then_inc(place_put, 1)
            if not capacity:
                pe.wait_ge(l_done, B)
                for t in range(B):
                    last = pe.matmul(ps_l[:, 0:E], onesb[:, :], chosen[:, B + t, :], start=(t == 0), stop=(t == B - 1))
                last.then_inc(counted, 1)

            for n in range(bounds[1], bounds[2]):
                shared_gu(n)

            pe.wait_ge(tile_marked, 1)
            for t in range(B):
                pe.wait_ge(row_marked, t + 1)
                for k in range(K):
                    last = pe.matmul(ps_p[:, 0:2 * NT].rearrange("p (s j) -> p s j", s=2), in_row[t % 2][:, k, :],
                                     in_tile[:, :, t * K + k, :],
                                     start=(t + k == 0), stop=(t * K + k == B * K - 1))
                last.then_inc(tokens_put, 1)

            for n in range(bounds[2], bounds[3]):
                shared_gu(n)
            if shared:
                pe.wait_ge(s_silu, early_steps)

            def owner_of(j):
                return nc.values_load(owner_i[0:1, bass.ds(j, 1)], engines=(mybir.EngineType.PE,), min_val=0,
                                      max_val=E - 1, skip_runtime_bounds_check_because="a count, held under E")

            def turn_in(j, r):
                pe.wait_ge(xin_in[r], (j - r) * (16 // RING) + (16 + xin_before))
                if after(j, 2):
                    pe.wait_ge(in_copied, j - 1)
                for c in range(KC):
                    last = pe.transpose(ps_x[r % 2][:, c * P:c * P + P], xin[r][:, c * P:c * P + P], core.ident[:, :])
                last.then_inc(in_turned, 1)

            def gate_up(j, r):
                if not capacity:
                    e = owner_of(j)
                if capacity:
                    pe.wait_ge(gu_in[r], (j - r) * (16 // RING) + 16)
                pe.wait_ge(in_copied, j + 1)
                if after(j, 2):
                    pe.wait_ge(e_mul, j - 1)
                for c in range(KC):
                    w = w_gu[r][:, c, :] if capacity else w_gu_all[:, bass.ds(e * (KC * 2 * FE) + c * 2 * FE, 2 * FE)]
                    last = pe.matmul(ps_g[r % 2][:, 0:2 * FE], xinT[r % 2][:, c, :], w, start=(c == 0), stop=(c == KC - 1))
                last.then_inc(gu_put, 1)

            def turn_h(j, u):
                pe.wait_ge(e_mul, j + 1)
                if after(j, 2):
                    pe.wait_ge(h_copied, j - 1)
                for c in range(NJ):
                    last = pe.transpose(ps_u[u][0:FCH, c * P:c * P + P], h_sb[u][:, c * FCH:(c + 1) * FCH], core.ident[:, :])
                last.then_inc(h_turned, 1)

            def down(j, r):
                if not capacity:
                    e = owner_of(j)
                if capacity:
                    pe.wait_ge(down_in[r], (j - r) * (16 // RING) + 16)
                pe.wait_ge(h_copied, j + 1)
                if after(j, 1):
                    pe.wait_ge(y_copied, j)
                for c in range(NJ):
                    w = w_d[r][:, c, :] if capacity else w_d_all[:, bass.ds(e * (NJ * D) + c * D, D)]
                    last = pe.matmul(ps_l[:, 0:D], hT_sb[r % 2][:, c, :], w, start=(c == 0), stop=(c == NJ - 1))
                last.then_inc(yd_put, 1)

            def expert_tile(j, r):
                if ahead(j, 1, NT):
                    gate_up(j + 1, (r + 1) % RING)
                turn_h(j, r % 2)
                if ahead(j, 2, NT):
                    turn_in(j + 2, (r + 2) % RING)
                if after(j, 1):
                    down(j - 1, (r - 1) % RING)

            if not capacity:
                pe.wait_ge(owner_done, 1)
                pe.wait_ge(ew_in, 32)
            turn_in(0, 0)
            turn_in(1, 1)
            gate_up(0, 0)
            over_ring(pe, expert_tile, NT, RING)
            down(NT - 1, (NT - 1) % RING)
            if shared:
                pe.wait_ge(e_mul, NT)
                pe.wait_ge(h_copied, NT)
                pe.wait_ge(y_copied, NT)
                shared_down(0)
                for n in range(early_steps, 3 * FS):
                    shared_gu(n)
                shared_down(1)
                for n in range(3 * FS, 4 * FS):
                    shared_gu(n)
                shared_down(2)
                shared_down(3)


STAGES = {
    "L1F": lambda core: moe_ffn(core, "l1f", 32, 4, 176, capacity=128, shared=704, rms=True),
    "L2F": lambda core: moe_ffn(core, "l2f", 16, 2, 128, shared=128, biased=True, renorm=True),
    "L3F": lambda core: moe_ffn(core, "l3f", 8, 2, 256, top_softmax=True, final=True),
    "L1A": lambda core: gated_long_conv(core, "l1a"),
    "L3A": lambda core: channel_attention(core, "l3a"),
    "L0F": lambda core: hadamard_ffn(core, "l0f"),
    "L0A": lambda core: gqa_attention(core, "l0a", dict(
        wq="l0a_wq", wk="l0a_wk", wv="l0a_wv", wo="l0a_wo", bq="l0a_bq", bk="l0a_bk", bv="l0a_bv", bo="l0a_bo"), True),
    "L2A": lambda core: gqa_attention(core, "l2a", dict(
        wq="l2a_wq", wk="l2a_wk", wv="l2a_wv", wo="l2a_wo", bo="l2a_bo"), False),
}


def build(nc, dram, out, stages):
    with ExitStack() as ctx:
        core = Core(nc, ctx, dram)
        core.out = out
        load_inputs(core)
        for s in stages:
            if s == "L1F":
                core.early.close()
            STAGES[s](core)


def lay_out(np, a):
    def chunks(w, p=P):
        w = np.asarray(w)
        return w.reshape(w.shape[0] // p, p, -1).transpose(1, 0, 2)

    def per_head(w):
        w = np.asarray(w)
        return np.repeat(w.reshape(G, 1, HD, -1), R, axis=1).reshape(H * HD, -1)

    ctx = np.asarray(a["ctx_2048"])
    o = {
        "x": a["x"],
        "ctx": ctx,
        "ctxT": ctx.reshape(B, P, KC, P).transpose(0, 3, 2, 1),
        "pair_mask": np.asarray(a["mask_SxS2_bc0"]),
        "pad_mask": np.asarray(a["mask_BxS2_bk0"]).reshape(T),
    }
    for s, n in (("l0a", "L0_xattn_"), ("l2a", "L2_xattn_")):
        o[f"{s}_wq"] = chunks(np.asarray(a[n + "Wq"]).T)
        o[f"{s}_wk"] = chunks(per_head(a[n + "Wk"]).T)
        o[f"{s}_wv"] = chunks(np.asarray(a[n + "Wv"]).T)
    o["l0f_wg"] = chunks(np.asarray(a["L0_ffn_w_gate"]).T).reshape(P, -1)
    o["l0f_wu"] = chunks(np.asarray(a["L0_ffn_w_up"]).T).reshape(P, -1)
    o["l0f_wd"] = chunks(np.asarray(a["L0_ffn_w_down"]).T).reshape(P, -1)
    had = np.ones((1, 1), np.float32)
    while had.shape[0] < P:
        had = np.block([[had, had], [had, -had]])
    o["had"] = had
    o["skip"] = a["fside_S2_0"]
    k = np.concatenate([np.zeros((16, P), np.float32), np.asarray(a["L1_xattn_k"])], axis=1)
    o["l1a_taps"] = np.stack([k[:, P - m:P - m + D] for m in range(P)])
    def experts(g, u, d, fch):
        g, u, d = (np.asarray(w) for w in (g, u, d))
        gu = np.concatenate([g, u], axis=2)
        return (gu.reshape(len(gu), KC, P, -1).transpose(0, 2, 1, 3),
                d.reshape(len(d), -1, fch, D).transpose(0, 2, 1, 3))

    o["l1f_w_gu"], o["l1f_w_d"] = experts(a["L1_ffn_w_gate"], a["L1_ffn_w_up"], a["L1_ffn_w_down"], 88)
    o["l2f_w_gu"], o["l2f_w_d"] = experts(a["L2_ffn_Wg"], a["L2_ffn_Wu"], a["L2_ffn_Wd"], 128)
    o["l3f_w_gu"], o["l3f_w_d"] = experts(a["L3_ffn_wi_0"], a["L3_ffn_wi_1"], a["L3_ffn_wo"], 128)
    o["l1f_router"] = chunks(np.concatenate([np.asarray(a["L1_ffn_w_router"]), np.asarray(a["L1_ffn_w_shared_gate"])], axis=1))
    o["l2f_router"] = chunks(np.asarray(a["L2_ffn_Wr"]).T)
    o["l3f_router"] = chunks(a["L3_ffn_gate_kernel"])
    o["l1f_norm_w"] = a["L1_ffn_w_norm"]
    o["l2f_bias"] = a["L2_ffn_bias"]
    for s, n in (("l1f", ("L1_ffn_sw_gate", "L1_ffn_sw_up", "L1_ffn_sw_down")),
                 ("l2f", ("L2_ffn_sWg", "L2_ffn_sWu", "L2_ffn_sWd"))):
        o[f"{s}_sw_g"], o[f"{s}_sw_u"], o[f"{s}_sw_d"] = chunks(a[n[0]]), chunks(a[n[1]]), a[n[2]]
    o["l0a_wo"] = chunks(np.asarray(a["L0_xattn_Wo"]).T)
    o["l2a_wo"] = chunks(np.asarray(a["L2_xattn_Wfc"]).T)
    o["l0a_bq"] = np.asarray(a["L0_xattn_bq"]).reshape(KC, P).T
    o["l0a_bk"] = per_head(a["L0_xattn_bk"]).reshape(KC, P).T
    o["l0a_bv"] = a["L0_xattn_bv"]
    o["l0a_bo"] = a["L0_xattn_bo"]
    o["l2a_bo"] = a["L2_xattn_bfc"]
    return {k: np.ascontiguousarray(v) for k, v in o.items()}


ALL = ("L0A", "L0F", "L1A", "L1F", "L2A", "L2F", "L3A", "L3F")


def kernel(**inputs):
    import numpy as np
    import concourse.bacc as bacc
    from concourse.bass_utils import run_bass_kernel_spmd

    arrays = {f"in_{k}": v for k, v in lay_out(np, inputs).items()}
    nc = bacc.Bacc("TRN2", target_bir_lowering=False, num_devices=1)
    dram = {k[3:]: nc.dram_tensor(k, v.shape, mybir.dt.from_np(v.dtype), kind="ExternalInput").ap()
            for k, v in arrays.items()}
    out = nc.dram_tensor("out_x", (B, P, D), F32, kind="ExternalOutput").ap()
    build(nc, dram, out, ALL)
    return run_bass_kernel_spmd(nc, [arrays], core_ids=[0]).results[0]["out_x"]
```
